# Optimizing a Trainium2 kernel written in Bass

```python
import numpy as np
import jax
import jax.numpy as jnp

def _softmax(x, axis=-1):
    return jax.nn.softmax(x, axis=axis)

def _gelu(x):
    return jax.nn.gelu(x, approximate=True)

def _silu(x):
    return jax.nn.silu(x)

def _sigmoid(x):
    return jax.nn.sigmoid(x)

def _layernorm(x, axis=-1, eps=1e-05):
    m = jnp.mean(x, axis=axis, keepdims=True)
    v = jnp.var(x, axis=axis, keepdims=True)
    return (x - m) / jnp.sqrt(v + eps)

def _scatter_add(tgt, idx, src, axis=0):
    return tgt.at[idx].add(src)

def _segment_sum(src, seg, n):
    return jax.ops.segment_sum(src, seg, n)
kernel_name = 'mk_gnn_preln_d4_gnn_r32_bb3615'

def setup_inputs(seed: int=0):
    np.random.seed(seed)
    _w = jnp.asarray

    def _rec_inputs():
        import jax
        import jax.numpy as jnp
        _gk = jax.random.key(seed)
        x = -0.0003713 + 1 * jax.random.normal(jax.random.fold_in(_gk, 1), (3125, 128), jnp.float32)
        src = jax.random.randint(jax.random.fold_in(_gk, 2), (100000,), 0, 3125, jnp.int32)
        dst = jax.random.randint(jax.random.fold_in(_gk, 3), (100000,), 0, 3125, jnp.int32)
        _o = jnp.argsort(dst, stable=True)
        src = src[_o]
        dst = dst[_o]
        edge_type_8 = jax.random.randint(jax.random.fold_in(_gk, 13), (100000,), 0, 8, jnp.int32)
        edge_weight1 = 0.000614103 + 0.999867 * jax.random.normal(jax.random.fold_in(_gk, 14), (100000, 1), jnp.float32)
        return (x, src, dst, edge_type_8, edge_weight1)
    x, src, dst, edge_type_8, edge_weight1 = _rec_inputs()

    def _L0_gnn_setup():
        import jax, jax.numpy as jnp
        import numpy as np
        N = 3125
        E = 50000
        D_IN = 128
        D_HID = 128

        def _sage_conv(x, src, dst, Wl, b, Wr, n_nodes):
            msgs = x[src]
            agg = jax.ops.segment_sum(msgs, dst, num_segments=n_nodes)
            deg = jax.ops.segment_sum(jnp.ones((src.shape[0],), x.dtype), dst, num_segments=n_nodes)
            agg = agg / jnp.maximum(deg, 1.0)[:, None]
            return agg @ Wl + b + x @ Wr
        key = jax.random.key(seed)
        ks = jax.random.split(key, 8)
        x = jax.random.normal(ks[0], (N, D_IN), dtype=jnp.float32)
        edge_index = jax.random.randint(ks[1], (2, E), 0, N, dtype=jnp.int64)
        s = 1.0 / np.sqrt(D_IN)
        W1l = jax.random.uniform(ks[2], (D_IN, D_HID), jnp.float32, -s, s)
        b1 = jnp.zeros((D_HID,), jnp.float32)
        W1r = jax.random.uniform(ks[3], (D_IN, D_HID), jnp.float32, -s, s)
        s2 = 1.0 / np.sqrt(D_HID)
        W2l = jax.random.uniform(ks[4], (D_HID, D_HID), jnp.float32, -s2, s2)
        b2 = jnp.zeros((D_HID,), jnp.float32)
        W2r = jax.random.uniform(ks[5], (D_HID, D_HID), jnp.float32, -s2, s2)
        return {'x': x, 'edge_index': edge_index, 'W1l': W1l, 'b1': b1, 'W1r': W1r, 'W2l': W2l, 'b2': b2, 'W2r': W2r}
    _L0_gnn_all = _L0_gnn_setup()
    _L0_gnn_in = {k: v for k, v in _L0_gnn_all.items() if k in ('W1l', 'b1', 'W1r', 'W2l', 'b2', 'W2r')}
    del _L0_gnn_all

    def _L1_gnn_setup():
        import jax, jax.numpy as jnp
        import numpy as np
        import math
        HEADS = 8
        CH = 16
        SCALE = 1.0 / math.sqrt(CH)

        def _transformer_conv(x, src, dst, qw, qb, kw, kb, vw, vb, sw, sb):
            N = x.shape[0]
            q = (x @ qw + qb).reshape(N, HEADS, CH)
            k = (x @ kw + kb).reshape(N, HEADS, CH)
            v = (x @ vw + vb).reshape(N, HEADS, CH)
            alpha = jnp.sum(q[dst] * k[src], axis=-1) * SCALE
            m = jax.ops.segment_max(alpha, dst, num_segments=N)
            a = jnp.exp(alpha - m[dst])
            denom = jax.ops.segment_sum(a, dst, num_segments=N)
            a = a / denom[dst]
            msg = v[src] * a[:, :, None]
            out = jax.ops.segment_sum(msg, dst, num_segments=N).reshape(N, HEADS * CH)
            return out + x @ sw + sb
        key = jax.random.key(seed)
        ks = jax.random.split(key, 16)
        N, E, IN = (50000, 25000, 128)
        D = HEADS * CH

        def lin(k, fi, fo):
            return jax.random.normal(k, (fi, fo), jnp.float32) / math.sqrt(fi)
        inp = {'x': jax.random.normal(ks[0], (N, IN), jnp.float32), 'edge_index': jax.random.randint(ks[1], (2, E), 0, N, dtype=jnp.int64), 'edge_attr': jax.random.normal(ks[2], (E, 1), jnp.float32), 'q_w0': lin(ks[3], IN, D), 'q_b0': jnp.zeros((D,), jnp.float32), 'k_w0': lin(ks[4], IN, D), 'k_b0': jnp.zeros((D,), jnp.float32), 'v_w0': lin(ks[5], IN, D), 'v_b0': jnp.zeros((D,), jnp.float32), 's_w0': lin(ks[6], IN, D), 's_b0': jnp.zeros((D,), jnp.float32), 'q_w1': lin(ks[7], D, D), 'q_b1': jnp.zeros((D,), jnp.float32), 'k_w1': lin(ks[8], D, D), 'k_b1': jnp.zeros((D,), jnp.float32), 'v_w1': lin(ks[9], D, D), 'v_b1': jnp.zeros((D,), jnp.float32), 's_w1': lin(ks[10], D, D), 's_b1': jnp.zeros((D,), jnp.float32)}
        return inp
    _L1_gnn_all = _L1_gnn_setup()
    _L1_gnn_in = {k: v for k, v in _L1_gnn_all.items() if k in ('q_w0', 'q_b0', 'k_w0', 'k_b0', 'v_w0', 'v_b0', 's_w0', 's_b0', 'q_w1', 'q_b1', 'k_w1', 'k_b1', 'v_w1', 'v_b1', 's_w1', 's_b1')}
    del _L1_gnn_all

    def _L2_gnn_setup():
        import jax, jax.numpy as jnp
        import numpy as np
        N = 3125
        E = 50000
        D = 128
        H = 8
        HD = D // H
        T = 8

        def _layernorm(x, g, b, eps=1e-05):
            m = jnp.mean(x, axis=-1, keepdims=True)
            v = jnp.mean((x - m) ** 2, axis=-1, keepdims=True)
            return (x - m) * jax.lax.rsqrt(v + eps) * g + b
        key = jax.random.key(seed)
        ks = jax.random.split(key, 16)
        s = 0.02
        inp = {'x': jax.random.normal(ks[0], (N, D), jnp.float32), 'edge_index': jax.random.randint(ks[1], (2, E), 0, N, jnp.int32), 'edge_type': jax.random.randint(ks[2], (E,), 0, T, jnp.int32), 'Wq': jax.random.normal(ks[3], (D, D), jnp.float32) * s, 'bq': jnp.zeros((D,), jnp.float32), 'Wk': jax.random.normal(ks[4], (D, D), jnp.float32) * s, 'bk': jnp.zeros((D,), jnp.float32), 'Wv': jax.random.normal(ks[5], (D, D), jnp.float32) * s, 'bv': jnp.zeros((D,), jnp.float32), 'Wo': jax.random.normal(ks[6], (D, D), jnp.float32) * s, 'bo': jnp.zeros((D,), jnp.float32), 'edge_bias': jax.random.normal(ks[7], (T, H), jnp.float32) * s, 'W1': jax.random.normal(ks[8], (D, D), jnp.float32) * s, 'b1': jnp.zeros((D,), jnp.float32), 'W2': jax.random.normal(ks[9], (D, D), jnp.float32) * s, 'b2': jnp.zeros((D,), jnp.float32), 'g1': jnp.ones((D,), jnp.float32), 'be1': jnp.zeros((D,), jnp.float32), 'g2': jnp.ones((D,), jnp.float32), 'be2': jnp.zeros((D,), jnp.float32)}
        return inp
    _L2_gnn_all = _L2_gnn_setup()
    _L2_gnn_in = {k: v for k, v in _L2_gnn_all.items() if k in ('Wq', 'bq', 'Wk', 'bk', 'Wv', 'bv', 'Wo', 'bo', 'edge_bias', 'W1', 'b1', 'W2', 'b2', 'g1', 'be1', 'g2', 'be2')}
    del _L2_gnn_all

    def _L3_gnn_setup():
        import jax, jax.numpy as jnp
        import numpy as np
        N_NODES = 3125
        N_EDGES = 50000
        D_IN, D_HID, D_OUT = (128, 128, 128)

        def _gin_layer(h, src, dst, W, b):
            msgs = h[src]
            agg = jax.ops.segment_max(msgs, dst, num_segments=N_NODES)
            agg = jnp.where(jnp.isfinite(agg), agg, jnp.zeros_like(agg))
            return (h + agg) @ W + b
        key = jax.random.key(seed)
        ks = jax.random.split(key, 6)
        h = jax.random.normal(ks[0], (N_NODES, D_IN), dtype=jnp.float32)
        src = jax.random.randint(ks[1], (N_EDGES,), 0, N_NODES, dtype=jnp.int32)
        dst = jax.random.randint(ks[2], (N_EDGES,), 0, N_NODES, dtype=jnp.int32)
        W1 = jax.random.normal(ks[3], (D_IN, D_HID), dtype=jnp.float32) * (1.0 / np.sqrt(D_IN))
        b1 = jnp.zeros((D_HID,), dtype=jnp.float32)
        W2 = jax.random.normal(ks[4], (D_HID, D_OUT), dtype=jnp.float32) * (1.0 / np.sqrt(D_HID))
        b2 = jnp.zeros((D_OUT,), dtype=jnp.float32)
        return {'h': h, 'src': src, 'dst': dst, 'W1': W1, 'b1': b1, 'W2': W2, 'b2': b2}
    _L3_gnn_all = _L3_gnn_setup()
    _L3_gnn_in = {k: v for k, v in _L3_gnn_all.items() if k in ('W1', 'b1', 'W2', 'b2')}
    del _L3_gnn_all
    return {'x': x, 'src': src, 'dst': dst, 'edge_type_8': edge_type_8, 'edge_weight1': edge_weight1, 'L0_gnn_W1l': _L0_gnn_in['W1l'], 'L0_gnn_b1': _L0_gnn_in['b1'], 'L0_gnn_W1r': _L0_gnn_in['W1r'], 'L0_gnn_W2l': _L0_gnn_in['W2l'], 'L0_gnn_b2': _L0_gnn_in['b2'], 'L0_gnn_W2r': _L0_gnn_in['W2r'], 'L1_gnn_q_w0': _L1_gnn_in['q_w0'], 'L1_gnn_q_b0': _L1_gnn_in['q_b0'], 'L1_gnn_k_w0': _L1_gnn_in['k_w0'], 'L1_gnn_k_b0': _L1_gnn_in['k_b0'], 'L1_gnn_v_w0': _L1_gnn_in['v_w0'], 'L1_gnn_v_b0': _L1_gnn_in['v_b0'], 'L1_gnn_s_w0': _L1_gnn_in['s_w0'], 'L1_gnn_s_b0': _L1_gnn_in['s_b0'], 'L1_gnn_q_w1': _L1_gnn_in['q_w1'], 'L1_gnn_q_b1': _L1_gnn_in['q_b1'], 'L1_gnn_k_w1': _L1_gnn_in['k_w1'], 'L1_gnn_k_b1': _L1_gnn_in['k_b1'], 'L1_gnn_v_w1': _L1_gnn_in['v_w1'], 'L1_gnn_v_b1': _L1_gnn_in['v_b1'], 'L1_gnn_s_w1': _L1_gnn_in['s_w1'], 'L1_gnn_s_b1': _L1_gnn_in['s_b1'], 'L2_gnn_Wq': _L2_gnn_in['Wq'], 'L2_gnn_bq': _L2_gnn_in['bq'], 'L2_gnn_Wk': _L2_gnn_in['Wk'], 'L2_gnn_bk': _L2_gnn_in['bk'], 'L2_gnn_Wv': _L2_gnn_in['Wv'], 'L2_gnn_bv': _L2_gnn_in['bv'], 'L2_gnn_Wo': _L2_gnn_in['Wo'], 'L2_gnn_bo': _L2_gnn_in['bo'], 'L2_gnn_edge_bias': _L2_gnn_in['edge_bias'], 'L2_gnn_W1': _L2_gnn_in['W1'], 'L2_gnn_b1': _L2_gnn_in['b1'], 'L2_gnn_W2': _L2_gnn_in['W2'], 'L2_gnn_b2': _L2_gnn_in['b2'], 'L2_gnn_g1': _L2_gnn_in['g1'], 'L2_gnn_be1': _L2_gnn_in['be1'], 'L2_gnn_g2': _L2_gnn_in['g2'], 'L2_gnn_be2': _L2_gnn_in['be2'], 'L3_gnn_W1': _L3_gnn_in['W1'], 'L3_gnn_b1': _L3_gnn_in['b1'], 'L3_gnn_W2': _L3_gnn_in['W2'], 'L3_gnn_b2': _L3_gnn_in['b2']}

def reference(x, src, dst, edge_type_8, edge_weight1, L0_gnn_W1l, L0_gnn_b1, L0_gnn_W1r, L0_gnn_W2l, L0_gnn_b2, L0_gnn_W2r, L1_gnn_q_w0, L1_gnn_q_b0, L1_gnn_k_w0, L1_gnn_k_b0, L1_gnn_v_w0, L1_gnn_v_b0, L1_gnn_s_w0, L1_gnn_s_b0, L1_gnn_q_w1, L1_gnn_q_b1, L1_gnn_k_w1, L1_gnn_k_b1, L1_gnn_v_w1, L1_gnn_v_b1, L1_gnn_s_w1, L1_gnn_s_b1, L2_gnn_Wq, L2_gnn_bq, L2_gnn_Wk, L2_gnn_bk, L2_gnn_Wv, L2_gnn_bv, L2_gnn_Wo, L2_gnn_bo, L2_gnn_edge_bias, L2_gnn_W1, L2_gnn_b1, L2_gnn_W2, L2_gnn_b2, L2_gnn_g1, L2_gnn_be1, L2_gnn_g2, L2_gnn_be2, L3_gnn_W1, L3_gnn_b1, L3_gnn_W2, L3_gnn_b2):
    import jax
    import jax.numpy as jnp

    def _L0_gnn_ref(x, edge_index, W1l, b1, W1r, W2l, b2, W2r):
        import jax, jax.numpy as jnp
        import numpy as np
        N = 3125
        E = 50000
        D_IN = 128
        D_HID = 128

        def _sage_conv(x, src, dst, Wl, b, Wr, n_nodes):
            msgs = x[src]
            agg = jax.ops.segment_sum(msgs, dst, num_segments=n_nodes)
            deg = jax.ops.segment_sum(jnp.ones((src.shape[0],), x.dtype), dst, num_segments=n_nodes)
            agg = agg / jnp.maximum(deg, 1.0)[:, None]
            return agg @ Wl + b + x @ Wr
        src, dst = (edge_index[0], edge_index[1])
        h = jax.nn.relu(_sage_conv(x, src, dst, W1l, b1, W1r, N))
        h = jax.nn.relu(_sage_conv(h, src, dst, W2l, b2, W2r, N))
        return h

    def _L1_gnn_ref(x, edge_index, edge_attr, q_w0, q_b0, k_w0, k_b0, v_w0, v_b0, s_w0, s_b0, q_w1, q_b1, k_w1, k_b1, v_w1, v_b1, s_w1, s_b1):
        import jax, jax.numpy as jnp
        import numpy as np
        import math
        HEADS = 8
        CH = 16
        SCALE = 1.0 / math.sqrt(CH)

        def _transformer_conv(x, src, dst, qw, qb, kw, kb, vw, vb, sw, sb):
            N = x.shape[0]
            q = (x @ qw + qb).reshape(N, HEADS, CH)
            k = (x @ kw + kb).reshape(N, HEADS, CH)
            v = (x @ vw + vb).reshape(N, HEADS, CH)
            alpha = jnp.sum(q[dst] * k[src], axis=-1) * SCALE
            m = jax.ops.segment_max(alpha, dst, num_segments=N)
            a = jnp.exp(alpha - m[dst])
            denom = jax.ops.segment_sum(a, dst, num_segments=N)
            a = a / denom[dst]
            msg = v[src] * a[:, :, None]
            out = jax.ops.segment_sum(msg, dst, num_segments=N).reshape(N, HEADS * CH)
            return out + x @ sw + sb
        src, dst = (edge_index[0], edge_index[1])
        h = _transformer_conv(x, src, dst, q_w0, q_b0, k_w0, k_b0, v_w0, v_b0, s_w0, s_b0)
        h = jax.nn.relu(h)
        h = _transformer_conv(h, src, dst, q_w1, q_b1, k_w1, k_b1, v_w1, v_b1, s_w1, s_b1)
        return h

    def _L2_gnn_ref(x, edge_index, edge_type, Wq, bq, Wk, bk, Wv, bv, Wo, bo, edge_bias, W1, b1, W2, b2, g1, be1, g2, be2):
        import jax, jax.numpy as jnp
        import numpy as np
        N = 3125
        E = 50000
        D = 128
        H = 8
        HD = D // H
        T = 8

        def _layernorm(x, g, b, eps=1e-05):
            m = jnp.mean(x, axis=-1, keepdims=True)
            v = jnp.mean((x - m) ** 2, axis=-1, keepdims=True)
            return (x - m) * jax.lax.rsqrt(v + eps) * g + b
        n = x.shape[0]
        scale = HD ** (-0.5)
        Q = (x @ Wq + bq).reshape(n, H, HD)
        K = (x @ Wk + bk).reshape(n, H, HD)
        V = (x @ Wv + bv).reshape(n, H, HD)
        src, dst = (edge_index[0], edge_index[1])
        attn = jnp.sum(Q[dst] * K[src], axis=-1) * scale + edge_bias[edge_type]
        mx = jax.ops.segment_max(attn, dst, num_segments=n)
        ex = jnp.exp(attn - mx[dst])
        sm = jax.ops.segment_sum(ex, dst, num_segments=n)
        a = ex / (sm[dst] + 1e-16)
        out = jax.ops.segment_sum(a[..., None] * V[src], dst, num_segments=n)
        out = out.reshape(n, D) @ Wo + bo
        x = _layernorm(x + out, g1, be1)
        ffn = jax.nn.gelu(x @ W1 + b1, approximate=False) @ W2 + b2
        return _layernorm(x + ffn, g2, be2)

    def _L3_gnn_ref(h, src, dst, W1, b1, W2, b2):
        import jax, jax.numpy as jnp
        import numpy as np
        N_NODES = 3125
        N_EDGES = 50000
        D_IN, D_HID, D_OUT = (128, 128, 128)

        def _gin_layer(h, src, dst, W, b):
            msgs = h[src]
            agg = jax.ops.segment_max(msgs, dst, num_segments=N_NODES)
            agg = jnp.where(jnp.isfinite(agg), agg, jnp.zeros_like(agg))
            return (h + agg) @ W + b
        x = _gin_layer(h, src, dst, W1, b1)
        x = jax.nn.relu(x)
        x = _gin_layer(x, src, dst, W2, b2)
        return x
    edge_index = jnp.stack([src, dst])
    h = jnp.maximum(_layernorm(x, axis=-1), 0.0)
    x = x + _L0_gnn_ref(h, edge_index, L0_gnn_W1l, L0_gnn_b1, L0_gnn_W1r, L0_gnn_W2l, L0_gnn_b2, L0_gnn_W2r)
    h = jnp.maximum(_layernorm(x, axis=-1), 0.0)
    x = x + _L1_gnn_ref(h, edge_index, edge_weight1, L1_gnn_q_w0, L1_gnn_q_b0, L1_gnn_k_w0, L1_gnn_k_b0, L1_gnn_v_w0, L1_gnn_v_b0, L1_gnn_s_w0, L1_gnn_s_b0, L1_gnn_q_w1, L1_gnn_q_b1, L1_gnn_k_w1, L1_gnn_k_b1, L1_gnn_v_w1, L1_gnn_v_b1, L1_gnn_s_w1, L1_gnn_s_b1)
    h = jnp.maximum(_layernorm(x, axis=-1), 0.0)
    x = x + _L2_gnn_ref(h, edge_index, edge_type_8, L2_gnn_Wq, L2_gnn_bq, L2_gnn_Wk, L2_gnn_bk, L2_gnn_Wv, L2_gnn_bv, L2_gnn_Wo, L2_gnn_bo, L2_gnn_edge_bias, L2_gnn_W1, L2_gnn_b1, L2_gnn_W2, L2_gnn_b2, L2_gnn_g1, L2_gnn_be1, L2_gnn_g2, L2_gnn_be2)
    h = jnp.maximum(_layernorm(x, axis=-1), 0.0)
    x = x + _L3_gnn_ref(h, src, dst, L3_gnn_W1, L3_gnn_b1, L3_gnn_W2, L3_gnn_b2)
    return x

_drawn_inputs = setup_inputs


def setup_inputs(seed=0):
    import zlib

    import numpy as np

    out = dict(_drawn_inputs(seed))
    spreads = {'L0_gnn_b1': (0.0, 0.377),
     'L0_gnn_b2': (0.0, 0.1),
     'L1_gnn_q_b0': (0.0, 0.8),
     'L1_gnn_k_b0': (0.0, 2.0),
     'L1_gnn_v_b0': (0.0, 0.1),
     'L1_gnn_s_b0': (0.0, 0.1),
     'L1_gnn_q_b1': (0.0, 0.8),
     'L1_gnn_k_b1': (0.0, 2.0),
     'L1_gnn_v_b1': (0.0, 0.1),
     'L1_gnn_s_b1': (0.0, 0.1),
     'L2_gnn_bq': (0.0, 2.0),
     'L2_gnn_bk': (0.0, 2.0),
     'L2_gnn_bv': (0.0, 0.8),
     'L2_gnn_bo': (0.0, 0.35),
     'L2_gnn_b1': (0.0, 0.8),
     'L2_gnn_b2': (0.0, 0.343),
     'L2_gnn_g1': (1.0, 0.2),
     'L2_gnn_be1': (0.0, 0.311),
     'L2_gnn_g2': (1.0, 0.2),
     'L2_gnn_be2': (0.0, 0.335),
     'L3_gnn_b1': (0.0, 0.319),
     'L3_gnn_b2': (0.0, 0.481)}
    factors = {'L1_gnn_q_w0': 4.129,
     'L1_gnn_k_w0': 4.085,
     'L1_gnn_q_w1': 8.0,
     'L1_gnn_k_w1': 8.0,
     'L2_gnn_Wq': 8.0,
     'L2_gnn_Wk': 8.0,
     'L2_gnn_Wv': 4.838,
     'L2_gnn_Wo': 3.046,
     'L2_gnn_edge_bias': 64.0,
     'L2_gnn_W1': 8.0,
     'L2_gnn_W2': 8.0}
    for name, (base, spread) in spreads.items():
        noise = np.random.default_rng([zlib.crc32(name.encode()), seed]).standard_normal(out[name].shape)
        drawn = base * np.exp(spread * noise) if base else spread * noise
        out[name] = jnp.asarray(drawn.astype(out[name].dtype))
    for name, factor in factors.items():
        out[name] = (out[name] * factor).astype(out[name].dtype)
    return out
```

```python
from contextlib import ExitStack

import concourse.bass as bass
from concourse import mybir

F32 = mybir.dt.float32
BF16 = mybir.dt.bfloat16
I32 = mybir.dt.int32
U8 = mybir.dt.uint8
ALU = mybir.AluOpType
ACT = mybir.ActivationFunctionType
AX = mybir.AxisListType

P = 128
N = 3125
E = 100000
D = 128
HEADS = 8
CH = D // HEADS
TYPES = 8
NP = 125
NB = N // NP
GROUP = 7
RING = 4
LOOPS = 28
GROUPS = RING * LOOPS
STEPS = GROUP * GROUPS
EPAD = P * STEPS
FULL = E // STEPS
REST = E - FULL * STEPS
LO = 64
HI = -(-(N + 1) // LO)
AW = D + 2 * HEADS
PER_BANK = 4
BLOCKS = [(b, min(b + PER_BANK, NB)) for b in range(0, NB, PER_BANK)]
NBLK = len(BLOCKS)
NEG = -1.0e30
SCALE = CH ** -0.5
EPS = 1e-5
SUM, ATT, MAX = "sum", "att", "max"
KINDS = [SUM, SUM, ATT, ATT, ATT, MAX, MAX]
PASSES = len(KINDS)


def job_plan():
    plan, at = {}, 0

    def add(name, n):
        nonlocal at
        plan[name] = at
        at += n
    add("T_h0", NBLK)
    add("T_agg0", NBLK), add("lin0", NBLK), add("T_h1", NBLK)
    add("T_agg1", NBLK), add("lin1", NBLK), add("T_in2", NBLK), add("qkvs2", NB)
    add("T_in3", NBLK), add("qkvs3", NB)
    add("T_in4", NBLK), add("qkv4", NB)
    add("T_att4", NBLK), add("wo4", NBLK), add("T_ffn4", NBLK), add("up4", NBLK), add("down4", NBLK)
    add("T_z5", NBLK), add("lin5", NBLK)
    add("T_z6", NBLK), add("lin6", NBLK)
    return plan


def gnn_kernel(nc, A):
    JOB = job_plan()
    MARK = {}
    ctx = ExitStack()
    with ctx:
        def sb(name, shape, dt=F32):
            return ctx.enter_context(nc.sbuf_tensor(name, shape, dt))

        def sem(name):
            return ctx.enter_context(nc.semaphore(name))

        def dram(name, shape, dt=F32):
            return nc.dram_tensor(name, shape, dt, kind="Internal").ap()

        table = {k: dram(f"table{k}", [N, 2 * D if KINDS[k] == ATT else D]) for k in range(PASSES)}
        qtable = {k: dram(f"qtable{k}", [N, 2 * D]) for k in range(PASSES) if KINDS[k] == ATT}
        rows = {SUM: dram("rows_plain", [EPAD, D]), ATT: dram("rows_att", [EPAD, AW])}
        rows[MAX] = rows[SUM]
        carry = {SUM: dram("carry_sum", [P + 1, D]), ATT: dram("carry_att", [P + 1, AW]),
                 MAX: dram("carry_max", [P + 1, D])}
        node_info = dram("node_info", [2, HI * LO])

        arena = sb("arena", [P, RING * GROUP * 3 * D])
        ring = arena[:, 0:RING * GROUP * 2 * D].rearrange("p (s j w) -> p s j w", s=RING, j=GROUP)
        window = arena[:, RING * GROUP * 2 * D:RING * (GROUP + 1) * 2 * D].rearrange("p (s w) -> p s w", s=RING)
        outs = sb("outs", [P, RING * GROUP * AW])
        out_plain = outs[:, 0:RING * GROUP * D].rearrange("p (s j w) -> p s j w", s=RING, j=GROUP)
        out_att = outs[:, :].rearrange("p (s j w) -> p s j w", s=RING, j=GROUP)
        work = sb("work", [P, 7168])
        XR = sb("XR", [P, NB, D])
        H = sb("H", [P, NB, D])
        KEEP = sb("KEEP", [P, NB * D])
        src_i = sb("src_i", [P, STEPS], I32)
        dst_i = sb("dst_i", [P, STEPS], I32)
        same = sb("same", [P, STEPS])
        fence = sb("fence", [P, STEPS])
        bias = sb("bias", [P, STEPS, HEADS])
        W = sb("W", [P, 20, D])
        brow = sb("brow", [1, 17, D])
        affine = sb("affine", [P, 4, D])
        ebias = sb("ebias", [P, TYPES, HEADS])
        ident = sb("ident", [P, P])
        upper = sb("upper", [HI, HI])
        ones = sb("ones", [1, P])
        far_note = sb("far_note", [1, 1])
        lo_iota = sb("lo_iota", [P, LO])
        lo_iota_i = sb("lo_iota_i", [P, LO], I32)
        edges_iota_i = sb("edges_iota_i", [P, P], I32)
        part_ends = sb("part_ends", [P, P])
        zero_bf = sb("zero_bf", [P, LO], BF16)
        stage_late = sb("stage_late", [P, RING, GROUP], U8)
        stage = sb("stage", [P, RING, 2, GROUP], I32)
        hot_lo = sb("hot_lo", [P, 2, GROUP, LO], BF16)
        hot_hi = sb("hot_hi", [P, 2, GROUP, HI], BF16)
        late = sb("late", [P, STEPS], U8)
        slow_i = sb("slow_i", [P, 1], I32)
        before = sb("before", [P, 1], I32)
        small = sb("small", [P, 16])
        whole = sb("whole", [P, P])
        fenceT = sb("fenceT", [P, P])
        carT = sb("carT", [P, 3, P])
        carE = sb("carE", [P, 2, P])
        tails = sb("tails", [P, 3, D])
        crow = sb("crow", [P, AW])
        neutral = sb("neutral", [1, 3, AW])
        deg_sb = sb("deg_sb", [HI, LO])
        end_sb = sb("end_sb", [HI, LO])
        hist_tmp = sb("hist_tmp", [HI, LO])
        info = sb("info", [P, 12, NB])
        last_i = sb("last_i", [P, NB], I32)
        carry_i = sb("carry_i", [P, NB], I32)
        count_junk = sb("count_junk", [P, P])
        stat = sb("stat", [P, 4, NB])
        fences = sb("fences", [P, RING, HEADS, GROUP + 1])
        UA = sb("UA", [P, RING, 2, HEADS, GROUP + 1])
        MS = sb("MS", [P, RING, HEADS, GROUP + 1])
        LS = sb("LS", [P, RING, HEADS, GROUP + 1])
        DE = sb("DE", [P, 2, 2, HEADS, GROUP])
        LD = sb("LD", [P, 2, HEADS, GROUP + 1])
        LA = sb("LA", [P, 2, HEADS, GROUP + 1])

        last_rows = arena[0:NP, 0:NB * AW]
        more_rows = arena[0:NP, NB * AW:2 * NB * AW]
        T1 = arena[:, 2 * NB * AW:2 * NB * AW + NB * D].rearrange("p (i f) -> p i f", f=D)
        KVN = arena[0:NP, 0:NB * 2 * D].rearrange("p (i f) -> p i f", f=2 * D)
        QN = arena[0:NP, NB * 2 * D:NB * 3 * D].rearrange("p (i f) -> p i f", f=D)
        aT = work[:, 0:N]
        T2 = work[:, NB * D:2 * NB * D].rearrange("p (i f) -> p i f", f=D)
        KN = KEEP[:, :].rearrange("p (i f) -> p i f", f=D)
        comb = outs[:, 0:4 * NB * HEADS].rearrange("p (a i h) -> p a i h", a=4, h=HEADS)
        GD, GS = GROUP * D, (GROUP + 1) * D
        prod = work[:, 0:GD].rearrange("p (j f) -> p j f", j=GROUP)
        msg = [work[:, GD + b * GS:GD + (b + 1) * GS] for b in range(2)]
        dB = [work[:, GD + (2 + b) * GS:GD + (3 + b) * GS] for b in range(2)]
        OS = [work[:, GD + (4 + b) * GS:GD + (5 + b) * GS] for b in range(2)]
        lohi = work[:, 0:2 * STEPS].rearrange("p (a t) -> p a t", a=2)
        lohi_i = work[:, 2 * STEPS:4 * STEPS].bitcast(I32).rearrange("p (a t) -> p a t", a=2)
        typef = work[:, 4 * STEPS:5 * STEPS]
        type_i = work[:, 6 * STEPS:7 * STEPS].bitcast(I32)
        hot_ty = work[:, 5 * STEPS:5 * STEPS + GROUP * TYPES].rearrange("p (j k) -> p j k", k=TYPES)
        bias_k = work[:, 5 * STEPS + 64:5 * STEPS + 64 + GROUP * TYPES * HEADS].rearrange(
            "p (j h k) -> p j h k", k=TYPES, h=HEADS)

        def by_edge(a):
            return a.rearrange("p (f t) -> p t f", t=GROUP + 1)[:, 1:GROUP + 1, :]

        def column(a, t):
            return a.rearrange("p (f t) -> p f t", t=GROUP + 1)[:, :, t]

        bank = [ctx.enter_context(nc.psum_tensor(f"bank{b}", [P, 512], F32)) for b in range(4)]
        hist_ps = ctx.enter_context(nc.psum_tensor("hist_ps", [P, 512], F32))
        cin_ps = ctx.enter_context(nc.psum_tensor("cin_ps", [P, 512], F32))
        cout_ps = ctx.enter_context(nc.psum_tensor("cout_ps", [P, 512], F32))
        flag_ps = ctx.enter_context(nc.psum_tensor("flag_ps", [P, 512], F32))

        s_x = sem("x_loaded")
        s_edges = sem("edges_loaded")
        s_weights = sem("weights_loaded")
        s_const = sem("constants_made")
        s_zero = sem("constants_cleared")
        s_before = sem("before_loaded")
        s_flagT = sem("flags_transposed")
        s_vec = sem("vec_done")
        s_pe = sem("pe_jobs")
        s_act = sem("act_jobs")
        s_root = sem("roots_taken")
        s_exp = sem("node_exps")
        s_table = sem("tables_stored")
        s_idx = sem("indices_staged")
        s_land = [sem(f"rows_landed{s}") for s in range(RING)]
        s_window = [sem(f"windows_landed{s}") for s in range(RING)]
        s_query = sem("edge_queries_landed")
        s_laid = sem("queries_laid")
        s_far = sem("far_groups_summed")
        s_store = [sem(f"rows_stored{s}") for s in range(RING)]
        s_agg = sem("agg_steps")
        s_att = sem("att_steps")
        s_weigh = sem("weights_exped")
        s_rows = sem("att_rows_laid")
        s_hot = sem("hots_made")
        s_hist = sem("hist_groups")
        s_bias = sem("bias_steps")
        s_off = sem("offsets_summed")
        s_info = sem("node_info_stored")
        s_infold = sem("node_info_loaded")
        s_neutral = sem("neutral_stored")
        s_cin = sem("carry_turned")
        s_cexp = sem("carry_exps")
        s_cout = sem("carry_turned_back")
        s_crow = sem("carry_laid")
        s_carry = sem("carry_stored")
        s_node = sem("node_rows_landed")
        s_out = sem("output_stored")

        width = {SUM: D, MAX: D, ATT: 2 * D}
        idx_per = {SUM: 1, MAX: 1, ATT: 4}
        agg_base, att_base, land_base, weigh_base, idx_base, crow_base = {}, {}, {}, {}, {}, {0: 0}
        A_STEPS = {k: 7 + (k == 4) for k in range(PASSES)}
        B_STEPS = 5
        a = t = l = w = x = 0
        for k in range(PASSES):
            agg_base[k], att_base[k], land_base[k], weigh_base[k] = a, t, l, w
            idx_base[k] = x
            x += idx_per[KINDS[k]] * GROUPS
            crow_base[k + 1] = crow_base[k] + (3 if KINDS[k] == ATT else 1)
            l += 16 * GROUP * LOOPS
            if KINDS[k] == ATT:
                t += (A_STEPS[k] + B_STEPS) * GROUPS
                w += 3 * GROUPS
            else:
                a += STEPS
        rows_base = weigh_base

        def store_base(k):
            return 16 * LOOPS * k

        def after_a(k, g, i):
            first = A_STEPS[k] * g + B_STEPS * (g - 1)
            if isinstance(g, int) and g == 0:
                first = 0
            return first + att_base[k] + i

        def after_b(k, g, i):
            na = GROUPS if isinstance(g, int) and g == GROUPS - 1 else g + 2
            return na * A_STEPS[k] + B_STEPS * g + att_base[k] + i

        W_ORDER = ["L0_gnn_W1l", "L0_gnn_W1r", "L0_gnn_W2l", "L0_gnn_W2r",
                   "L1_gnn_k_w0", "L1_gnn_v_w0", "L1_gnn_q_w0", "L1_gnn_s_w0",
                   "L1_gnn_k_w1", "L1_gnn_v_w1", "L1_gnn_q_w1", "L1_gnn_s_w1",
                   "L2_gnn_Wk", "L2_gnn_Wv", "L2_gnn_Wq", "L2_gnn_Wo", "L2_gnn_W1", "L2_gnn_W2",
                   "L3_gnn_W1", "L3_gnn_W2"]
        B_ORDER = ["L0_gnn_b1", "L0_gnn_b2",
                   "L1_gnn_k_b0", "L1_gnn_v_b0", "L1_gnn_q_b0", "L1_gnn_s_b0",
                   "L1_gnn_k_b1", "L1_gnn_v_b1", "L1_gnn_q_b1", "L1_gnn_s_b1",
                   "L2_gnn_bk", "L2_gnn_bv", "L2_gnn_bq", "L2_gnn_bo", "L2_gnn_b2", "L3_gnn_b1", "L3_gnn_b2"]
        AFFINE = ["L2_gnn_g1", "L2_gnn_be1", "L2_gnn_g2", "L2_gnn_be2"]
        wi = {n: i for i, n in enumerate(W_ORDER)}
        bi = {n: i for i, n in enumerate(B_ORDER)}
        colb = sb("colb", [P, 1])
        N_WEIGHTS = len(W_ORDER) + len(B_ORDER) + len(AFFINE) + 2

        def cin_count(k):
            return k + 1

        def att_number(k):
            return [j for j in range(PASSES) if KINDS[j] == ATT].index(k)

        def table_count(k):
            return 16 * sum(5 if KINDS[j] == ATT else 1 for j in range(k + 1))

        def slot_out(k, s):
            return (out_att if KINDS[k] == ATT else out_plain)[:, s, :, :]

        block = ctx.enter_context(nc.Block())

        @block.vector
        def _(v):
            done = [0]

            def step(ins, mark=None):
                done[0] += 1
                ins.then_inc(s_vec, 1)
                v.wait_ge(s_vec, done[0])
                if mark:
                    MARK[mark] = done[0]

            def ready(semaphore, value):
                if not (isinstance(value, int) and value == 0):
                    v.wait_ge(semaphore, value)

            roots = [0]

            def norm(src, dst, tmp, relu=True, gain=None, shift=None, mark=None):
                s_, m_, r_, q_ = (stat[0:NP, i, :] for i in range(4))
                wide = [NP, NB, D]
                step(v.tensor_reduce(s_, src, AX.X, ALU.add))
                step(v.tensor_scalar(m_, s_, 1.0 / D, None, ALU.mult))
                step(v.tensor_tensor(dst, src, m_.unsqueeze(2).to_broadcast(wide), ALU.subtract))
                step(v.tensor_tensor(tmp, dst, dst, ALU.mult))
                step(v.tensor_reduce(s_, tmp, AX.X, ALU.add))
                step(v.tensor_scalar(r_, s_, 1.0 / D, EPS, ALU.mult, ALU.add), f"var{roots[0]}")
                roots[0] += 1
                v.wait_ge(s_root, roots[0])
                step(v.reciprocal(r_, q_))
                rb = r_.unsqueeze(2).to_broadcast(wide)
                if relu:
                    step(v.scalar_tensor_tensor(dst, dst, 0.0, rb, ALU.max, ALU.mult), mark)
                else:
                    step(v.tensor_tensor(dst, dst, rb, ALU.mult))
                    step(v.tensor_tensor(dst, dst, gain.unsqueeze(1).to_broadcast(wide), ALU.mult))
                    step(v.tensor_tensor(dst, dst, shift.unsqueeze(1).to_broadcast(wide), ALU.add), mark)

            def node(t3):
                return t3[0:NP, :, :]

            step(v.memset(src_i[:, :], 0))
            step(v.memset(dst_i[:, :], N))
            step(v.memset(type_i[:, :], 0))
            step(v.memset(before[:, :], -1), "pads")
            step(v.memset(outs[:, :], 0.0))
            step(v.memset(window, 0.0))
            step(v.memset(carT[:, 1, :], 1.0))
            step(v.memset(MS[:, :, :, :], 0.0))
            step(v.memset(LS[:, :, :, :], 0.0))
            step(v.memset(fences[:, :, :, :], NEG))
            step(v.memset(LD[:, :, :, :], 0.0))
            step(v.memset(ones[:, :], 1.0))
            step(v.memset(zero_bf[:, :], 0.0))
            step(v.memset(neutral[:, 0, :], 0.0))
            step(v.memset(neutral[:, 1, :], NEG))
            step(v.memset(neutral[:, 2, :], 0.0))
            step(v.memset(neutral[:, 2, D:D + HEADS], NEG), "consts")

            v.wait_ge(s_x, 16)
            norm(node(XR), node(H), node(T1), mark="h0")

            v.wait_ge(s_edges, 16 * 6)
            dstf = work[:, 0:STEPS]
            step(v.tensor_copy(dstf, dst_i[:, :]))
            step(v.memset(same[:, 0:1], 0.0))
            step(v.tensor_tensor(same[:, 1:STEPS], dstf[:, 1:STEPS], dstf[:, 0:STEPS - 1], ALU.is_equal))
            step(v.tensor_scalar(fence[:, :], same[:, :], -1.0, -NEG, ALU.add, ALU.mult), "flags")
            v.wait_ge(s_before, 16)
            step(v.tensor_copy(small[:, 0:1], before[:, :]))
            step(v.tensor_tensor(small[:, 1:2], dstf[:, 0:1], small[:, 0:1], ALU.is_equal))
            step(v.tensor_tensor(small[:, 2:3], dstf[:, 0:1], dstf[:, STEPS - 1:STEPS], ALU.is_equal))
            step(v.tensor_tensor(small[:, 3:4], small[:, 1:2], small[:, 2:3], ALU.mult))
            step(v.tensor_copy(tails[:, 0, :], small[:, 3:4].to_broadcast([P, P])), "whole")
            step(v.tensor_single_scalar(lohi_i[:, 0, :], dst_i[:, :], LO - 1, ALU.bitwise_and))
            step(v.tensor_single_scalar(lohi_i[:, 1, :], dst_i[:, :], LO.bit_length() - 1, ALU.arith_shift_right))
            step(v.tensor_scalar(dst_i[:, :], dst_i[:, :], float(N - 1), None, ALU.min))
            step(v.tensor_copy(dstf, dst_i[:, :]))
            by_group = dstf.rearrange("p (g j) -> p g j", j=GROUP)
            ahead = work[:, 5 * STEPS:6 * STEPS].rearrange("p (g j) -> p g j", j=GROUP)
            step(v.tensor_tensor(ahead, by_group, by_group[:, :, 0:1].to_broadcast([P, GROUPS, GROUP]),
                                 ALU.subtract))
            step(v.tensor_reduce(small[:, 5:6], ahead, AX.XY, ALU.max))
            step(v.tensor_scalar(small[:, 5:6], small[:, 5:6], 1.0, None, ALU.is_gt), "far")
            v.wait_ge(s_far, 1)
            step(v.tensor_scalar(slow_i[:, :], flag_ps[:, 300:301], 0.0, None, ALU.is_gt))
            step(v.tensor_scalar(small[:, 6:7], flag_ps[:, 300:301], 0.0, None, ALU.is_equal))
            step(v.tensor_scalar(late[:, :], work[:, 5 * STEPS:6 * STEPS], 0.0, small[:, 6:7], ALU.is_gt, ALU.mult),
                 "windows")
            step(v.tensor_copy(lohi[:, :, :], lohi_i[:, :, :]))
            step(v.tensor_copy(typef, type_i[:, :]))
            v.wait_ge(s_const, 2)
            step(v.tensor_copy(lo_iota[:, :], lo_iota_i[:, :]))
            step(v.tensor_copy(part_ends[:, :], edges_iota_i[:, :]))
            v.wait_ge(s_flagT, 1)
            step(v.tensor_copy(whole[:, :], flag_ps[:, 0:P]))
            step(v.tensor_scalar(fenceT[:, :], whole[:, :], -1.0, -NEG, ALU.add, ALU.mult), "whole_T")

            def plain_group(k, it, s):
                g = it * RING + s
                v.wait_ge(s_land[s], (it + 1) * (16 * GROUP) + land_base[k])
                ready(s_store[s], it * 16 + store_base(k))
                if k == 0:
                    hots(it, s)
                if k == 1:
                    edge_bias(it, s)
                first = it * (RING * GROUP) + s * GROUP
                flags = same if KINDS[k] == SUM else fence
                ops = (ALU.mult, ALU.add) if KINDS[k] == SUM else (ALU.add, ALU.max)
                for j in range(GROUP):
                    prev = out_plain[:, s, j - 1, :] if j else out_plain[:, (s - 1) % RING, GROUP - 1, :]
                    ready(s_agg, first + (agg_base[k] + j))
                    v.scalar_tensor_tensor(out_plain[:, s, j, :], prev, flags[:, bass.ds(first + j, 1)],
                                           ring_plain(s, j), *ops).then_inc(s_agg, 1)

            def ring_plain(s, j):
                return ring[:, s, j, 0:D]

            def hots(it, s):
                b = s % 2
                first = it * (RING * GROUP) + s * GROUP
                ready(s_hist, it * RING + s)
                v.tensor_tensor(hot_lo[:, b, :, :],
                                lohi[:, 0, bass.ds(first, GROUP)].unsqueeze(2).to_broadcast([P, GROUP, LO]),
                                lo_iota[:, :].unsqueeze(1).to_broadcast([P, GROUP, LO]),
                                ALU.is_equal).then_inc(s_hot, 1)
                v.tensor_tensor(hot_hi[:, b, :, :],
                                lohi[:, 1, bass.ds(first, GROUP)].unsqueeze(2).to_broadcast([P, GROUP, HI]),
                                lo_iota[:, 0:HI].unsqueeze(1).to_broadcast([P, GROUP, HI]),
                                ALU.is_equal).then_inc(s_hot, 1)

            def edge_bias(it, s):
                first = it * (RING * GROUP) + s * GROUP
                g3 = (it * RING + s) * 3
                ready(s_bias, g3)
                v.tensor_tensor(hot_ty[:, :, :],
                                typef[:, bass.ds(first, GROUP)].unsqueeze(2).to_broadcast([P, GROUP, TYPES]),
                                lo_iota[:, 0:TYPES].unsqueeze(1).to_broadcast([P, GROUP, TYPES]),
                                ALU.is_equal).then_inc(s_bias, 1)
                v.wait_ge(s_bias, g3 + 1)
                v.tensor_tensor(bias_k,
                                hot_ty.unsqueeze(2).to_broadcast([P, GROUP, HEADS, TYPES]),
                                ebias[:, :, :].rearrange("p k h -> p h k").unsqueeze(1).to_broadcast(
                                    [P, GROUP, HEADS, TYPES]), ALU.mult).then_inc(s_bias, 1)
                v.wait_ge(s_bias, g3 + 2)
                v.tensor_reduce(bias[:, bass.ds(first, GROUP), :], bias_k, AX.X, ALU.add).then_inc(s_bias, 1)

            def part_a(k, it, s, g):
                b = s % 2
                n = 0

                def chain(ins):
                    nonlocal n
                    n += 1
                    ins.then_inc(s_att, 1)
                    v.wait_ge(s_att, after_a(k, g, n))

                first = it * (RING * GROUP) + s * GROUP
                wide = [P, GROUP, D]
                v.wait_ge(s_laid, g + (att_number(k) * GROUPS + 1))
                n += 1
                v.tensor_copy(UA[:, s, 1, :, 0], MS[:, (s - 1) % RING, :, GROUP]).then_inc(s_att, 1)
                chain(v.copy_predicated(prod, stage_late[:, s, :].unsqueeze(2).to_broadcast(wide),
                                        window[:, s, D:2 * D].unsqueeze(1).to_broadcast(wide)))
                v.wait_ge(s_land[s], (it + 1) * (16 * GROUP) + land_base[k])
                chain(v.tensor_tensor(prod, prod, ring[:, s, :, 0:D], ALU.mult))
                scores = UA[:, s, 1, :, 1:GROUP + 1].rearrange("p h j -> p j h")
                chain(v.tensor_reduce(scores, prod.rearrange("p j (h c) -> p j h c", c=CH), AX.X, ALU.add))
                if k == 4:
                    chain(v.tensor_tensor(scores, scores, bias[:, bass.ds(first, GROUP), :], ALU.add))
                v.wait_ge(s_idx, g * 4 + (idx_base[k] + 4))
                chain(v.tensor_tensor_scan(flat(MS[:, s, :, :]), flat(fences[:, s, :, :]),
                                           flat(UA[:, s, 1, :, :]), 0.0, ALU.add, ALU.max))
                chain(v.tensor_tensor(UA[:, s, 0, :, 1:GROUP + 1], MS[:, s, :, 0:GROUP],
                                      fences[:, s, :, 1:GROUP + 1], ALU.add))
                chain(v.tensor_tensor(DE[:, b, :, :, :], UA[:, s, :, :, 1:GROUP + 1],
                                      MS[:, s, :, 1:GROUP + 1].unsqueeze(1).to_broadcast([P, 2, HEADS, GROUP]),
                                      ALU.subtract))
                assert n == A_STEPS[k]

            def flat(a):
                return a.rearrange("p h t -> p (h t)")

            def part_b(k, it, s, g):
                b = s % 2
                n = 0

                def chain(ins):
                    nonlocal n
                    n += 1
                    ins.then_inc(s_att, 1)
                    v.wait_ge(s_att, after_b(k, g, n))

                v.wait_ge(s_weigh, g * 3 + (weigh_base[k] + 3))
                chain(v.tensor_copy(LA[:, b, :, 0], LS[:, (s - 1) % RING, :, GROUP]))
                chain(v.tensor_tensor_scan(flat(LS[:, s, :, :]), flat(LD[:, b, :, :]), flat(LA[:, b, :, :]),
                                           0.0, ALU.mult, ALU.add))
                vals = ring[:, s, :, D:2 * D].rearrange("p j (h c) -> p j h c", c=CH)
                wts = LA[:, b, :, 1:GROUP + 1].rearrange("p h j -> p j h").unsqueeze(3).to_broadcast(
                    [P, GROUP, HEADS, CH])
                chain(v.tensor_tensor(by_edge(msg[b]).rearrange("p j (h c) -> p j h c", c=CH), vals, wts,
                                      ALU.mult))
                chain(v.tensor_copy(column(msg[b], 0), column(OS[1 - b], GROUP)))
                if not (isinstance(g, int) and g < 2):
                    v.wait_ge(s_rows, g * 3 + (rows_base[k] - 3))
                chain(v.tensor_tensor_scan(OS[b], dB[b], msg[b], 0.0, ALU.mult, ALU.add))
                assert n == B_STEPS

            def carry_scan(k):
                v.wait_ge(s_cin, cin_count(k))
                turned = cin_ps[:, 0:3 * P].rearrange("p (a q) -> p a q", a=3)
                if KINDS[k] == SUM:
                    step(v.tensor_tensor_scan(carT[:, 0, :], whole[:, :], turned[:, 0, :], 0.0,
                                              ALU.mult, ALU.add), f"carry{k}")
                elif KINDS[k] == MAX:
                    step(v.tensor_tensor_scan(carT[:, 0, :], fenceT[:, :], turned[:, 0, :], NEG,
                                              ALU.add, ALU.max), f"carry{k}")
                else:
                    m = carT[:, 1, :]
                    step(v.tensor_tensor_scan(m, fenceT[:, :], turned[:, 1, :], 0.0, ALU.add, ALU.max))
                    step(v.tensor_copy(carE[:, 0, 0:1], fenceT[:, 0:1]))
                    step(v.tensor_tensor(carE[:, 0, 1:P], m[:, 0:P - 1], fenceT[:, 1:P], ALU.add))
                    step(v.tensor_tensor(carE[:, 0, :], carE[:, 0, :], m, ALU.subtract))
                    step(v.tensor_tensor(carE[:, 1, :], turned[:, 1, :], m, ALU.subtract), f"carry_in{k}")
                    v.wait_ge(s_cexp, att_number(k) + 1)
                    for i in (0, 2):
                        step(v.tensor_tensor(carT[:, i, :], turned[:, i, :], carE[:, 1, :], ALU.mult))
                        step(v.tensor_tensor_scan(carT[:, i, :], carE[:, 0, :], carT[:, i, :], 0.0,
                                                  ALU.mult, ALU.add), f"carry{k}")

            def run_pass(k):
                if KINDS[k] != ATT:
                    for s in range(RING):
                        plain_group(k, 0, s)
                    with v.Fori(1, LOOPS) as it:
                        for s in range(RING):
                            plain_group(k, it, s)
                    v.wait_ge(s_agg, agg_base[k] + STEPS)
                else:
                    part_a(k, 0, 0, 0)
                    for s in range(RING):
                        att_group(k, 0, s)
                    with v.Fori(1, LOOPS - 1) as it:
                        for s in range(RING):
                            att_group(k, it, s)
                    for s in range(RING):
                        att_group(k, LOOPS - 1, s)
                    b = (RING - 1) % 2
                    step(v.tensor_copy(tails[:, 0, :], column(OS[b], GROUP)))
                    for i, a in ((1, MS), (2, LS)):
                        step(v.tensor_copy(tails[:, i, :].rearrange("p (h c) -> p h c", c=CH),
                                           a[:, RING - 1, :, GROUP].unsqueeze(2).to_broadcast([P, HEADS, CH])),
                             f"tails{k}")

            def att_group(k, it, s):
                g = it * RING + s
                if not (isinstance(it, int) and g == GROUPS - 1):
                    s1 = (s + 1) % RING
                    part_a(k, it + (1 if s == RING - 1 else 0), s1, g + 1)
                part_b(k, it, s, g)

            def node_tables():
                v.wait_ge(s_hist, GROUPS + 2)
                step(v.tensor_copy(deg_sb[:, :], hist_ps[0:HI, 0:LO]))
                step(v.memset(hist_tmp[:, :], 1.0))
                step(v.tensor_tensor_scan(end_sb[:, :], hist_tmp[:, :], deg_sb[:, :], 0.0, ALU.mult, ALU.add),
                     "row_totals")
                v.wait_ge(s_off, 1)
                step(v.tensor_copy(small[0:HI, 4:5], flag_ps[0:HI, 256:257]))
                step(v.tensor_scalar(end_sb[:, :], end_sb[:, :], small[0:HI, 4:5], None, ALU.add), "info")
                v.wait_ge(s_infold, 32)
                deg, end, has, last, first, part, thr, strad, rdeg = (info[0:NP, i, :] for i in range(9))
                step(v.tensor_scalar(has, deg, 1.0, None, ALU.min))
                step(v.tensor_scalar(last, end, -1.0, 0.0, ALU.add, ALU.max))
                step(v.tensor_tensor(first, end, deg, ALU.subtract))
                for i in range(NB):
                    step(v.tensor_scalar(count_junk[0:NP, :], part_ends[0:NP, :], last[:, i:i + 1], 0.0,
                                         ALU.is_le, ALU.add, accum_out=part[:, i:i + 1]))
                step(v.tensor_scalar(thr, part, float(STEPS), None, ALU.mult))
                step(v.tensor_tensor(strad, first, thr, ALU.is_lt))
                step(v.tensor_scalar(thr, part, -1.0 - P, None, ALU.add))
                step(v.tensor_tensor(thr, thr, strad, ALU.mult))
                step(v.tensor_scalar(carry_i[0:NP, :], thr, float(P), None, ALU.add))
                step(v.tensor_copy(last_i[0:NP, :], last))
                step(v.tensor_scalar(thr, deg, 1.0, None, ALU.max))
                step(v.reciprocal(rdeg, thr), "node_tables")

            has3 = info[0:NP, 2, :].unsqueeze(2).to_broadcast([NP, NB, D])
            rdeg3 = info[0:NP, 8, :].unsqueeze(2).to_broadcast([NP, NB, D])

            def plain_rows(k):
                v.wait_ge(s_node, 16 * 2 * NB * (k + 1))
                l3 = last_rows[:, 0:NB * D].rearrange("p (i f) -> p i f", f=D)
                m3 = more_rows[:, 0:NB * D].rearrange("p (i f) -> p i f", f=D)
                return l3, m3

            def joined(k, dst, last_mark=None):
                l3, m3 = plain_rows(k)
                step(v.tensor_tensor(dst, l3, m3, ALU.add if KINDS[k] == SUM else ALU.max))
                step(v.tensor_tensor(dst, dst, has3, ALU.mult))
                if KINDS[k] == SUM:
                    step(v.tensor_tensor(dst, dst, rdeg3, ALU.mult), last_mark)

            def attended(k, dst):
                v.wait_ge(s_node, 16 * 2 * NB * (k + 1))
                l3 = last_rows.rearrange("p (i f) -> p i f", f=AW)
                m3 = more_rows.rearrange("p (i f) -> p i f", f=AW)
                top, wl, wm, den = (comb[0:NP, i, :, :] for i in range(4))
                mx, dn = slice(D, D + HEADS), slice(D + HEADS, AW)
                step(v.tensor_tensor(top, l3[:, :, mx], m3[:, :, mx], ALU.max))
                step(v.tensor_tensor(wl, l3[:, :, mx], top, ALU.subtract))
                step(v.tensor_tensor(wm, m3[:, :, mx], top, ALU.subtract), f"parts{k}")
                v.wait_ge(s_exp, att_number(k) + 1)
                step(v.tensor_tensor(top, l3[:, :, dn], wl, ALU.mult))
                step(v.tensor_tensor(den, m3[:, :, dn], wm, ALU.mult))
                step(v.tensor_tensor(den, top, den, ALU.add))
                if k == 4:
                    step(v.tensor_scalar(den, den, 1e-16, None, ALU.add))
                step(v.reciprocal(top, den))
                step(v.tensor_tensor(top, top, info[0:NP, 2, :].unsqueeze(2).to_broadcast([NP, NB, HEADS]),
                                     ALU.mult))
                step(v.tensor_tensor(wl, wl, top, ALU.mult))
                step(v.tensor_tensor(wm, wm, top, ALU.mult))
                for rows3, wt in ((l3, wl), (m3, wm)):
                    vals = rows3[:, :, 0:D].rearrange("p i (h c) -> p i h c", c=CH)
                    step(v.tensor_tensor(vals, vals, wt.unsqueeze(3).to_broadcast([NP, NB, HEADS, CH]),
                                         ALU.mult))
                step(v.tensor_tensor(dst, l3[:, :, 0:D], m3[:, :, 0:D], ALU.add))

            run_pass(0)
            node_tables()
            carry_scan(0)
            joined(0, node(T1), "agg0")
            v.wait_ge(s_weights, 16 * N_WEIGHTS)
            run_pass(1)
            carry_scan(1)
            joined(1, node(T1), "agg1")
            v.wait_ge(s_act, JOB["lin1"] + NBLK)
            step(v.tensor_tensor(node(XR), node(XR), node(T2), ALU.add))
            norm(node(XR), node(H), node(T1), mark="in2")

            def clear_carries(k):
                v.wait_ge(s_act, JOB[{2: "qkvs2", 3: "qkvs3", 4: "qkv4"}[k]] + NB)
                step(v.memset(work[:, GD:GD + 6 * GS], 0.0), f"cleared{k}")

            clear_carries(2)
            run_pass(2)
            carry_scan(2)
            attended(2, node(T2))
            step(v.tensor_tensor(node(T2), node(T2), node(KN), ALU.add))
            step(v.tensor_scalar(node(T2), node(T2), 0.0, None, ALU.max), "in3")

            clear_carries(3)
            run_pass(3)
            carry_scan(3)
            attended(3, node(T2))
            step(v.tensor_tensor(node(T2), node(T2), node(KN), ALU.add))
            step(v.tensor_tensor(node(XR), node(XR), node(T2), ALU.add))
            norm(node(XR), node(H), node(T1), mark="in4")

            clear_carries(4)
            run_pass(4)
            carry_scan(4)
            attended(4, node(T2))
            MARK["att4"] = done[0]
            v.wait_ge(s_act, JOB["wo4"] + NBLK)
            step(v.tensor_tensor(node(T1), node(T1), node(H), ALU.add))
            norm(node(T1), node(T2), last_rows[:, 0:NB * D].rearrange("p (i f) -> p i f", f=D), relu=False,
                 gain=affine[0:NP, 0, :], shift=affine[0:NP, 1, :], mark="ffn4")
            v.wait_ge(s_act, JOB["down4"] + NBLK)
            step(v.tensor_tensor(node(T1), node(T1), node(T2), ALU.add))
            norm(node(T1), node(T2), last_rows[:, 0:NB * D].rearrange("p (i f) -> p i f", f=D), relu=False,
                 gain=affine[0:NP, 2, :], shift=affine[0:NP, 3, :])
            step(v.tensor_tensor(node(XR), node(XR), node(T2), ALU.add))
            norm(node(XR), node(H), node(T1), mark="h5")

            run_pass(5)
            carry_scan(5)
            joined(5, node(T1))
            step(v.tensor_tensor(node(T1), node(T1), node(H), ALU.add), "z5")
            run_pass(6)
            carry_scan(6)
            joined(6, node(T1))
            step(v.tensor_tensor(node(T1), node(T1), node(H), ALU.add), "z6")
            v.wait_ge(s_act, JOB["lin6"] + NBLK)
            step(v.tensor_tensor(node(XR), node(XR), node(T2), ALU.add), "result")

        @block.tensor
        def _(pe):
            def open_bank(j):
                if j >= 4:
                    pe.wait_ge(s_act, j - 3)
                return bank[j % 4]

            def turn(name, src, mark=None, jobs=None):
                if mark is not None:
                    pe.wait_ge(s_vec, MARK[mark])
                if jobs is not None:
                    pe.wait_ge(s_act, jobs)
                for n, (b0, b1) in enumerate(BLOCKS):
                    ps = open_bank(JOB[name] + n)
                    for i in range(b0, b1):
                        ins = pe.transpose(ps[:, (i - b0) * NP:(i - b0 + 1) * NP], src[0:NP, i, :],
                                           ident[0:NP, 0:NP])
                    ins.then_inc(s_pe, 1)

            def linear(name, terms, b_at, xt_name):
                for n, (b0, b1) in enumerate(BLOCKS):
                    ps = open_bank(JOB[name] + n)
                    pe.wait_ge(s_act, JOB[xt_name] + n + 1)
                    for i in range(b0, b1):
                        acc = ps[0:NP, (i - b0) * D:(i - b0 + 1) * D]
                        for m, (xt, w_at) in enumerate(terms):
                            pe.matmul(acc, xt[:, i * NP:(i + 1) * NP], W[:, w_at, :], start=(m == 0), stop=False)
                        ins = pe.matmul(acc, ones[0:1, 0:NP], brow[0:1, b_at, :], start=False, stop=True)
                    ins.then_inc(s_pe, 1)

            def project(name, xt, w_at, n_w, b_at, xt_name):
                for i in range(NB):
                    ps = open_bank(JOB[name] + i)
                    pe.wait_ge(s_act, JOB[xt_name] + i // PER_BANK + 1)
                    acc = ps[0:NP, 0:n_w * D]
                    pe.matmul(acc, xt[:, i * NP:(i + 1) * NP], W[:, w_at:w_at + n_w, :], start=True, stop=False)
                    pe.matmul(acc, ones[0:1, 0:NP], brow[0:1, b_at:b_at + n_w, :], start=False, stop=True)\
                        .then_inc(s_pe, 1)

            def carry_turns(k):
                n = 3 if KINDS[k] == ATT else 1
                if KINDS[k] == ATT:
                    pe.wait_ge(s_vec, MARK[f"tails{k}"])
                else:
                    pe.wait_ge(s_agg, agg_base[k] + STEPS)
                for i in range(n):
                    src = tails[:, i, :] if KINDS[k] == ATT else out_plain[:, RING - 1, GROUP - 1, :]
                    ins = pe.transpose(cin_ps[:, i * P:(i + 1) * P], src, ident[:, :])
                ins.then_inc(s_cin, 1)
                pe.wait_ge(s_vec, MARK[f"carry{k}"])
                if k:
                    pe.wait_ge(s_crow, crow_base[k])
                for i in range(n):
                    ins = pe.transpose(cout_ps[:, i * P:(i + 1) * P], carT[:, i, :], ident[:, :])
                ins.then_inc(s_cout, 1)

            pe.wait_ge(s_const, 4)
            pe.wait_ge(s_vec, MARK["whole"])
            pe.matmul(flag_ps[:, 0:P], tails[:, 0, :], ident[:, :], start=True, stop=True).then_inc(s_flagT, 1)
            pe.wait_ge(s_vec, MARK["far"])
            pe.matmul(flag_ps[:, 300:301], carT[:, 1, :], small[:, 5:6], start=True, stop=True).then_inc(s_far, 1)
            turn("T_h0", H, "h0")
            pe.matmul(hist_ps[0:HI, 0:LO], zero_bf[:, 0:HI], zero_bf[:, :], start=True, stop=False,
                      skip_group_check=True).then_inc(s_hist, 1)
            with pe.Fori(0, LOOPS) as it:
                for s in range(RING):
                    pe.wait_ge(s_hot, (it * RING + (s + 1)) * 2)
                    for j in range(GROUP):
                        ins = pe.matmul(hist_ps[0:HI, 0:LO], hot_hi[:, s % 2, j, :], hot_lo[:, s % 2, j, :],
                                        start=False, stop=False, skip_group_check=True)
                    ins.then_inc(s_hist, 1)
            pe.matmul(hist_ps[0:HI, 0:LO], zero_bf[:, 0:HI], zero_bf[:, :], start=False, stop=True,
                      skip_group_check=True).then_inc(s_hist, 1)
            pe.wait_ge(s_vec, MARK["row_totals"])
            pe.matmul(flag_ps[0:HI, 256:257], upper[:, :], end_sb[:, LO - 1:LO], start=True, stop=True)\
                .then_inc(s_off, 1)
            carry_turns(0)
            pe.wait_ge(s_weights, 16 * N_WEIGHTS)
            turn("T_agg0", T1, "agg0")
            linear("lin0", [(aT, wi["L0_gnn_W1l"]), (KEEP, wi["L0_gnn_W1r"])], bi["L0_gnn_b1"], "T_agg0")
            turn("T_h1", H, None, JOB["lin0"] + NBLK)
            carry_turns(1)
            turn("T_agg1", T1, "agg1")
            linear("lin1", [(aT, wi["L0_gnn_W2l"]), (KEEP, wi["L0_gnn_W2r"])], bi["L0_gnn_b2"], "T_agg1")
            turn("T_in2", H, "in2")
            project("qkvs2", aT, wi["L1_gnn_k_w0"], 4, bi["L1_gnn_k_b0"], "T_in2")
            carry_turns(2)
            turn("T_in3", T2, "in3")
            project("qkvs3", aT, wi["L1_gnn_k_w1"], 4, bi["L1_gnn_k_b1"], "T_in3")
            carry_turns(3)
            turn("T_in4", H, "in4")
            project("qkv4", aT, wi["L2_gnn_Wk"], 3, bi["L2_gnn_bk"], "T_in4")
            carry_turns(4)
            turn("T_att4", T2, "att4")
            linear("wo4", [(aT, wi["L2_gnn_Wo"])], bi["L2_gnn_bo"], "T_att4")
            turn("T_ffn4", T2, "ffn4")
            for n, (b0, b1) in enumerate(BLOCKS):
                ps = open_bank(JOB["up4"] + n)
                pe.wait_ge(s_act, JOB["T_ffn4"] + n + 1)
                pe.matmul(ps[:, 0:(b1 - b0) * NP], W[:, wi["L2_gnn_W1"], :], KEEP[:, b0 * NP:b1 * NP],
                          start=True, stop=True).then_inc(s_pe, 1)
            linear("down4", [(aT, wi["L2_gnn_W2"])], bi["L2_gnn_b2"], "up4")
            carry_turns(5)
            turn("T_z5", T1, "z5")
            linear("lin5", [(aT, wi["L3_gnn_W1"])], bi["L3_gnn_b1"], "T_z5")
            carry_turns(6)
            turn("T_z6", T1, "z6")
            linear("lin6", [(aT, wi["L3_gnn_W2"])], bi["L3_gnn_b2"], "T_z6")

        @block.scalar
        def _(act):
            def evacuate(name, n, dst, func=ACT.Copy, **more):
                j = JOB[name] + n
                act.wait_ge(s_pe, j + 1)
                return act.activation(dst, bank_view(j, dst), func, **more)

            def bank_view(j, dst):
                shape = list(dst.shape)
                n = 1
                for d in shape[1:]:
                    n *= d
                flat = bank[j % 4][0:shape[0], 0:n]
                return flat if len(shape) == 2 else flat.rearrange("p (i f) -> p i f", f=shape[2])

            def turned(name, dst):
                for n, (b0, b1) in enumerate(BLOCKS):
                    evacuate(name, n, dst[:, b0 * NP:b1 * NP]).then_inc(s_act, 1)

            def laid(name, dst, func=ACT.Copy):
                for n, (b0, b1) in enumerate(BLOCKS):
                    evacuate(name, n, dst[0:NP, b0:b1, :], func).then_inc(s_act, 1)

            def projected(name, n_w):
                for i in range(NB):
                    j = JOB[name] + i
                    ps = bank[j % 4][0:NP, :]
                    act.wait_ge(s_pe, j + 1)
                    act.activation(KVN[:, i, :], ps[:, 0:2 * D], ACT.Copy)
                    if n_w == 4:
                        act.activation(KN[0:NP, i, :], ps[:, 3 * D:4 * D], ACT.Copy)
                    act.activation(QN[:, i, :], ps[:, 2 * D:3 * D], ACT.Copy, scale=SCALE).then_inc(s_act, 1)

            def root(n):
                act.wait_ge(s_vec, MARK[f"var{n}"])
                act.activation(stat[0:NP, 3, :], stat[0:NP, 2, :], ACT.Sqrt).then_inc(s_root, 1)

            def stage_group(k, it, s, far=False):
                first = it * (RING * GROUP) + s * GROUP
                act.copy(stage[:, s, 0, :], src_i[:, bass.ds(first, GROUP)]).then_inc(s_idx, 1)
                if KINDS[k] == ATT:
                    act.copy(stage_late[:, s, :], late[:, bass.ds(first, GROUP)]).then_inc(s_idx, 1)
                    act.activation(stage[:, s, 1, :], dst_i[:, bass.ds(first, GROUP)], ACT.Copy,
                                   scale=2.0 if far else 1.0).then_inc(s_idx, 1)
                    act.copy(fences[:, s, :, 1:GROUP + 1],
                             fence[:, bass.ds(first, GROUP)].unsqueeze(1).to_broadcast([P, HEADS, GROUP]))\
                        .then_inc(s_idx, 1)

            def weigh(k, s, g):
                b = s % 2
                act.wait_ge(s_att, after_a(k, g, A_STEPS[k]))
                act.activation(LD[:, b, :, 1:GROUP + 1], DE[:, b, 0, :, :], ACT.Exp).then_inc(s_weigh, 1)
                act.activation(LA[:, b, :, 1:GROUP + 1], DE[:, b, 1, :, :], ACT.Exp).then_inc(s_weigh, 1)
                act.activation(dB[b].rearrange("p (h c t) -> p h c t", h=HEADS, c=CH)[:, :, :, 1:GROUP + 1],
                               DE[:, b, 0, :, :].unsqueeze(2).to_broadcast([P, HEADS, CH, GROUP]), ACT.Exp)\
                    .then_inc(s_weigh, 1)

            def lay_rows(k, it, s, g):
                act.wait_ge(s_att, after_b(k, g, B_STEPS))
                act.wait_ge(s_store[s], it * 16 + store_base(k))
                act.copy(out_att[:, s, :, 0:D], by_edge(OS[s % 2])).then_inc(s_rows, 1)
                act.copy(out_att[:, s, :, D:D + HEADS],
                         MS[:, s, :, 1:GROUP + 1].rearrange("p h j -> p j h")).then_inc(s_rows, 1)
                act.copy(out_att[:, s, :, D + HEADS:AW],
                         LS[:, s, :, 1:GROUP + 1].rearrange("p h j -> p j h")).then_inc(s_rows, 1)

            def lay_queries(k, it, s, g, far):
                done = g + (att_number(k) * GROUPS + 1)
                if far:
                    act.wait_ge(s_query, done * (16 * GROUP))
                    act.copy(far_note[:, :], ones[0:1, 0:1]).then_inc(s_laid, 1)
                else:
                    act.wait_ge(s_window[s], it * 16 + (att_number(k) * LOOPS + 1) * 16)
                    act.copy(prod, window[:, s, 0:D].unsqueeze(1).to_broadcast([P, GROUP, D])).then_inc(s_laid, 1)

            def att_pass(k, far):
                for s in range(RING):
                    stage_group(k, 0, s, far)
                lay_queries(k, 0, 0, 0, far)
                weigh(k, 0, 0)
                lay_queries(k, 0, 1, 1, far)
                with act.Fori(0, LOOPS - 1) as it:
                    for s in range(RING):
                        g = it * RING + s
                        weigh(k, (s + 1) % RING, g + 1)
                        lay_queries(k, it + (s + 2) // RING, (s + 2) % RING, g + 2, far)
                        lay_rows(k, it, s, g)
                        stage_group(k, it + 1, s, far)
                for s in range(RING):
                    g = (LOOPS - 1) * RING + s
                    if s + 1 < RING:
                        weigh(k, s + 1, g + 1)
                    if s + 2 < RING:
                        lay_queries(k, LOOPS - 1, s + 2, g + 2, far)
                    lay_rows(k, LOOPS - 1, s, g)

            def run_pass(k):
                if KINDS[k] == ATT:
                    with act.If(slow > 0):
                        att_pass(k, True)
                    with act.Else():
                        att_pass(k, False)
                    return
                for s in range(RING):
                    stage_group(k, 0, s)
                with act.Fori(0, LOOPS - 1) as it:
                    for s in range(RING):
                        act.wait_ge(s_agg, it * (RING * GROUP) + (agg_base[k] + (s + 1) * GROUP))
                        stage_group(k, it + 1, s)

            def carry_rows(k):
                if KINDS[k] == ATT:
                    act.wait_ge(s_vec, MARK[f"carry_in{k}"])
                    act.activation(carE[:, :, :], carE[:, :, :], ACT.Exp).then_inc(s_cexp, 1)
                act.wait_ge(s_cout, k + 1)
                if k:
                    act.wait_ge(s_carry, 16 * k)
                act.copy(crow[:, 0:D], cout_ps[:, 0:D]).then_inc(s_crow, 1)
                if KINDS[k] == ATT:
                    for i in (1, 2):
                        act.copy(crow[:, D + (i - 1) * HEADS:D + i * HEADS],
                                 cout_ps[:, i * D:(i + 1) * D].rearrange("p (h c) -> p h c", c=CH)[:, :, 0])\
                            .then_inc(s_crow, 1)

            def node_exps(k):
                act.wait_ge(s_vec, MARK[f"parts{k}"])
                act.activation(comb[0:NP, 1:3, :, :], comb[0:NP, 1:3, :, :], ACT.Exp).then_inc(s_exp, 1)

            root(0)
            act.wait_ge(s_edges, 16 * 6)
            turned("T_h0", KEEP)
            run_pass(0)
            carry_rows(0)
            turned("T_agg0", aT)
            act.wait_ge(s_table, table_count(0))
            laid("lin0", H, ACT.Relu)
            turned("T_h1", KEEP)
            run_pass(1)
            carry_rows(1)
            turned("T_agg1", aT)
            laid("lin1", T2, ACT.Relu)
            root(1)
            act.wait_ge(s_vec, MARK["windows"])
            slow = act.value_load(slow_i[0:1, 0:1], min_val=0, max_val=1)
            turned("T_in2", aT)
            projected("qkvs2", 4)
            run_pass(2)
            carry_rows(2)
            node_exps(2)
            turned("T_in3", aT)
            projected("qkvs3", 4)
            run_pass(3)
            carry_rows(3)
            node_exps(3)
            root(2)
            turned("T_in4", aT)
            projected("qkv4", 3)
            run_pass(4)
            carry_rows(4)
            node_exps(4)
            turned("T_att4", aT)
            laid("wo4", T1)
            root(3)
            turned("T_ffn4", KEEP)
            for n, (b0, b1) in enumerate(BLOCKS):
                evacuate("up4", n, aT[:, b0 * NP:b1 * NP], ACT.Gelu, bias=colb[:, 0:1]).then_inc(s_act, 1)
            laid("down4", T1)
            root(4)
            root(5)
            run_pass(5)
            carry_rows(5)
            turned("T_z5", aT)
            act.wait_ge(s_table, table_count(5))
            laid("lin5", H, ACT.Relu)
            run_pass(6)
            carry_rows(6)
            turned("T_z6", aT)
            laid("lin6", T2)

        @block.sync
        def _(sp):
            def by_part(a):
                return a.rearrange("(p i) f -> p i f", i=NB)

            sp.dma_start(XR[0:NP, :, :], by_part(A["x"])).then_inc(s_x, 16)
            sp.wait_ge(s_vec, MARK["pads"])
            for dst, name in ((src_i, "src"), (dst_i, "dst"), (type_i, "edge_type_8")):
                sp.dma_start(dst[0:FULL, :], A[name][0:FULL * STEPS].rearrange("(p t) -> p t", t=STEPS))\
                    .then_inc(s_edges, 16)
                sp.dma_start(dst[FULL:FULL + 1, 0:REST], A[name][FULL * STEPS:E].rearrange("(p t) -> p t", p=1))\
                    .then_inc(s_edges, 16)
            sp.dma_start(before[1:FULL + 1, :],
                         A["dst"][0:FULL * STEPS].rearrange("(p t) -> p t", t=STEPS)[:, STEPS - 1:STEPS],
                         allow_slow_non_contiguous=True).then_inc(s_before, 16)
            for i, n in enumerate(W_ORDER):
                sp.dma_start(W[:, i, :], A[n]).then_inc(s_weights, 16)
            for i, n in enumerate(B_ORDER):
                sp.dma_start(brow[0:1, i, :], A[n].unsqueeze(0)).then_inc(s_weights, 16)
            for i, n in enumerate(AFFINE):
                sp.dma_start(affine[:, i, :], A[n].partition_broadcast(P)).then_inc(s_weights, 16)
            sp.dma_start(ebias[:, :, :].rearrange("p k h -> p (k h)"),
                         A["L2_gnn_edge_bias"].rearrange("k h -> (k h)").partition_broadcast(P))\
                .then_inc(s_weights, 16)
            sp.dma_start(colb[:, :], A["L2_gnn_b1"].unsqueeze(1), allow_slow_non_contiguous=True).then_inc(s_weights, 16)
            sp.wait_ge(s_vec, MARK["consts"])
            for i, kind in enumerate((SUM, MAX, ATT)):
                w = AW if kind == ATT else D
                sp.dma_start(carry[kind][P:P + 1, :], neutral[0:1, i, 0:w]).then_inc(s_neutral, 16)

            def store_rows(k):
                w = AW if KINDS[k] == ATT else D
                dst = rows[KINDS[k]].rearrange("(p t) f -> p (t f)", t=STEPS)
                with sp.Fori(0, LOOPS) as it:
                    for s in range(RING):
                        g = it * RING + s
                        if KINDS[k] == ATT:
                            sp.wait_ge(s_rows, g * 3 + (rows_base[k] + 3))
                        else:
                            sp.wait_ge(s_agg, g * GROUP + (agg_base[k] + GROUP))
                        sp.dma_start(dst[:, bass.ds(g * (GROUP * w), GROUP * w)],
                                     slot_out(k, s).rearrange("p j f -> p (j f)")).then_inc(s_store[s], 16)

            def store_carry(k):
                w = AW if KINDS[k] == ATT else D
                sp.wait_ge(s_crow, crow_base[k + 1])
                sp.dma_start(carry[KINDS[k]][0:P, :], crow[:, 0:w]).then_inc(s_carry, 16)

            def after_pass(k):
                store_rows(k)
                if k == 0:
                    sp.wait_ge(s_vec, MARK["info"])
                    for i, a in enumerate((deg_sb, end_sb)):
                        sp.dma_start(node_info[i].rearrange("(h l) -> h l", l=LO), a[:, :]).then_inc(s_info, 16)
                    sp.wait_ge(s_info, 32)
                    for i in range(2):
                        sp.dma_start(info[0:NP, i, :], node_info[i, 0:N].rearrange("(p i) -> p i", i=NB))\
                            .then_inc(s_infold, 16)
                store_carry(k)

            def store_qkv(k, name):
                sp.wait_ge(s_act, JOB[name] + NB)
                sp.dma_start(by_part(table[k]), KVN).then_inc(s_table, 16)
                at, after = by_part(qtable[k][:, 0:D]), by_part(qtable[k][:, D:2 * D])
                sp.dma_start(at, QN).then_inc(s_table, 16)
                sp.dma_start(after[:, 0:NB - 1, :], QN[:, 1:NB, :]).then_inc(s_table, 16)
                sp.dma_start(after[0:NP - 1, NB - 1, :], QN[1:NP, 0, :]).then_inc(s_table, 16)
                sp.dma_start(after[NP - 1:NP, NB - 1, :], QN[NP - 1:NP, NB - 1, :]).then_inc(s_table, 16)

            sp.wait_ge(s_vec, MARK["h0"])
            sp.dma_start(by_part(table[0]), H[0:NP, :, :]).then_inc(s_table, 16)
            after_pass(0)
            sp.wait_ge(s_act, JOB["lin0"] + NBLK)
            sp.dma_start(by_part(table[1]), H[0:NP, :, :]).then_inc(s_table, 16)
            after_pass(1)
            store_qkv(2, "qkvs2")
            after_pass(2)
            store_qkv(3, "qkvs3")
            after_pass(3)
            store_qkv(4, "qkv4")
            after_pass(4)
            sp.wait_ge(s_vec, MARK["h5"])
            sp.dma_start(by_part(table[5]), H[0:NP, :, :]).then_inc(s_table, 16)
            after_pass(5)
            sp.wait_ge(s_act, JOB["lin5"] + NBLK)
            sp.dma_start(by_part(table[6]), H[0:NP, :, :]).then_inc(s_table, 16)
            after_pass(6)
            sp.wait_ge(s_vec, MARK["result"])
            sp.dma_start(by_part(A["out"]), XR[0:NP, :, :]).then_inc(s_out, 16)
            sp.wait_ge(s_out, 16)

        @block.gpsimd
        def _(pool):
            pool.iota(lo_iota_i[:, :], [[1, LO]], base=0, channel_multiplier=0).then_inc(s_const, 1)
            pool.iota(edges_iota_i[:, :], [[STEPS, P]], base=STEPS, channel_multiplier=0).then_inc(s_const, 1)
            pool.memset(ident[:, :], 0.0).then_inc(s_zero, 1)
            pool.memset(upper[:, :], 1.0).then_inc(s_zero, 1)
            pool.wait_ge(s_zero, 2)
            pool.affine_select(out=ident[:, :], in_=ident[:, :], compare_op=ALU.not_equal, fill=1.0, base=0,
                               pattern=[[-1, P]], channel_multiplier=1).then_inc(s_const, 1)
            pool.affine_select(out=upper[:, :], in_=upper[:, :], compare_op=ALU.is_gt, fill=0.0, base=0,
                               pattern=[[1, HI]], channel_multiplier=-1).then_inc(s_const, 1)

            def fetch(dst, tab, idx, done):
                pool.indirect_dma_start(dst, None, tab, bass.IndirectOffsetOnAxis(ap=idx, axis=0))\
                    .then_inc(done, 16)

            def rows_of_group(k, s):
                for j in range(GROUP):
                    fetch(ring[:, s, j, 0:width[KINDS[k]]], table[k], stage[:, s, 0, j:j + 1], s_land[s])

            def staged(k, it, s):
                per = idx_per[KINDS[k]]
                pool.wait_ge(s_idx, (it * RING + s) * per + (idx_base[k] + per))
                pool.nop(nofuse=True)

            def far_group(k, it, s):
                g = it * RING + s
                staged(k, it, s)
                rows_of_group(k, s)
                if not (isinstance(it, int) and g == 0):
                    pool.wait_ge(s_att, after_a(k, g - 1, A_STEPS[k]))
                    pool.nop(nofuse=True)
                for j in range(GROUP):
                    fetch(prod[:, j, :], qtable[k].rearrange("n (a f) -> (n a) f", a=2),
                          stage[:, s, 1, j:j + 1], s_query)

            def run_pass(k):
                pool.wait_ge(s_table, table_count(k))
                if KINDS[k] != ATT:
                    with pool.Fori(0, LOOPS) as it:
                        for s in range(RING):
                            staged(k, it, s)
                            rows_of_group(k, s)
                    return
                with pool.If(slow > 0):
                    for s in range(RING):
                        far_group(k, 0, s)
                    with pool.Fori(1, LOOPS) as it:
                        for s in range(RING):
                            far_group(k, it, s)
                with pool.Else():
                    with pool.Fori(0, LOOPS) as it:
                        for s in range(RING):
                            staged(k, it, s)
                            fetch(window[:, s, :], qtable[k], stage[:, s, 1, 0:1], s_window[s])
                            rows_of_group(k, s)

            def fetch_nodes(k):
                w = AW if KINDS[k] == ATT else D
                if k == 0:
                    pool.wait_ge(s_vec, MARK["node_tables"])
                    pool.wait_ge(s_neutral, 48)
                for s in range(RING):
                    pool.wait_ge(s_store[s], store_base(k + 1))
                for i in range(NB):
                    fetch(last_rows[:, i * w:(i + 1) * w], rows[KINDS[k]], last_i[0:NP, i:i + 1], s_node)
                pool.wait_ge(s_carry, 16 * (k + 1))
                for i in range(NB):
                    fetch(more_rows[:, i * w:(i + 1) * w], carry[KINDS[k]], carry_i[0:NP, i:i + 1], s_node)

            pool.wait_ge(s_const, 4)
            run_pass(0)
            fetch_nodes(0)
            pool.wait_ge(s_vec, MARK["windows"])
            slow = pool.value_load(slow_i[0:1, 0:1], min_val=0, max_val=1)
            for k in range(1, PASSES):
                run_pass(k)
                fetch_nodes(k)


_UNUSED = ("edge_weight1",)


def kernel(**inputs):
    import numpy as _np
    import concourse.bacc as _bacc
    from concourse import mybir as _mybir
    from concourse.bass_utils import run_bass_kernel_spmd as _run

    nc = _bacc.Bacc("TRN2", target_bir_lowering=False, num_devices=1)
    arrays, handles = {}, {}
    for name in inputs:
        if name in _UNUSED:
            continue
        a = _np.ascontiguousarray(inputs[name])
        arrays[f"in_{name}"] = a
        handles[name] = nc.dram_tensor(f"in_{name}", a.shape, _mybir.dt.from_np(a.dtype), kind="ExternalInput").ap()
    handles["out"] = nc.dram_tensor("out_x", (N, D), F32, kind="ExternalOutput").ap()
    gnn_kernel(nc, handles)
    r = _run(nc, [arrays], core_ids=[0])
    return r.results[0]["out_x"]
```

```python
from contextlib import ExitStack

import concourse.bass as bass
from concourse import mybir

F32 = mybir.dt.float32
BF16 = mybir.dt.bfloat16
I32 = mybir.dt.int32
U8 = mybir.dt.uint8
ALU = mybir.AluOpType
ACT = mybir.ActivationFunctionType
AX = mybir.AxisListType

P = 128
N = 3125
E = 100000
D = 128
HEADS = 8
CH = D // HEADS
TYPES = 8
NP = 125
NB = N // NP
GROUP = 7
RING = 4
LOOPS = 28
GROUPS = RING * LOOPS
STEPS = GROUP * GROUPS
EPAD = P * STEPS
FULL = E // STEPS
REST = E - FULL * STEPS
LO = 64
HI = -(-(N + 1) // LO)
AW = D + 2 * HEADS
PER_BANK = 4
BLOCKS = [(b, min(b + PER_BANK, NB)) for b in range(0, NB, PER_BANK)]
NBLK = len(BLOCKS)
QBUF = 4
NEG = -1.0e30
SCALE = CH ** -0.5
EPS = 1e-5
SUM, ATT, MAX = "sum", "att", "max"
KINDS = [SUM, SUM, ATT, ATT, ATT, MAX, MAX]
PASSES = len(KINDS)


PHASES = {
    "start": [[], [], ["T_h0"]],
    "sage1": [["T_agg0"], ["lin0"], ["T_h1"]],
    "sage2": [["T_agg1"], ["lin1"], [], [], ["T_in2"], ["qkvs2"]],
    "conv1": [["T_in3"], ["qkvs3"]],
    "conv2": [[], [], ["T_in4"], ["qkv4"]],
    "graph": [["T_att4"], ["wo4"], [], [], ["T_ffn4"]],
    "gelu": [["up4"]],
    "ffn": [["down4"], [], [], []],
    "gin1": [["T_z5"], ["lin5"]],
    "gin2": [["T_z6"], ["lin6"], []],
}


def in_stages(phase):
    n = len(PHASES[phase])
    for slot in range(NBLK + n - 1):
        for stage in reversed(range(n)):
            if 0 <= slot - stage < NBLK:
                yield stage, slot - stage


def job_plan():
    plan, at = {}, 0
    for phase, stages in PHASES.items():
        for stage, b in in_stages(phase):
            for name in stages[stage]:
                n = BLOCKS[b][1] - BLOCKS[b][0] if name.startswith("qkv") else 1
                plan[name, b] = (at, n)
                at += n
    return plan


def gnn_kernel(nc, A):
    JOB = job_plan()
    MARK = {}
    NORM = {}

    def job_end(name, b):
        first, n = JOB[name, b]
        return first + n

    ctx = ExitStack()
    with ctx:
        def sb(name, shape, dt=F32):
            return ctx.enter_context(nc.sbuf_tensor(name, shape, dt))

        def sem(name):
            return ctx.enter_context(nc.semaphore(name))

        def dram(name, shape, dt=F32):
            return nc.dram_tensor(name, shape, dt, kind="Internal").ap()

        table = {k: dram(f"table{k}", [N, 2 * D if KINDS[k] == ATT else D]) for k in range(PASSES)}
        qtable = {k: dram(f"qtable{k}", [N, 2 * D]) for k in range(PASSES) if KINDS[k] == ATT}
        rows = {SUM: dram("rows_plain", [EPAD, D]), ATT: dram("rows_att", [EPAD, AW])}
        rows[MAX] = rows[SUM]
        node_info = dram("node_info", [2, HI * LO])

        arena = sb("arena", [P, RING * GROUP * 3 * D])
        ring = arena[:, 0:RING * GROUP * 2 * D].rearrange("p (s j w) -> p s j w", s=RING, j=GROUP)
        window = arena[:, RING * GROUP * 2 * D:RING * (GROUP + 1) * 2 * D].rearrange("p (s w) -> p s w", s=RING)
        outs = sb("outs", [P, RING * GROUP * AW])
        out_plain = outs[:, 0:RING * GROUP * D].rearrange("p (s j w) -> p s j w", s=RING, j=GROUP)
        out_att = outs[:, :].rearrange("p (s j w) -> p s j w", s=RING, j=GROUP)
        work = sb("work", [P, 7168])
        XR = sb("XR", [P, NB, D])
        H = sb("H", [P, NB, D])
        KEEP = sb("KEEP", [P, NB * D])
        src_i = sb("src_i", [P, STEPS], I32)
        dst_i = sb("dst_i", [P, STEPS], I32)
        same = sb("same", [P, STEPS])
        fence = sb("fence", [P, STEPS])
        bias = sb("bias", [P, STEPS, HEADS])
        W = sb("W", [P, 20, D])
        brow3 = sb("brow3", [3, 17, D], BF16)
        affine = sb("affine", [P, 4, D])
        ebias = sb("ebias", [P, TYPES, HEADS])
        ident = sb("ident", [P, P])
        upper = sb("upper", [HI, HI])
        ones = sb("ones", [1, P])
        ones_bf = sb("ones_bf", [3, P], BF16)
        far_note = sb("far_note", [1, 1])
        lo_iota = sb("lo_iota", [P, LO])
        lo_iota_i = sb("lo_iota_i", [P, LO], I32)
        part_i = sb("part_i", [P, 1], I32)
        head_i = sb("head_i", [P, 1], I32)
        zero_bf = sb("zero_bf", [P, LO], BF16)
        near_late = sb("near_late", [P, RING, GROUP], U8)
        near_idx = sb("near_idx", [P, RING, 2, GROUP], I32)
        hot_lo = sb("hot_lo", [P, 2, GROUP, LO], BF16)
        hot_hi = sb("hot_hi", [P, 2, GROUP, HI], BF16)
        late = sb("late", [P, STEPS], U8)
        slow_i = sb("slow_i", [P, 1], I32)
        before = sb("before", [P, 1], I32)
        small = sb("small", [P, 16])
        whole = sb("whole", [P, P])
        fenceT = sb("fenceT", [P, P])
        carT = sb("carT", [P, 3, P])
        carE = sb("carE", [P, 2, P])
        tails = sb("tails", [P, 3, D])
        contT = sb("contT", [P, P])
        contF = sb("contF", [P, P])
        head = sb("head", [P, AW])
        head_w = sb("head_w", [P, 3, HEADS])
        deg_sb = sb("deg_sb", [HI, LO])
        end_sb = sb("end_sb", [HI, LO])
        hist_tmp = sb("hist_tmp", [HI, LO])
        info = sb("info", [P, 5, NB])
        last_i = sb("last_i", [P, NB], I32)
        bn_st = sb("bn_st", [P, NB, 6])
        mean_var = sb("mean_var", [P, NB, 2])
        var = sb("var", [P, NB])
        root = sb("root", [P, NB])
        rinv = sb("rinv", [P, NB])
        rden = sb("rden", [P, NB, HEADS])
        fences = sb("fences", [P, RING, HEADS, GROUP + 1])
        UA = sb("UA", [P, RING, 2, HEADS, GROUP + 1])
        MS = sb("MS", [P, RING, HEADS, GROUP + 1])
        LS = sb("LS", [P, RING, HEADS, GROUP + 1])
        DE = sb("DE", [P, 2, 2, HEADS, GROUP])
        LD = sb("LD", [P, 2, HEADS, GROUP + 1])
        LA = sb("LA", [P, 2, HEADS, GROUP + 1])

        last_rows = arena[0:NP, 0:NB * AW]
        kvq = arena[0:NP, NB * AW:NB * AW + QBUF * PER_BANK * 3 * D].rearrange(
            "p (s i f) -> p s i f", s=QBUF, f=3 * D)
        T1 = outs[:, 0:NB * D].rearrange("p (i f) -> p i f", f=D)
        aT = work[:, 0:N]
        T2 = work[:, NB * D:2 * NB * D].rearrange("p (i f) -> p i f", f=D)
        KN = KEEP[:, :].rearrange("p (i f) -> p i f", f=D)

        def node_rows(k):
            w = AW if KINDS[k] == ATT else D
            return last_rows[:, 0:NB * w].rearrange("p (i f) -> p i f", f=w)

        brow = arena[0:1, RING * (GROUP + 1) * 2 * D:RING * (GROUP + 1) * 2 * D + 17 * D].rearrange(
            "p (i f) -> p i f", f=D)
        brow_low = work[0:1, 5 * STEPS:5 * STEPS + 17 * D].bitcast(BF16).rearrange("p (a i f) -> p a i f", a=2, f=D)
        GD, GS = GROUP * D, (GROUP + 1) * D
        prod = work[:, 0:GD].rearrange("p (j f) -> p j f", j=GROUP)
        msg = [work[:, GD + b * GS:GD + (b + 1) * GS] for b in range(2)]
        dB = [work[:, GD + (2 + b) * GS:GD + (3 + b) * GS] for b in range(2)]
        OS = [work[:, GD + (4 + b) * GS:GD + (5 + b) * GS] for b in range(2)]
        lohi = work[:, 0:2 * STEPS].rearrange("p (a t) -> p a t", a=2)
        lohi_i = work[:, 2 * STEPS:4 * STEPS].bitcast(I32).rearrange("p (a t) -> p a t", a=2)
        typef = work[:, 4 * STEPS:5 * STEPS]
        type_i = work[:, 6 * STEPS:7 * STEPS].bitcast(I32)
        hot_ty = work[:, 5 * STEPS:5 * STEPS + GROUP * TYPES].rearrange("p (j k) -> p j k", k=TYPES)
        bias_k = work[:, 5 * STEPS + 64:5 * STEPS + 64 + GROUP * TYPES * HEADS].rearrange(
            "p (j h k) -> p j h k", k=TYPES, h=HEADS)

        def by_edge(a):
            return a.rearrange("p (f t) -> p t f", t=GROUP + 1)[:, 1:GROUP + 1, :]

        def column(a, t):
            return a.rearrange("p (f t) -> p f t", t=GROUP + 1)[:, :, t]

        bank = [ctx.enter_context(nc.psum_tensor(f"bank{b}", [P, 512], F32)) for b in range(4)]
        hist_ps = ctx.enter_context(nc.psum_tensor("hist_ps", [P, 512], F32))
        cin_ps = ctx.enter_context(nc.psum_tensor("cin_ps", [P, 512], F32))
        cout_ps = ctx.enter_context(nc.psum_tensor("cout_ps", [P, 512], F32))
        flag_ps = ctx.enter_context(nc.psum_tensor("flag_ps", [P, 512], F32))

        s_x = [sem(f"x_loaded{b}") for b in range(NBLK)]
        s_edges = sem("edges_loaded")
        s_weights = sem("weights_loaded")
        s_parts = sem("bias_parts_laid")
        s_const = sem("constants_made")
        s_zero = sem("constants_cleared")
        s_before = sem("before_loaded")
        s_flagT = sem("flags_transposed")
        s_vec = sem("vec_done")
        s_pe = sem("pe_jobs")
        s_act = sem("act_jobs")
        s_root = sem("roots_taken")
        s_norm = sem("norm_scaled")
        s_table = sem("tables_stored")
        s_idx = sem("indices_staged")
        s_land = [sem(f"rows_landed{s}") for s in range(RING)]
        s_window = [sem(f"windows_landed{s}") for s in range(RING)]
        s_query = sem("edge_queries_landed")
        s_laid = sem("queries_laid")
        s_far = sem("far_groups_summed")
        s_store = [sem(f"rows_stored{s}") for s in range(RING)]
        s_agg = sem("agg_steps")
        s_att = sem("att_steps")
        s_weigh = sem("weights_exped")
        s_rows = sem("att_rows_laid")
        s_hot = sem("hots_made")
        s_hist = sem("hist_groups")
        s_bias = sem("bias_steps")
        s_off = sem("offsets_summed")
        s_info = sem("node_info_stored")
        s_infold = sem("node_info_loaded")
        s_kvq = [sem(f"kvq_stored{i}") for i in range(QBUF)]
        s_cin = sem("carry_turned")
        s_cexp = sem("carry_exps")
        s_cout = sem("carry_turned_back")
        s_head = sem("heads_landed")
        s_hexp = sem("head_exps")
        s_patch = sem("heads_stored")
        s_node = [sem(f"node_rows_landed{b}") for b in range(NBLK)]
        s_out = sem("output_stored")

        width = {SUM: D, MAX: D, ATT: 2 * D}
        idx_per = {SUM: 1, MAX: 1, ATT: 4}
        agg_base, att_base, land_base, weigh_base, idx_base = {}, {}, {}, {}, {}
        A_STEPS = {k: 7 + (k == 4) for k in range(PASSES)}
        B_STEPS = 5
        a = t = l = w = x = 0
        for k in range(PASSES):
            agg_base[k], att_base[k], land_base[k], weigh_base[k] = a, t, l, w
            idx_base[k] = x
            x += idx_per[KINDS[k]] * GROUPS
            l += 16 * GROUP * LOOPS
            if KINDS[k] == ATT:
                t += (A_STEPS[k] + B_STEPS) * GROUPS
                w += 3 * GROUPS
            else:
                a += STEPS
        rows_base = weigh_base

        def store_base(k):
            return 16 * LOOPS * k

        def after_a(k, g, i):
            first = A_STEPS[k] * g + B_STEPS * (g - 1)
            if isinstance(g, int) and g == 0:
                first = 0
            return first + att_base[k] + i

        def after_b(k, g, i):
            na = GROUPS if isinstance(g, int) and g == GROUPS - 1 else g + 2
            return na * A_STEPS[k] + B_STEPS * g + att_base[k] + i

        W_ORDER = ["L0_gnn_W1l", "L0_gnn_W1r", "L0_gnn_W2l", "L0_gnn_W2r",
                   "L1_gnn_k_w0", "L1_gnn_v_w0", "L1_gnn_q_w0", "L1_gnn_s_w0",
                   "L1_gnn_k_w1", "L1_gnn_v_w1", "L1_gnn_q_w1", "L1_gnn_s_w1",
                   "L2_gnn_Wk", "L2_gnn_Wv", "L2_gnn_Wq", "L2_gnn_Wo", "L2_gnn_W1", "L2_gnn_W2",
                   "L3_gnn_W1", "L3_gnn_W2"]
        B_ORDER = ["L0_gnn_b1", "L0_gnn_b2",
                   "L1_gnn_k_b0", "L1_gnn_v_b0", "L1_gnn_q_b0", "L1_gnn_s_b0",
                   "L1_gnn_k_b1", "L1_gnn_v_b1", "L1_gnn_q_b1", "L1_gnn_s_b1",
                   "L2_gnn_bk", "L2_gnn_bv", "L2_gnn_bq", "L2_gnn_bo", "L2_gnn_b2", "L3_gnn_b1", "L3_gnn_b2"]
        AFFINE = ["L2_gnn_g1", "L2_gnn_be1", "L2_gnn_g2", "L2_gnn_be2"]
        wi = {n: i for i, n in enumerate(W_ORDER)}
        bi = {n: i for i, n in enumerate(B_ORDER)}
        colb = sb("colb", [P, 1])
        N_WEIGHTS = len(W_ORDER) + len(B_ORDER) + len(AFFINE) + 2

        def cin_count(k):
            return k + 1

        def att_number(k):
            return [j for j in range(PASSES) if KINDS[j] == ATT].index(k)

        def table_count(k):
            return 16 * NBLK * sum(KINDS[j] != ATT for j in range(k + 1))

        def kvq_stores(b):
            return 3 + (b in (0, NBLK - 1))

        def kvq_count(k, b):
            mine = range(b % QBUF, NBLK, QBUF)
            return 16 * (att_number(k) * sum(kvq_stores(i) for i in mine) + sum(kvq_stores(i) for i in mine if i <= b))

        def node_count(k, b):
            return 16 * (BLOCKS[b][1] - BLOCKS[b][0]) * (k + 1)

        def slot_out(k, s):
            return (out_att if KINDS[k] == ATT else out_plain)[:, s, :, :]

        block = ctx.enter_context(nc.Block())

        @block.vector
        def _(v):
            done = [0]

            def step(ins, mark=None):
                done[0] += 1
                ins.then_inc(s_vec, 1)
                v.wait_ge(s_vec, done[0])
                if mark:
                    MARK[mark] = done[0]

            def ready(semaphore, value):
                if not (isinstance(value, int) and value == 0):
                    v.wait_ge(semaphore, value)

            def tiles(a, b):
                return a[0:NP, BLOCKS[b][0]:BLOCKS[b][1], :]

            def spread(a, b, last=D):
                b0, b1 = BLOCKS[b]
                return a[0:NP, b0:b1].unsqueeze(2).to_broadcast([NP, b1 - b0, last])

            roots = {}

            def moments(name, src, b):
                b0, b1 = BLOCKS[b]
                for i in range(b0, b1):
                    ins = v.bn_stats(bn_st[0:NP, i, :], src[0:NP, i, :])
                step(ins)
                for i in range(b0, b1):
                    ins = v.bn_aggr(mean_var[0:NP, i, :], bn_st[0:NP, i, :])
                step(ins)
                step(v.tensor_scalar(var[0:NP, b0:b1], mean_var[0:NP, b0:b1, 1], EPS, None, ALU.add),
                     f"var_{name}_{b}")
                roots[name, b] = len(roots) + 1

            def rectified(src, dst, b):
                for i in range(*BLOCKS[b]):
                    ins = v.tensor_scalar(dst[0:NP, i, :], src[0:NP, i, :], mean_var[0:NP, i, 0:1], 0.0,
                                          ALU.subtract, ALU.max)
                step(ins)

            def inverse_root(name, b):
                b0, b1 = BLOCKS[b]
                v.wait_ge(s_root, roots[name, b])
                step(v.reciprocal(rinv[0:NP, b0:b1], root[0:NP, b0:b1]), f"rinv_{name}_{b}")

            def mapped(name, src, dst, b, row, mark=None):
                inverse_root(name, b)
                for i in range(*BLOCKS[b]):
                    ins = v.tensor_scalar(dst[0:NP, i, :], src[0:NP, i, :], mean_var[0:NP, i, 0:1],
                                          rinv[0:NP, i:i + 1], ALU.subtract, ALU.mult)
                step(ins)
                d3 = tiles(dst, b)
                wide = list(d3.shape)
                step(v.tensor_tensor(d3, d3, affine[0:NP, row, :].unsqueeze(1).to_broadcast(wide), ALU.mult))
                step(v.tensor_tensor(d3, d3, affine[0:NP, row + 1, :].unsqueeze(1).to_broadcast(wide), ALU.add), mark)

            step(v.memset(src_i[:, :], 0))
            step(v.memset(dst_i[:, :], N))
            step(v.memset(type_i[:, :], 0))
            step(v.memset(before[:, :], -1), "pads")
            for stage, b in in_stages("start"):
                if stage == 0:
                    v.wait_ge(s_x[b], 16)
                    moments("h0", XR, b)
                    rectified(XR, H, b)
                elif stage == 1:
                    inverse_root("h0", b)
            step(v.memset(outs[:, :], 0.0))
            step(v.memset(window, 0.0))
            step(v.memset(carT[:, 1, :], 1.0))
            step(v.memset(MS[:, :, :, :], 0.0))
            step(v.memset(LS[:, :, :, :], 0.0))
            step(v.memset(fences[:, :, :, :], NEG))
            step(v.memset(LD[:, :, :, :], 0.0))
            step(v.memset(ones[:, :], 1.0))
            step(v.memset(ones_bf[:, :], 1.0))
            step(v.memset(zero_bf[:, :], 0.0), "consts")

            v.wait_ge(s_edges, 16 * 6)
            dstf = work[:, 0:STEPS]
            step(v.tensor_copy(dstf, dst_i[:, :]))
            step(v.memset(same[:, 0:1], 0.0))
            step(v.tensor_tensor(same[:, 1:STEPS], dstf[:, 1:STEPS], dstf[:, 0:STEPS - 1], ALU.is_equal))
            step(v.tensor_scalar(fence[:, :], same[:, :], -1.0, -NEG, ALU.add, ALU.mult), "flags")
            v.wait_ge(s_before, 16)
            step(v.tensor_copy(small[:, 0:1], before[:, :]))
            step(v.tensor_tensor(small[:, 1:2], dstf[:, 0:1], small[:, 0:1], ALU.is_equal))
            step(v.tensor_tensor(small[:, 2:3], dstf[:, 0:1], dstf[:, STEPS - 1:STEPS], ALU.is_equal))
            step(v.tensor_tensor(small[:, 3:4], small[:, 1:2], small[:, 2:3], ALU.mult))
            step(v.tensor_copy(tails[:, 1, :], small[:, 1:2].to_broadcast([P, P])))
            step(v.tensor_copy(tails[:, 0, :], small[:, 3:4].to_broadcast([P, P])), "whole")
            step(v.tensor_tensor(typef, dstf, dstf[:, 0:1].to_broadcast([P, STEPS]), ALU.is_equal))
            step(v.tensor_reduce(small[:, 7:8], typef, AX.X, ALU.add))
            v.wait_ge(s_const, 2)
            step(v.tensor_copy(small[:, 8:9], part_i[:, :]))
            step(v.tensor_tensor(head_i[:, :], small[:, 7:8], small[:, 8:9], ALU.add), "heads")
            step(v.tensor_single_scalar(lohi_i[:, 0, :], dst_i[:, :], LO - 1, ALU.bitwise_and))
            step(v.tensor_single_scalar(lohi_i[:, 1, :], dst_i[:, :], LO.bit_length() - 1, ALU.arith_shift_right))
            step(v.tensor_scalar(dst_i[:, :], dst_i[:, :], float(N - 1), None, ALU.min))
            step(v.tensor_copy(dstf, dst_i[:, :]))
            by_group = dstf.rearrange("p (g j) -> p g j", j=GROUP)
            ahead = work[:, 5 * STEPS:6 * STEPS].rearrange("p (g j) -> p g j", j=GROUP)
            step(v.tensor_tensor(ahead, by_group, by_group[:, :, 0:1].to_broadcast([P, GROUPS, GROUP]),
                                 ALU.subtract))
            step(v.tensor_reduce(small[:, 5:6], ahead, AX.XY, ALU.max))
            step(v.tensor_scalar(small[:, 5:6], small[:, 5:6], 1.0, None, ALU.is_gt), "far")
            v.wait_ge(s_far, 1)
            step(v.tensor_scalar(slow_i[:, :], flag_ps[:, 300:301], 0.0, None, ALU.is_gt))
            step(v.tensor_scalar(small[:, 6:7], flag_ps[:, 300:301], 0.0, None, ALU.is_equal))
            step(v.tensor_scalar(late[:, :], work[:, 5 * STEPS:6 * STEPS], 0.0, small[:, 6:7], ALU.is_gt, ALU.mult),
                 "windows")
            step(v.tensor_copy(lohi[:, :, :], lohi_i[:, :, :]))
            step(v.tensor_copy(typef, type_i[:, :]))
            step(v.tensor_copy(lo_iota[:, :], lo_iota_i[:, :]))
            v.wait_ge(s_flagT, 1)
            step(v.tensor_copy(whole[:, :], flag_ps[:, 0:P]))
            step(v.tensor_copy(contT[:, :], flag_ps[:, P:2 * P]))
            step(v.tensor_scalar(contF[:, :], contT[:, :], -1.0, -NEG, ALU.add, ALU.mult))
            step(v.tensor_scalar(fenceT[:, :], whole[:, :], -1.0, -NEG, ALU.add, ALU.mult), "whole_T")

            def plain_group(k, it, s):
                g = it * RING + s
                v.wait_ge(s_land[s], (it + 1) * (16 * GROUP) + land_base[k])
                ready(s_store[s], it * 16 + store_base(k))
                if k == 0:
                    hots(it, s)
                if k == 1:
                    edge_bias(it, s)
                first = it * (RING * GROUP) + s * GROUP
                flags = same if KINDS[k] == SUM else fence
                ops = (ALU.mult, ALU.add) if KINDS[k] == SUM else (ALU.add, ALU.max)
                for j in range(GROUP):
                    prev = out_plain[:, s, j - 1, :] if j else out_plain[:, (s - 1) % RING, GROUP - 1, :]
                    ready(s_agg, first + (agg_base[k] + j))
                    v.scalar_tensor_tensor(out_plain[:, s, j, :], prev, flags[:, bass.ds(first + j, 1)],
                                           ring_plain(s, j), *ops).then_inc(s_agg, 1)

            def ring_plain(s, j):
                return ring[:, s, j, 0:D]

            def hots(it, s):
                b = s % 2
                first = it * (RING * GROUP) + s * GROUP
                ready(s_hist, it * RING + s)
                v.tensor_tensor(hot_lo[:, b, :, :],
                                lohi[:, 0, bass.ds(first, GROUP)].unsqueeze(2).to_broadcast([P, GROUP, LO]),
                                lo_iota[:, :].unsqueeze(1).to_broadcast([P, GROUP, LO]),
                                ALU.is_equal).then_inc(s_hot, 1)
                v.tensor_tensor(hot_hi[:, b, :, :],
                                lohi[:, 1, bass.ds(first, GROUP)].unsqueeze(2).to_broadcast([P, GROUP, HI]),
                                lo_iota[:, 0:HI].unsqueeze(1).to_broadcast([P, GROUP, HI]),
                                ALU.is_equal).then_inc(s_hot, 1)

            def edge_bias(it, s):
                first = it * (RING * GROUP) + s * GROUP
                g3 = (it * RING + s) * 3
                ready(s_bias, g3)
                v.tensor_tensor(hot_ty[:, :, :],
                                typef[:, bass.ds(first, GROUP)].unsqueeze(2).to_broadcast([P, GROUP, TYPES]),
                                lo_iota[:, 0:TYPES].unsqueeze(1).to_broadcast([P, GROUP, TYPES]),
                                ALU.is_equal).then_inc(s_bias, 1)
                v.wait_ge(s_bias, g3 + 1)
                v.tensor_tensor(bias_k,
                                hot_ty.unsqueeze(2).to_broadcast([P, GROUP, HEADS, TYPES]),
                                ebias[:, :, :].rearrange("p k h -> p h k").unsqueeze(1).to_broadcast(
                                    [P, GROUP, HEADS, TYPES]), ALU.mult).then_inc(s_bias, 1)
                v.wait_ge(s_bias, g3 + 2)
                v.tensor_reduce(bias[:, bass.ds(first, GROUP), :], bias_k, AX.X, ALU.add).then_inc(s_bias, 1)

            def part_a(k, it, s, g):
                b = s % 2
                n = 0

                def chain(ins):
                    nonlocal n
                    n += 1
                    ins.then_inc(s_att, 1)
                    v.wait_ge(s_att, after_a(k, g, n))

                first = it * (RING * GROUP) + s * GROUP
                wide = [P, GROUP, D]
                v.wait_ge(s_laid, g + (att_number(k) * GROUPS + 1))
                n += 1
                v.tensor_copy(UA[:, s, 1, :, 0], MS[:, (s - 1) % RING, :, GROUP]).then_inc(s_att, 1)
                chain(v.copy_predicated(prod, near_late[:, s, :].unsqueeze(2).to_broadcast(wide),
                                        window[:, s, D:2 * D].unsqueeze(1).to_broadcast(wide)))
                v.wait_ge(s_land[s], (it + 1) * (16 * GROUP) + land_base[k])
                chain(v.tensor_tensor(prod, prod, ring[:, s, :, 0:D], ALU.mult))
                scores = UA[:, s, 1, :, 1:GROUP + 1].rearrange("p h j -> p j h")
                chain(v.tensor_reduce(scores, prod.rearrange("p j (h c) -> p j h c", c=CH), AX.X, ALU.add))
                if k == 4:
                    chain(v.tensor_tensor(scores, scores, bias[:, bass.ds(first, GROUP), :], ALU.add))
                v.wait_ge(s_idx, g * 4 + (idx_base[k] + 4))
                chain(v.tensor_tensor_scan(flat(MS[:, s, :, :]), flat(fences[:, s, :, :]),
                                           flat(UA[:, s, 1, :, :]), 0.0, ALU.add, ALU.max))
                chain(v.tensor_tensor(UA[:, s, 0, :, 1:GROUP + 1], MS[:, s, :, 0:GROUP],
                                      fences[:, s, :, 1:GROUP + 1], ALU.add))
                chain(v.tensor_tensor(DE[:, b, :, :, :], UA[:, s, :, :, 1:GROUP + 1],
                                      MS[:, s, :, 1:GROUP + 1].unsqueeze(1).to_broadcast([P, 2, HEADS, GROUP]),
                                      ALU.subtract))
                assert n == A_STEPS[k]

            def flat(a):
                return a.rearrange("p h t -> p (h t)")

            def part_b(k, it, s, g):
                b = s % 2
                n = 0

                def chain(ins):
                    nonlocal n
                    n += 1
                    ins.then_inc(s_att, 1)
                    v.wait_ge(s_att, after_b(k, g, n))

                v.wait_ge(s_weigh, g * 3 + (weigh_base[k] + 3))
                chain(v.tensor_copy(LA[:, b, :, 0], LS[:, (s - 1) % RING, :, GROUP]))
                chain(v.tensor_tensor_scan(flat(LS[:, s, :, :]), flat(LD[:, b, :, :]), flat(LA[:, b, :, :]),
                                           0.0, ALU.mult, ALU.add))
                vals = ring[:, s, :, D:2 * D].rearrange("p j (h c) -> p j h c", c=CH)
                wts = LA[:, b, :, 1:GROUP + 1].rearrange("p h j -> p j h").unsqueeze(3).to_broadcast(
                    [P, GROUP, HEADS, CH])
                chain(v.tensor_tensor(by_edge(msg[b]).rearrange("p j (h c) -> p j h c", c=CH), vals, wts,
                                      ALU.mult))
                chain(v.tensor_copy(column(msg[b], 0), column(OS[1 - b], GROUP)))
                if not (isinstance(g, int) and g < 2):
                    v.wait_ge(s_rows, g * 3 + (rows_base[k] - 3))
                chain(v.tensor_tensor_scan(OS[b], dB[b], msg[b], 0.0, ALU.mult, ALU.add))
                assert n == B_STEPS

            def carry_scan(k):
                v.wait_ge(s_cin, cin_count(k))
                turned = cin_ps[:, 0:3 * P].rearrange("p (a q) -> p a q", a=3)
                if KINDS[k] == SUM:
                    step(v.tensor_tensor_scan(carT[:, 0, :], whole[:, :], turned[:, 0, :], 0.0, ALU.mult, ALU.add))
                elif KINDS[k] == MAX:
                    step(v.tensor_tensor_scan(carT[:, 0, :], fenceT[:, :], turned[:, 0, :], NEG, ALU.add, ALU.max))
                else:
                    m = carT[:, 1, :]
                    step(v.tensor_tensor_scan(m, fenceT[:, :], turned[:, 1, :], 0.0, ALU.add, ALU.max))
                    step(v.tensor_copy(carE[:, 0, 0:1], fenceT[:, 0:1]))
                    step(v.tensor_tensor(carE[:, 0, 1:P], m[:, 0:P - 1], fenceT[:, 1:P], ALU.add))
                    step(v.tensor_tensor(carE[:, 0, :], carE[:, 0, :], m, ALU.subtract))
                    step(v.tensor_tensor(carE[:, 1, :], turned[:, 1, :], m, ALU.subtract), f"carry_in{k}")
                    v.wait_ge(s_cexp, att_number(k) + 1)
                    for i in (0, 2):
                        step(v.tensor_tensor(carT[:, i, :], turned[:, i, :], carE[:, 1, :], ALU.mult))
                        step(v.tensor_tensor_scan(carT[:, i, :], carE[:, 0, :], carT[:, i, :], 0.0,
                                                  ALU.mult, ALU.add))
                for i in (0, 1, 2) if KINDS[k] == ATT else (0,):
                    by_max = KINDS[k] == MAX or i == 1
                    step(v.memset(tails[:, i, 0:1], NEG if by_max else 0.0))
                    step(v.tensor_tensor(tails[:, i, 1:P], carT[:, i, 0:P - 1], (contF if by_max else contT)[:, 1:P],
                                         ALU.add if by_max else ALU.mult), f"carry{k}")

            def join_heads(k):
                v.wait_ge(s_cout, k + 1)
                if KINDS[k] != ATT:
                    v.wait_ge(s_head, 16 * (k + 1))
                    step(v.tensor_tensor(head[:, 0:D], head[:, 0:D], cout_ps[:, 0:D],
                                         ALU.add if KINDS[k] == SUM else ALU.max), f"head{k}")
                    return
                before_o, before_m, before_l = (cout_ps[:, i * P:(i + 1) * P].rearrange("p (h c) -> p h c", c=CH)
                                                for i in range(3))
                mx, dn = head[:, D:D + HEADS], head[:, D + HEADS:AW]
                wide = [P, HEADS, CH]
                step(v.tensor_copy(head_w[:, 2, :], before_m[:, :, 0]))
                v.wait_ge(s_head, 16 * (k + 1))
                step(v.tensor_tensor(head_w[:, 0, :], mx, head_w[:, 2, :], ALU.max))
                step(v.tensor_tensor(head_w[:, 1, :], mx, head_w[:, 0, :], ALU.subtract))
                step(v.tensor_tensor(head_w[:, 2, :], head_w[:, 2, :], head_w[:, 0, :], ALU.subtract), f"head_in{k}")
                v.wait_ge(s_hexp, att_number(k) + 1)
                old, new = head_w[:, 2, :], head_w[:, 1, :]
                vals = head[:, 0:D].rearrange("p (h c) -> p h c", c=CH)
                more = tails[:, 0, :].rearrange("p (h c) -> p h c", c=CH)
                step(v.tensor_tensor(vals, vals, new.unsqueeze(2).to_broadcast(wide), ALU.mult))
                step(v.tensor_tensor(more, before_o, old.unsqueeze(2).to_broadcast(wide), ALU.mult))
                step(v.tensor_tensor(vals, vals, more, ALU.add))
                step(v.tensor_tensor(dn, dn, new, ALU.mult))
                step(v.tensor_tensor(old, old, before_l[:, :, 0], ALU.mult))
                step(v.tensor_tensor(dn, dn, old, ALU.add))
                step(v.tensor_copy(mx, head_w[:, 0, :]), f"head{k}")

            def prepare_weights():
                v.wait_ge(s_weights, 16 * N_WEIGHTS)
                for name in ("L1_gnn_q_w0", "L1_gnn_q_w1", "L2_gnn_Wq"):
                    step(v.tensor_scalar(W[:, wi[name], :], W[:, wi[name], :], SCALE, None, ALU.mult))
                for name in ("L1_gnn_q_b0", "L1_gnn_q_b1", "L2_gnn_bq"):
                    step(v.tensor_scalar(brow[:, bi[name], :], brow[:, bi[name], :], SCALE, None, ALU.mult))
                parts = brow3[0:1, :, :], brow_low[:, 0, :, :], brow_low[:, 1, :, :]
                for i, part in enumerate(parts):
                    step(v.tensor_copy(part, brow), "biases")
                    if i < 2:
                        step(v.tensor_tensor(brow, brow, part, ALU.subtract))

            def run_pass(k):
                if KINDS[k] != ATT:
                    for s in range(RING):
                        plain_group(k, 0, s)
                    if k == 0:
                        prepare_weights()
                    with v.Fori(1, LOOPS) as it:
                        for s in range(RING):
                            plain_group(k, it, s)
                    v.wait_ge(s_agg, agg_base[k] + STEPS)
                else:
                    part_a(k, 0, 0, 0)
                    for s in range(RING):
                        att_group(k, 0, s)
                    with v.Fori(1, LOOPS - 1) as it:
                        for s in range(RING):
                            att_group(k, it, s)
                    for s in range(RING):
                        att_group(k, LOOPS - 1, s)
                    b = (RING - 1) % 2
                    step(v.tensor_copy(tails[:, 0, :], column(OS[b], GROUP)))
                    for i, a in ((1, MS), (2, LS)):
                        step(v.tensor_copy(tails[:, i, :].rearrange("p (h c) -> p h c", c=CH),
                                           a[:, RING - 1, :, GROUP].unsqueeze(2).to_broadcast([P, HEADS, CH])),
                             f"tails{k}")

            def att_group(k, it, s):
                g = it * RING + s
                if not (isinstance(it, int) and g == GROUPS - 1):
                    s1 = (s + 1) % RING
                    part_a(k, it + (1 if s == RING - 1 else 0), s1, g + 1)
                part_b(k, it, s, g)

            def degrees():
                v.wait_ge(s_hist, GROUPS + 2)
                step(v.tensor_copy(deg_sb[:, :], hist_ps[0:HI, 0:LO]))
                step(v.memset(hist_tmp[:, :], 1.0))
                step(v.tensor_tensor_scan(end_sb[:, :], hist_tmp[:, :], deg_sb[:, :], 0.0, ALU.mult, ALU.add),
                     "row_totals")
                v.wait_ge(s_off, 1)
                step(v.tensor_copy(small[0:HI, 4:5], flag_ps[0:HI, 256:257]))
                step(v.tensor_scalar(end_sb[:, :], end_sb[:, :], small[0:HI, 4:5], None, ALU.add), "info")

            deg, end, has, per_degree, tmp_n = (info[0:NP, i, :] for i in range(5))

            def node_tables():
                v.wait_ge(s_infold, 32)
                step(v.tensor_scalar(end, end, -1.0, 0.0, ALU.add, ALU.max))
                step(v.tensor_copy(last_i[0:NP, :], end), "last")
                step(v.tensor_scalar(has, deg, 1.0, None, ALU.min))
                step(v.tensor_scalar(tmp_n, deg, 1.0, None, ALU.max))
                step(v.reciprocal(tmp_n, tmp_n))
                step(v.tensor_tensor(per_degree, tmp_n, has, ALU.mult))

            def joined(k, b, name):
                v.wait_ge(s_node[b], node_count(k, b))
                rows3 = tiles(node_rows(k), b)
                weight = per_degree if KINDS[k] == SUM else has
                step(v.tensor_tensor(rows3, rows3, spread(weight, b), ALU.mult),
                     f"{name}_{b}" if KINDS[k] == SUM else None)
                if KINDS[k] == MAX:
                    step(v.tensor_tensor(rows3, rows3, tiles(H, b), ALU.add), f"{name}_{b}")

            def attended(k, b, mark=None):
                b0, b1 = BLOCKS[b]
                v.wait_ge(s_node[b], node_count(k, b))
                rows3 = tiles(node_rows(k), b)
                r3 = rden[0:NP, b0:b1, :]
                dens = rows3[:, :, D + HEADS:AW]
                if k == 4:
                    step(v.tensor_scalar(dens, dens, 1e-16, None, ALU.add))
                step(v.reciprocal(r3, dens))
                step(v.tensor_tensor(r3, r3, spread(has, b, HEADS), ALU.mult))
                vals = rows3[:, :, 0:D].rearrange("p i (h c) -> p i h c", c=CH)
                step(v.tensor_tensor(vals, vals, r3.unsqueeze(3).to_broadcast([NP, b1 - b0, HEADS, CH]), ALU.mult),
                     mark)

            def plus(dst, a, b, mark=None):
                step(v.tensor_tensor(dst, dst, a, ALU.add), mark)

            run_pass(0)
            degrees()
            carry_scan(0)
            join_heads(0)
            node_tables()
            for stage, b in in_stages("sage1"):
                if stage == 0:
                    joined(0, b, "agg0")

            run_pass(1)
            carry_scan(1)
            join_heads(1)
            for stage, b in in_stages("sage2"):
                if stage == 0:
                    joined(1, b, "agg1")
                elif stage == 2:
                    v.wait_ge(s_act, job_end("lin1", b))
                    plus(tiles(XR, b), tiles(T2, b), b)
                    moments("in2", XR, b)
                    rectified(XR, H, b)
                elif stage == 3:
                    inverse_root("in2", b)

            def clear_carries(k, name):
                v.wait_ge(s_act, job_end(name, NBLK - 1))
                step(v.memset(work[:, GD:GD + 6 * GS], 0.0), f"cleared{k}")

            clear_carries(2, "qkvs2")
            run_pass(2)
            carry_scan(2)
            join_heads(2)
            for stage, b in in_stages("conv1"):
                if stage == 0:
                    attended(2, b)
                    plus(tiles(node_rows(2), b)[:, :, 0:D], tiles(KN, b), b, f"in3_{b}")

            clear_carries(3, "qkvs3")
            run_pass(3)
            carry_scan(3)
            join_heads(3)
            for stage, b in in_stages("conv2"):
                if stage == 0:
                    attended(3, b)
                    plus(tiles(XR, b), tiles(KN, b), b)
                    plus(tiles(XR, b), tiles(node_rows(3), b)[:, :, 0:D], b)
                    moments("in4", XR, b)
                    rectified(XR, H, b)
                elif stage == 1:
                    inverse_root("in4", b)

            clear_carries(4, "qkv4")
            run_pass(4)
            carry_scan(4)
            join_heads(4)
            for stage, b in in_stages("graph"):
                if stage == 0:
                    attended(4, b, f"att4_{b}")
                elif stage == 2:
                    v.wait_ge(s_act, job_end("wo4", b))
                    plus(tiles(T1, b), tiles(H, b), b)
                    moments("ffn4", T1, b)
                elif stage == 3:
                    mapped("ffn4", T1, T2, b, 0, f"ffn4_{b}")
            for stage, b in in_stages("ffn"):
                if stage == 1:
                    v.wait_ge(s_act, job_end("down4", b))
                    plus(tiles(T1, b), tiles(T2, b), b)
                    moments("out4", T1, b)
                elif stage == 2:
                    mapped("out4", T1, T2, b, 2)
                    plus(tiles(XR, b), tiles(T2, b), b)
                    moments("h5", XR, b)
                    rectified(XR, H, b)
                elif stage == 3:
                    inverse_root("h5", b)

            run_pass(5)
            carry_scan(5)
            join_heads(5)
            for stage, b in in_stages("gin1"):
                if stage == 0:
                    joined(5, b, "z5")
            run_pass(6)
            carry_scan(6)
            join_heads(6)
            for stage, b in in_stages("gin2"):
                if stage == 0:
                    joined(6, b, "z6")
                elif stage == 2:
                    v.wait_ge(s_act, job_end("lin6", b))
                    plus(tiles(XR, b), tiles(T2, b), b, f"result_{b}")

        @block.scalar
        def _(act):
            scaled = [0]

            def turned(name, b, dst, func=ACT.Copy, **more):
                b0, b1 = BLOCKS[b]
                j = JOB[name, b][0]
                act.wait_ge(s_pe, j + 1)
                act.activation(dst[:, b0 * NP:b1 * NP], bank[j % 4][:, 0:(b1 - b0) * NP], func, **more)\
                    .then_inc(s_act, 1)

            def laid(name, b, dst, func=ACT.Copy):
                b0, b1 = BLOCKS[b]
                j = JOB[name, b][0]
                act.wait_ge(s_pe, j + 1)
                act.activation(dst[0:NP, b0:b1, :],
                               bank[j % 4][0:NP, 0:(b1 - b0) * D].rearrange("p (i f) -> p i f", f=D), func)\
                    .then_inc(s_act, 1)

            def projected(k, name, b, n_w):
                b0, b1 = BLOCKS[b]
                used = kvq_count(k, b) - 16 * kvq_stores(b)
                if used:
                    act.wait_ge(s_kvq[b % QBUF], used)
                for i in range(b0, b1):
                    j = JOB[name, b][0] + i - b0
                    ps = bank[j % 4][0:NP, :]
                    act.wait_ge(s_pe, j + 1)
                    if n_w == 4:
                        act.activation(KN[0:NP, i, :], ps[:, 3 * D:4 * D], ACT.Copy)
                    act.activation(kvq[:, b % QBUF, i - b0, :], ps[:, 0:3 * D], ACT.Copy).then_inc(s_act, 1)

            def take_root(name, b):
                b0, b1 = BLOCKS[b]
                act.wait_ge(s_vec, MARK[f"var_{name}_{b}"])
                act.activation(root[0:NP, b0:b1], var[0:NP, b0:b1], ACT.Sqrt).then_inc(s_root, 1)

            def scale_rows(name, b):
                act.wait_ge(s_vec, MARK[f"rinv_{name}_{b}"])
                for i in range(*BLOCKS[b]):
                    ins = act.activation(H[0:NP, i, :], H[0:NP, i, :], ACT.Copy, scale=rinv[0:NP, i:i + 1])
                ins.then_inc(s_norm, 1)
                scaled[0] += 1
                NORM[name, b] = scaled[0]

            def stage_group(k, it, s, far=False):
                first = it * (RING * GROUP) + s * GROUP
                act.copy(near_idx[:, s, 0, :], src_i[:, bass.ds(first, GROUP)]).then_inc(s_idx, 1)
                if KINDS[k] == ATT:
                    act.copy(near_late[:, s, :], late[:, bass.ds(first, GROUP)]).then_inc(s_idx, 1)
                    act.activation(near_idx[:, s, 1, :], dst_i[:, bass.ds(first, GROUP)], ACT.Copy,
                                   scale=2.0 if far else 1.0).then_inc(s_idx, 1)
                    act.copy(fences[:, s, :, 1:GROUP + 1],
                             fence[:, bass.ds(first, GROUP)].unsqueeze(1).to_broadcast([P, HEADS, GROUP]))\
                        .then_inc(s_idx, 1)

            def weigh(k, s, g):
                b = s % 2
                act.wait_ge(s_att, after_a(k, g, A_STEPS[k]))
                act.activation(LD[:, b, :, 1:GROUP + 1], DE[:, b, 0, :, :], ACT.Exp).then_inc(s_weigh, 1)
                act.activation(LA[:, b, :, 1:GROUP + 1], DE[:, b, 1, :, :], ACT.Exp).then_inc(s_weigh, 1)
                act.activation(dB[b].rearrange("p (h c t) -> p h c t", h=HEADS, c=CH)[:, :, :, 1:GROUP + 1],
                               DE[:, b, 0, :, :].unsqueeze(2).to_broadcast([P, HEADS, CH, GROUP]), ACT.Exp)\
                    .then_inc(s_weigh, 1)

            def lay_rows(k, it, s, g):
                act.wait_ge(s_att, after_b(k, g, B_STEPS))
                act.wait_ge(s_store[s], it * 16 + store_base(k))
                act.copy(out_att[:, s, :, 0:D], by_edge(OS[s % 2])).then_inc(s_rows, 1)
                act.copy(out_att[:, s, :, D:D + HEADS],
                         MS[:, s, :, 1:GROUP + 1].rearrange("p h j -> p j h")).then_inc(s_rows, 1)
                act.copy(out_att[:, s, :, D + HEADS:AW],
                         LS[:, s, :, 1:GROUP + 1].rearrange("p h j -> p j h")).then_inc(s_rows, 1)

            def lay_queries(k, it, s, g, far):
                done = g + (att_number(k) * GROUPS + 1)
                if far:
                    act.wait_ge(s_query, done * (16 * GROUP))
                    act.copy(far_note[:, :], ones[0:1, 0:1]).then_inc(s_laid, 1)
                else:
                    act.wait_ge(s_window[s], it * 16 + (att_number(k) * LOOPS + 1) * 16)
                    act.copy(prod, window[:, s, 0:D].unsqueeze(1).to_broadcast([P, GROUP, D])).then_inc(s_laid, 1)

            def att_pass(k, far):
                for s in range(RING):
                    stage_group(k, 0, s, far)
                lay_queries(k, 0, 0, 0, far)
                weigh(k, 0, 0)
                lay_queries(k, 0, 1, 1, far)
                with act.Fori(0, LOOPS - 1) as it:
                    for s in range(RING):
                        g = it * RING + s
                        weigh(k, (s + 1) % RING, g + 1)
                        lay_queries(k, it + (s + 2) // RING, (s + 2) % RING, g + 2, far)
                        lay_rows(k, it, s, g)
                        stage_group(k, it + 1, s, far)
                for s in range(RING):
                    g = (LOOPS - 1) * RING + s
                    if s + 1 < RING:
                        weigh(k, s + 1, g + 1)
                    if s + 2 < RING:
                        lay_queries(k, LOOPS - 1, s + 2, g + 2, far)
                    lay_rows(k, LOOPS - 1, s, g)

            def run_pass(k):
                if KINDS[k] == ATT:
                    with act.If(slow > 0):
                        att_pass(k, True)
                    with act.Else():
                        att_pass(k, False)
                    return
                for s in range(RING):
                    stage_group(k, 0, s)
                with act.Fori(0, LOOPS - 1) as it:
                    for s in range(RING):
                        act.wait_ge(s_agg, it * (RING * GROUP) + (agg_base[k] + (s + 1) * GROUP))
                        stage_group(k, it + 1, s)

            def carry_exps(k):
                act.wait_ge(s_vec, MARK[f"carry_in{k}"])
                act.activation(carE[:, :, :], carE[:, :, :], ACT.Exp).then_inc(s_cexp, 1)
                act.wait_ge(s_vec, MARK[f"head_in{k}"])
                act.activation(head_w[:, 1:3, :], head_w[:, 1:3, :], ACT.Exp).then_inc(s_hexp, 1)

            for stage, b in in_stages("start"):
                if stage == 0:
                    take_root("h0", b)
                elif stage == 1:
                    scale_rows("h0", b)
                else:
                    turned("T_h0", b, KEEP)
            act.wait_ge(s_edges, 16 * 6)
            run_pass(0)
            for stage, b in in_stages("sage1"):
                if stage == 0:
                    turned("T_agg0", b, aT)
                elif stage == 1:
                    laid("lin0", b, H, ACT.Relu)
                else:
                    turned("T_h1", b, KEEP)
            run_pass(1)
            for stage, b in in_stages("sage2"):
                if stage == 0:
                    turned("T_agg1", b, aT)
                elif stage == 1:
                    laid("lin1", b, T2, ACT.Relu)
                elif stage == 2:
                    take_root("in2", b)
                elif stage == 3:
                    scale_rows("in2", b)
                elif stage == 4:
                    turned("T_in2", b, aT)
                else:
                    projected(2, "qkvs2", b, 4)
            act.wait_ge(s_vec, MARK["windows"])
            slow = act.value_load(slow_i[0:1, 0:1], min_val=0, max_val=1)
            run_pass(2)
            carry_exps(2)
            for stage, b in in_stages("conv1"):
                if stage == 0:
                    turned("T_in3", b, aT, ACT.Relu)
                else:
                    projected(3, "qkvs3", b, 4)
            run_pass(3)
            carry_exps(3)
            for stage, b in in_stages("conv2"):
                if stage == 0:
                    take_root("in4", b)
                elif stage == 1:
                    scale_rows("in4", b)
                elif stage == 2:
                    turned("T_in4", b, aT)
                else:
                    projected(4, "qkv4", b, 3)
            run_pass(4)
            carry_exps(4)
            for stage, b in in_stages("graph"):
                if stage == 0:
                    turned("T_att4", b, aT)
                elif stage == 1:
                    laid("wo4", b, T1)
                elif stage == 2:
                    take_root("ffn4", b)
                elif stage == 4:
                    turned("T_ffn4", b, KEEP)
            for stage, b in in_stages("gelu"):
                turned("up4", b, aT, ACT.Gelu, bias=colb[:, 0:1])
            for stage, b in in_stages("ffn"):
                if stage == 0:
                    laid("down4", b, T1)
                elif stage == 1:
                    take_root("out4", b)
                elif stage == 2:
                    take_root("h5", b)
                else:
                    scale_rows("h5", b)
            run_pass(5)
            for stage, b in in_stages("gin1"):
                if stage == 0:
                    turned("T_z5", b, aT)
                else:
                    laid("lin5", b, H, ACT.Relu)
            run_pass(6)
            for stage, b in in_stages("gin2"):
                if stage == 0:
                    turned("T_z6", b, aT)
                elif stage == 1:
                    laid("lin6", b, T2)

        @block.tensor
        def _(pe):
            def open_bank(j):
                if j >= 4:
                    pe.wait_ge(s_act, j - 3)
                return bank[j % 4]

            def turn(name, b, src):
                b0, b1 = BLOCKS[b]
                ps = open_bank(JOB[name, b][0])
                for i in range(b0, b1):
                    ins = pe.transpose(ps[:, (i - b0) * NP:(i - b0 + 1) * NP], src[0:NP, i, 0:D], ident[0:NP, 0:NP])
                ins.then_inc(s_pe, 1)

            def linear(name, b, terms, b_at, xt_name):
                b0, b1 = BLOCKS[b]
                ps = open_bank(JOB[name, b][0])
                pe.wait_ge(s_act, job_end(xt_name, b))
                for i in range(b0, b1):
                    acc = ps[0:NP, (i - b0) * D:(i - b0 + 1) * D]
                    for m, (xt, w_at) in enumerate(terms):
                        pe.matmul(acc, xt[:, i * NP:(i + 1) * NP], W[:, w_at, :], start=(m == 0), stop=False)
                    ins = pe.matmul(acc, ones_bf[:, 0:NP], brow3[:, b_at, :], start=False, stop=True)
                ins.then_inc(s_pe, 1)

            def project(name, b, w_at, n_w, b_at, xt_name):
                b0, b1 = BLOCKS[b]
                pe.wait_ge(s_act, job_end(xt_name, b))
                for i in range(b0, b1):
                    ps = open_bank(JOB[name, b][0] + i - b0)
                    acc = ps[0:NP, 0:n_w * D]
                    pe.matmul(acc, aT[:, i * NP:(i + 1) * NP], W[:, w_at:w_at + n_w, :], start=True, stop=False)
                    pe.matmul(acc, ones_bf[:, 0:NP], brow3[:, b_at:b_at + n_w, :], start=False, stop=True)\
                        .then_inc(s_pe, 1)

            def carry_turns(k):
                n = 3 if KINDS[k] == ATT else 1
                if KINDS[k] == ATT:
                    pe.wait_ge(s_vec, MARK[f"tails{k}"])
                else:
                    pe.wait_ge(s_agg, agg_base[k] + STEPS)
                for i in range(n):
                    src = tails[:, i, :] if KINDS[k] == ATT else out_plain[:, RING - 1, GROUP - 1, :]
                    ins = pe.transpose(cin_ps[:, i * P:(i + 1) * P], src, ident[:, :])
                ins.then_inc(s_cin, 1)
                pe.wait_ge(s_vec, MARK[f"carry{k}"])
                for i in range(n):
                    ins = pe.transpose(cout_ps[:, i * P:(i + 1) * P], tails[:, i, :], ident[:, :])
                ins.then_inc(s_cout, 1)

            pe.wait_ge(s_const, 4)
            for stage, b in in_stages("start"):
                if stage == 2:
                    pe.wait_ge(s_norm, NORM["h0", b])
                    turn("T_h0", b, H)
            pe.wait_ge(s_vec, MARK["whole"])
            pe.matmul(flag_ps[:, P:2 * P], tails[:, 1, :], ident[:, :], start=True, stop=True)
            pe.matmul(flag_ps[:, 0:P], tails[:, 0, :], ident[:, :], start=True, stop=True).then_inc(s_flagT, 1)
            pe.wait_ge(s_vec, MARK["far"])
            pe.matmul(flag_ps[:, 300:301], carT[:, 1, :], small[:, 5:6], start=True, stop=True).then_inc(s_far, 1)
            pe.matmul(hist_ps[0:HI, 0:LO], zero_bf[:, 0:HI], zero_bf[:, :], start=True, stop=False,
                      skip_group_check=True).then_inc(s_hist, 1)
            with pe.Fori(0, LOOPS) as it:
                for s in range(RING):
                    pe.wait_ge(s_hot, (it * RING + (s + 1)) * 2)
                    for j in range(GROUP):
                        ins = pe.matmul(hist_ps[0:HI, 0:LO], hot_hi[:, s % 2, j, :], hot_lo[:, s % 2, j, :],
                                        start=False, stop=False, skip_group_check=True)
                    ins.then_inc(s_hist, 1)
            pe.matmul(hist_ps[0:HI, 0:LO], zero_bf[:, 0:HI], zero_bf[:, :], start=False, stop=True,
                      skip_group_check=True).then_inc(s_hist, 1)
            pe.wait_ge(s_vec, MARK["row_totals"])
            pe.matmul(flag_ps[0:HI, 256:257], upper[:, :], end_sb[:, LO - 1:LO], start=True, stop=True)\
                .then_inc(s_off, 1)
            carry_turns(0)
            pe.wait_ge(s_vec, MARK["biases"])
            pe.wait_ge(s_parts, 32)
            for stage, b in in_stages("sage1"):
                if stage == 0:
                    pe.wait_ge(s_vec, MARK[f"agg0_{b}"])
                    turn("T_agg0", b, node_rows(0))
                elif stage == 1:
                    linear("lin0", b, [(aT, wi["L0_gnn_W1l"]), (KEEP, wi["L0_gnn_W1r"])], bi["L0_gnn_b1"], "T_agg0")
                else:
                    pe.wait_ge(s_act, job_end("lin0", b))
                    turn("T_h1", b, H)
            carry_turns(1)
            for stage, b in in_stages("sage2"):
                if stage == 0:
                    pe.wait_ge(s_vec, MARK[f"agg1_{b}"])
                    turn("T_agg1", b, node_rows(1))
                elif stage == 1:
                    linear("lin1", b, [(aT, wi["L0_gnn_W2l"]), (KEEP, wi["L0_gnn_W2r"])], bi["L0_gnn_b2"], "T_agg1")
                elif stage == 4:
                    pe.wait_ge(s_norm, NORM["in2", b])
                    turn("T_in2", b, H)
                elif stage == 5:
                    project("qkvs2", b, wi["L1_gnn_k_w0"], 4, bi["L1_gnn_k_b0"], "T_in2")
            carry_turns(2)
            for stage, b in in_stages("conv1"):
                if stage == 0:
                    pe.wait_ge(s_vec, MARK[f"in3_{b}"])
                    turn("T_in3", b, node_rows(2))
                else:
                    project("qkvs3", b, wi["L1_gnn_k_w1"], 4, bi["L1_gnn_k_b1"], "T_in3")
            carry_turns(3)
            for stage, b in in_stages("conv2"):
                if stage == 2:
                    pe.wait_ge(s_norm, NORM["in4", b])
                    turn("T_in4", b, H)
                elif stage == 3:
                    project("qkv4", b, wi["L2_gnn_Wk"], 3, bi["L2_gnn_bk"], "T_in4")
            carry_turns(4)
            for stage, b in in_stages("graph"):
                if stage == 0:
                    pe.wait_ge(s_vec, MARK[f"att4_{b}"])
                    turn("T_att4", b, node_rows(4))
                elif stage == 1:
                    linear("wo4", b, [(aT, wi["L2_gnn_Wo"])], bi["L2_gnn_bo"], "T_att4")
                elif stage == 4:
                    pe.wait_ge(s_vec, MARK[f"ffn4_{b}"])
                    turn("T_ffn4", b, T2)
            for stage, b in in_stages("gelu"):
                b0, b1 = BLOCKS[b]
                ps = open_bank(JOB["up4", b][0])
                pe.wait_ge(s_act, job_end("T_ffn4", b))
                pe.matmul(ps[:, 0:(b1 - b0) * NP], W[:, wi["L2_gnn_W1"], :], KEEP[:, b0 * NP:b1 * NP],
                          start=True, stop=True).then_inc(s_pe, 1)
            for stage, b in in_stages("ffn"):
                if stage == 0:
                    linear("down4", b, [(aT, wi["L2_gnn_W2"])], bi["L2_gnn_b2"], "up4")
            carry_turns(5)
            for stage, b in in_stages("gin1"):
                if stage == 0:
                    pe.wait_ge(s_vec, MARK[f"z5_{b}"])
                    turn("T_z5", b, node_rows(5))
                else:
                    linear("lin5", b, [(aT, wi["L3_gnn_W1"])], bi["L3_gnn_b1"], "T_z5")
            carry_turns(6)
            for stage, b in in_stages("gin2"):
                if stage == 0:
                    pe.wait_ge(s_vec, MARK[f"z6_{b}"])
                    turn("T_z6", b, node_rows(6))
                elif stage == 1:
                    linear("lin6", b, [(aT, wi["L3_gnn_W2"])], bi["L3_gnn_b2"], "T_z6")

        @block.sync
        def _(sp):
            def by_part(a):
                return a.rearrange("(p i) f -> p i f", i=NB)

            def block_of(a, b):
                return by_part(a)[:, BLOCKS[b][0]:BLOCKS[b][1], :]

            for b, (b0, b1) in enumerate(BLOCKS):
                sp.dma_start(XR[0:NP, b0:b1, :], block_of(A["x"], b)).then_inc(s_x[b], 16)
            sp.wait_ge(s_vec, MARK["pads"])
            for dst, name in ((src_i, "src"), (dst_i, "dst"), (type_i, "edge_type_8")):
                sp.dma_start(dst[0:FULL, :], A[name][0:FULL * STEPS].rearrange("(p t) -> p t", t=STEPS))\
                    .then_inc(s_edges, 16)
                sp.dma_start(dst[FULL:FULL + 1, 0:REST], A[name][FULL * STEPS:E].rearrange("(p t) -> p t", p=1))\
                    .then_inc(s_edges, 16)
            sp.dma_start(before[1:FULL + 1, :],
                         A["dst"][0:FULL * STEPS].rearrange("(p t) -> p t", t=STEPS)[:, STEPS - 1:STEPS],
                         allow_slow_non_contiguous=True).then_inc(s_before, 16)
            for b, (b0, b1) in enumerate(BLOCKS):
                sp.wait_ge(s_norm, NORM["h0", b])
                sp.dma_start(block_of(table[0], b), H[0:NP, b0:b1, :]).then_inc(s_table, 16)
            for i, n in enumerate(W_ORDER):
                sp.dma_start(W[:, i, :], A[n]).then_inc(s_weights, 16)
            for i, n in enumerate(B_ORDER):
                sp.dma_start(brow[:, i, :], A[n].unsqueeze(0)).then_inc(s_weights, 16)
            for i, n in enumerate(AFFINE):
                sp.dma_start(affine[:, i, :], A[n].partition_broadcast(P)).then_inc(s_weights, 16)
            sp.dma_start(ebias[:, :, :].rearrange("p k h -> p (k h)"),
                         A["L2_gnn_edge_bias"].rearrange("k h -> (k h)").partition_broadcast(P))\
                .then_inc(s_weights, 16)
            sp.dma_start(colb[:, :], A["L2_gnn_b1"].unsqueeze(1), allow_slow_non_contiguous=True).then_inc(s_weights, 16)

            def store_rows(k):
                w = AW if KINDS[k] == ATT else D
                dst = rows[KINDS[k]].rearrange("(p t) f -> p (t f)", t=STEPS)
                with sp.Fori(0, LOOPS) as it:
                    for s in range(RING):
                        g = it * RING + s
                        if KINDS[k] == ATT:
                            sp.wait_ge(s_rows, g * 3 + (rows_base[k] + 3))
                        else:
                            sp.wait_ge(s_agg, g * GROUP + (agg_base[k] + GROUP))
                        sp.dma_start(dst[:, bass.ds(g * (GROUP * w), GROUP * w)],
                                     slot_out(k, s).rearrange("p j f -> p (j f)")).then_inc(s_store[s], 16)

            def store_kvq(k, name):
                at, after = by_part(qtable[k][:, 0:D]), by_part(qtable[k][:, D:2 * D])
                for b, (b0, b1) in enumerate(BLOCKS):
                    rows3 = kvq[:, b % QBUF, 0:b1 - b0, :]
                    queries = rows3[:, :, 2 * D:3 * D]
                    done = s_kvq[b % QBUF]
                    sp.wait_ge(s_act, job_end(name, b))
                    sp.dma_start(block_of(table[k], b), rows3[:, :, 0:2 * D]).then_inc(done, 16)
                    sp.dma_start(at[:, b0:b1, :], queries).then_inc(done, 16)
                    if b == 0:
                        sp.dma_start(after[:, 0:b1 - 1, :], queries[:, 1:b1, :]).then_inc(done, 16)
                        sp.dma_start(after[0:NP - 1, NB - 1, :], queries[1:NP, 0, :]).then_inc(done, 16)
                    else:
                        sp.dma_start(after[:, b0 - 1:b1 - 1, :], queries).then_inc(done, 16)
                    if b == NBLK - 1:
                        sp.dma_start(after[NP - 1:NP, NB - 1, :], queries[NP - 1:NP, b1 - b0 - 1, :])\
                            .then_inc(done, 16)

            def store_linear(k, name):
                for b, (b0, b1) in enumerate(BLOCKS):
                    sp.wait_ge(s_act, job_end(name, b))
                    sp.dma_start(block_of(table[k], b), H[0:NP, b0:b1, :]).then_inc(s_table, 16)

            sp.wait_ge(s_vec, MARK["biases"])
            for i in range(2):
                sp.dma_start(brow3[1 + i:2 + i, :, :], brow_low[:, i, :, :]).then_inc(s_parts, 16)
            store_rows(0)
            sp.wait_ge(s_vec, MARK["info"])
            for i, a in enumerate((deg_sb, end_sb)):
                sp.dma_start(node_info[i].rearrange("(h l) -> h l", l=LO), a[:, :]).then_inc(s_info, 16)
            sp.wait_ge(s_info, 32)
            for i in range(2):
                sp.dma_start(info[0:NP, i, :], node_info[i, 0:N].rearrange("(p i) -> p i", i=NB))\
                    .then_inc(s_infold, 16)
            store_linear(1, "lin0")
            store_rows(1)
            store_kvq(2, "qkvs2")
            store_rows(2)
            store_kvq(3, "qkvs3")
            store_rows(3)
            store_kvq(4, "qkv4")
            store_rows(4)
            for b, (b0, b1) in enumerate(BLOCKS):
                sp.wait_ge(s_norm, NORM["h5", b])
                sp.dma_start(block_of(table[5], b), H[0:NP, b0:b1, :]).then_inc(s_table, 16)
            store_rows(5)
            store_linear(6, "lin5")
            store_rows(6)
            for b, (b0, b1) in enumerate(BLOCKS):
                sp.wait_ge(s_vec, MARK[f"result_{b}"])
                sp.dma_start(block_of(A["out"], b), XR[0:NP, b0:b1, :]).then_inc(s_out, 16)
            sp.wait_ge(s_out, 16 * NBLK)

        @block.gpsimd
        def _(pool):
            pool.iota(lo_iota_i[:, :], [[1, LO]], base=0, channel_multiplier=0).then_inc(s_const, 1)
            pool.iota(part_i[:, :], [[0, 1]], base=-1, channel_multiplier=STEPS).then_inc(s_const, 1)
            pool.memset(ident[:, :], 0.0).then_inc(s_zero, 1)
            pool.memset(upper[:, :], 1.0).then_inc(s_zero, 1)
            pool.wait_ge(s_zero, 2)
            pool.affine_select(out=ident[:, :], in_=ident[:, :], compare_op=ALU.not_equal, fill=1.0, base=0,
                               pattern=[[-1, P]], channel_multiplier=1).then_inc(s_const, 1)
            pool.affine_select(out=upper[:, :], in_=upper[:, :], compare_op=ALU.is_gt, fill=0.0, base=0,
                               pattern=[[1, HI]], channel_multiplier=-1).then_inc(s_const, 1)

            def fetch(dst, tab, idx, done):
                pool.indirect_dma_start(dst, None, tab, bass.IndirectOffsetOnAxis(ap=idx, axis=0))\
                    .then_inc(done, 16)

            def rows_of_group(k, s):
                for j in range(GROUP):
                    fetch(ring[:, s, j, 0:width[KINDS[k]]], table[k], near_idx[:, s, 0, j:j + 1], s_land[s])

            def staged(k, it, s):
                per = idx_per[KINDS[k]]
                pool.wait_ge(s_idx, (it * RING + s) * per + (idx_base[k] + per))
                pool.nop(nofuse=True)

            def far_group(k, it, s):
                g = it * RING + s
                staged(k, it, s)
                rows_of_group(k, s)
                if not (isinstance(it, int) and g == 0):
                    pool.wait_ge(s_att, after_a(k, g - 1, A_STEPS[k]))
                    pool.nop(nofuse=True)
                for j in range(GROUP):
                    fetch(prod[:, j, :], qtable[k].rearrange("n (a f) -> (n a) f", a=2),
                          near_idx[:, s, 1, j:j + 1], s_query)

            def run_pass(k):
                if KINDS[k] == ATT:
                    for b in range(NBLK - QBUF, NBLK):
                        pool.wait_ge(s_kvq[b % QBUF], kvq_count(k, b))
                else:
                    pool.wait_ge(s_table, table_count(k))
                if KINDS[k] != ATT:
                    with pool.Fori(0, LOOPS) as it:
                        for s in range(RING):
                            staged(k, it, s)
                            rows_of_group(k, s)
                    return
                with pool.If(slow > 0):
                    for s in range(RING):
                        far_group(k, 0, s)
                    with pool.Fori(1, LOOPS) as it:
                        for s in range(RING):
                            far_group(k, it, s)
                with pool.Else():
                    with pool.Fori(0, LOOPS) as it:
                        for s in range(RING):
                            staged(k, it, s)
                            fetch(window[:, s, :], qtable[k], near_idx[:, s, 1, 0:1], s_window[s])
                            rows_of_group(k, s)

            def fetch_nodes(k):
                w = AW if KINDS[k] == ATT else D
                if k == 0:
                    pool.wait_ge(s_vec, MARK["heads"])
                for s in range(RING):
                    pool.wait_ge(s_store[s], store_base(k + 1))
                fetch(head[:, 0:w], rows[KINDS[k]], head_i[:, 0:1], s_head)
                pool.wait_ge(s_vec, MARK[f"head{k}"])
                pool.indirect_dma_start(rows[KINDS[k]], bass.IndirectOffsetOnAxis(ap=head_i[:, 0:1], axis=0),
                                        head[:, 0:w], None).then_inc(s_patch, 16)
                pool.wait_ge(s_patch, 16 * (k + 1))
                if k == 0:
                    pool.wait_ge(s_vec, MARK["last"])
                for b, (b0, b1) in enumerate(BLOCKS):
                    for i in range(b0, b1):
                        fetch(node_rows(k)[:, i, :], rows[KINDS[k]], last_i[0:NP, i:i + 1], s_node[b])

            pool.wait_ge(s_const, 4)
            run_pass(0)
            fetch_nodes(0)
            pool.wait_ge(s_vec, MARK["windows"])
            slow = pool.value_load(slow_i[0:1, 0:1], min_val=0, max_val=1)
            for k in range(1, PASSES):
                run_pass(k)
                fetch_nodes(k)


_UNUSED = ("edge_weight1",)


def kernel(**inputs):
    import numpy as _np
    import concourse.bacc as _bacc
    from concourse import mybir as _mybir
    from concourse.bass_utils import run_bass_kernel_spmd as _run

    nc = _bacc.Bacc("TRN2", target_bir_lowering=False, num_devices=1)
    arrays, handles = {}, {}
    for name in inputs:
        if name in _UNUSED:
            continue
        a = _np.ascontiguousarray(inputs[name])
        arrays[f"in_{name}"] = a
        handles[name] = nc.dram_tensor(f"in_{name}", a.shape, _mybir.dt.from_np(a.dtype), kind="ExternalInput").ap()
    handles["out"] = nc.dram_tensor("out_x", (N, D), F32, kind="ExternalOutput").ap()
    gnn_kernel(nc, handles)
    r = _run(nc, [arrays], core_ids=[0])
    return r.results[0]["out_x"]
```

```python
from contextlib import ExitStack

import concourse.bass as bass
from concourse import mybir

F32 = mybir.dt.float32
BF16 = mybir.dt.bfloat16
I32 = mybir.dt.int32
U8 = mybir.dt.uint8
ALU = mybir.AluOpType
ACT = mybir.ActivationFunctionType
AX = mybir.AxisListType

P = 128
N = 3125
E = 100000
D = 128
HEADS = 8
CH = D // HEADS
TYPES = 8
NP = 125
NB = N // NP
GROUP = 7
RING = 4
LOOPS = 28
PER_WINDOW = 2
SPAN = PER_WINDOW * GROUP
GROUPS = RING * LOOPS
WINDOWS = RING // PER_WINDOW
STEPS = GROUP * GROUPS
EPAD = P * STEPS
FULL = E // STEPS
REST = E - FULL * STEPS
LO = 64
HI = -(-(N + 1) // LO)
AW = D + 2 * HEADS
PER_BANK = 4
BLOCKS = [(b, min(b + PER_BANK, NB)) for b in range(0, NB, PER_BANK)]
NBLK = len(BLOCKS)
QBUF = 4
NEG = -1.0e30
SCALE = CH ** -0.5
EPS = 1e-5
SUM, ATT, MAX = "sum", "att", "max"
KINDS = [SUM, SUM, ATT, ATT, ATT, MAX, MAX]
PASSES = len(KINDS)
PICKS = {0: [1, 1, 1, 1], 1: [1, 1, 1, 1], 5: [2, 1, 1, 1], 6: [2, 1, 1, 1]}


PHASES = {
    "start": [[], [], ["T_h0"]],
    "sage1": [["T_agg0"], ["lin0"], ["T_h1"]],
    "sage2": [["T_agg1"], ["lin1"], [], [], ["T_in2"], ["qkvs2"]],
    "conv1": [["T_in3"], ["qkvs3"]],
    "conv2": [[], [], ["T_in4"], ["qkv4"]],
    "graph": [["T_att4"], ["wo4"], [], [], ["T_ffn4"], ["up4"], ["down4"], [], [], []],
    "gin1": [["T_z5"], ["lin5"]],
    "gin2": [["T_z6"], ["lin6"], []],
}


def in_stages(phase):
    n = len(PHASES[phase])
    for slot in range(NBLK + n - 1):
        for stage in reversed(range(n)):
            if 0 <= slot - stage < NBLK:
                yield stage, slot - stage


def job_plan():
    plan, at = {}, 0
    for phase, stages in PHASES.items():
        for stage, b in in_stages(phase):
            for name in stages[stage]:
                n = BLOCKS[b][1] - BLOCKS[b][0] if name.startswith("qkv") else 1
                plan[name, b] = (at, n)
                at += n
    return plan


def gnn_kernel(nc, A):
    JOB = job_plan()
    MARK = {}
    NORM = {}

    def job_end(name, b):
        first, n = JOB[name, b]
        return first + n

    ctx = ExitStack()
    with ctx:
        def sb(name, shape, dt=F32):
            return ctx.enter_context(nc.sbuf_tensor(name, shape, dt))

        def sem(name):
            return ctx.enter_context(nc.semaphore(name))

        def dram(name, shape, dt=F32):
            return nc.dram_tensor(name, shape, dt, kind="Internal").ap()

        table = {k: dram(f"table{k}", [N, 2 * D if KINDS[k] == ATT else D]) for k in range(PASSES)}
        qtable = {k: dram(f"qtable{k}", [N, 2 * D]) for k in range(PASSES) if KINDS[k] == ATT}
        rows = {SUM: dram("rows_plain", [EPAD, D]), ATT: dram("rows_att", [EPAD, AW])}
        rows[MAX] = rows[SUM]
        dst_unsorted = dram("dst_unsorted", [EPAD], I32)
        sorted_edges = dram("sorted_edges", [EPAD, 4], I32)
        node_info = dram("node_info", [2, HI * LO])

        arena = sb("arena", [P, RING * GROUP * 3 * D])
        ring = arena[:, 0:RING * GROUP * 2 * D].rearrange("p (s j w) -> p s j w", s=RING, j=GROUP)
        window = arena[:, RING * GROUP * 2 * D:RING * GROUP * 2 * D + WINDOWS * 2 * D].rearrange(
            "p (s w) -> p s w", s=WINDOWS)
        ring_plain = arena[:, 0:RING * GROUP * D].rearrange("p (s j w) -> p s j w", s=RING, j=GROUP)
        TABLE_AT = RING * GROUP * D
        parts3 = arena[0:NP, TABLE_AT:TABLE_AT + 3 * NB * D // 2].bitcast(BF16).rearrange(
            "p (a i f) -> p a i f", a=3, f=D)
        TILE_AT = TABLE_AT + 3 * NB * D // 2
        tile_no = arena[0:NP, TILE_AT:TILE_AT + NB * P // 2].bitcast(BF16).rearrange("p (i e) -> p i e", e=P)
        PICK_AT = TILE_AT + NB * P // 2
        outs = sb("outs", [P, RING * GROUP * AW])
        out_plain = outs[:, 0:RING * GROUP * D].rearrange("p (s j w) -> p s j w", s=RING, j=GROUP)
        out_att = outs[:, :].rearrange("p (s j w) -> p s j w", s=RING, j=GROUP)
        work = sb("work", [P, 7760])
        XR = sb("XR", [P, NB, D])
        H = sb("H", [P, NB, D])
        KEEP = sb("KEEP", [P, NB * D])
        src_i = sb("src_i", [P, STEPS], I32)
        dst_i = sb("dst_i", [P, STEPS], I32)
        same = sb("same", [P, STEPS])
        fence = sb("fence", [P, STEPS])
        bias = sb("bias", [P, STEPS, HEADS])
        W = sb("W", [P, 20, D])
        brow3 = sb("brow3", [3, 17, D], BF16)
        affine = sb("affine", [P, 4, D])
        ebias = sb("ebias", [P, TYPES, HEADS])
        ident = sb("ident", [P, P])
        upper = sb("upper", [HI, HI])
        ones_bf = sb("ones_bf", [3, P], BF16)
        far_note = sb("far_note", [1, 1])
        lo_iota = sb("lo_iota", [P, LO])
        lo_iota_i = sb("lo_iota_i", [P, LO], I32)
        first_i = sb("first_i", [P, 1], I32)
        tile_base = sb("tile_base", [P, 1])
        part_i = sb("part_i", [P, 1], I32)
        head_i = sb("head_i", [P, 1], I32)
        zero_bf = sb("zero_bf", [P, LO], BF16)
        near_late = sb("near_late", [P, RING, GROUP], U8)
        near_idx = sb("near_idx", [P, RING, 2, GROUP], I32)
        hot_lo = sb("hot_lo", [P, 2, GROUP, LO], BF16)
        hot_hi = sb("hot_hi", [P, 2, GROUP, HI], BF16)
        late = sb("late", [P, STEPS], U8)
        unsorted_i = sb("unsorted_i", [P, 1], I32)
        slow_i = sb("slow_i", [P, 1], I32)
        sort_half = sb("sort_half", [P, P])
        sort_below = sb("sort_below", [P, 4 * GROUP])
        row4 = sb("row4", [P, 4], I32)
        rank_one = sb("rank_one", [P, 1], I32)
        before = sb("before", [P, 1], I32)
        small = sb("small", [P, 16])
        whole = sb("whole", [P, P])
        fenceT = sb("fenceT", [P, P])
        carT = sb("carT", [P, 3, P])
        carE = sb("carE", [P, 2, P])
        tails = sb("tails", [P, 3, D])
        contT = sb("contT", [P, P])
        contF = sb("contF", [P, P])
        head = sb("head", [P, AW])
        head_w = sb("head_w", [P, 3, HEADS])
        deg_sb = sb("deg_sb", [HI, LO])
        end_sb = sb("end_sb", [HI, LO])
        hist_tmp = sb("hist_tmp", [HI, LO])
        info = sb("info", [P, 5, NB])
        last_i = sb("last_i", [P, NB], I32)
        bn_st = sb("bn_st", [P, NB, 6])
        mean_var = sb("mean_var", [P, NB, 2])
        var = sb("var", [P, NB])
        root = sb("root", [P, NB])
        rinv = sb("rinv", [P, NB])
        rden = sb("rden", [P, NB, HEADS])
        fences = sb("fences", [P, RING, HEADS, GROUP + 1])
        UA = sb("UA", [P, RING, 2, HEADS, GROUP + 1])
        MS = sb("MS", [P, RING, HEADS, GROUP + 1])
        LS = sb("LS", [P, RING, HEADS, GROUP + 1])
        DE = sb("DE", [P, 2, 2, HEADS, GROUP])
        LD = sb("LD", [P, 2, HEADS, GROUP + 1])
        LA = sb("LA", [P, 2, HEADS, GROUP + 1])

        last_rows = arena[0:NP, 0:NB * AW]
        kvq = arena[0:NP, NB * AW:NB * AW + QBUF * PER_BANK * 3 * D].rearrange(
            "p (s i f) -> p s i f", s=QBUF, f=3 * D)
        T1 = outs[:, 0:NB * D].rearrange("p (i f) -> p i f", f=D)
        aT = work[:, 0:N]
        T2 = work[:, NB * D:2 * NB * D].rearrange("p (i f) -> p i f", f=D)
        KN = KEEP[:, :].rearrange("p (i f) -> p i f", f=D)

        def node_rows(k):
            w = AW if KINDS[k] == ATT else D
            return last_rows[:, 0:NB * w].rearrange("p (i f) -> p i f", f=w)

        SEVERAL = 4 * GROUP
        dstf, bound, rank, column_no, later, equal = (work[:, i * STEPS:(i + 1) * STEPS] for i in range(6))
        rank_i = bound.bitcast(I32)
        column_no_i = later.bitcast(I32)
        part_less_i = rank[:, 0:P].bitcast(I32)
        below = arena[:, 0:SEVERAL * STEPS // 4].bitcast(U8).rearrange("p (a t) -> p a t", a=SEVERAL)
        other_i = arena[:, 7 * STEPS:8 * STEPS].bitcast(I32)
        other = arena[:, 8 * STEPS:9 * STEPS]
        edges_back = arena[:, 0:4 * STEPS].bitcast(I32).rearrange("p (t c) -> p t c", c=4)
        MORE_AT = NB * P + STEPS + GROUP * TYPES * (1 + HEADS)
        bias_flat = bias[:, :, :].rearrange("p t h -> p (t h)")
        brow = bias_flat[0:1, NB * P:NB * P + 17 * D].rearrange("p (i f) -> p i f", f=D)
        LOW_AT = NB * P + STEPS
        brow_low = work[0:1, LOW_AT:LOW_AT + 17 * D].bitcast(BF16).rearrange("p (a i f) -> p a i f", a=2, f=D)
        GD, GS = GROUP * D, (GROUP + 1) * D
        prod = work[:, 0:GD].rearrange("p (j f) -> p j f", j=GROUP)
        msg = [work[:, GD + b * GS:GD + (b + 1) * GS] for b in range(2)]
        dB = [work[:, GD + (2 + b) * GS:GD + (3 + b) * GS] for b in range(2)]
        OS = [work[:, GD + (4 + b) * GS:GD + (5 + b) * GS] for b in range(2)]
        lohi = work[:, 0:2 * STEPS].rearrange("p (a t) -> p a t", a=2)
        lohi_i = work[:, 2 * STEPS:4 * STEPS].bitcast(I32).rearrange("p (a t) -> p a t", a=2)
        typef = work[:, NB * P:NB * P + STEPS]
        type_i = work[:, 6 * STEPS:7 * STEPS].bitcast(I32)
        hot_ty = work[:, NB * P + STEPS:NB * P + STEPS + GROUP * TYPES].rearrange("p (j k) -> p j k", k=TYPES)
        bias_k = work[:, NB * P + STEPS + GROUP * TYPES:MORE_AT].rearrange(
            "p (j h k) -> p j h k", k=TYPES, h=HEADS)
        left = {k: (bias_flat if k == 0 else work)[0:NP, 0:NB * D].rearrange("p (i f) -> p i f", f=D)
                for k in PICKS}
        HOT = NB * P // 2
        HOT_AT = {0: [(bias_flat, 0), (bias_flat, HOT), (work, 2 * STEPS), (work, LOW_AT + 17 * D)],
                  1: [(work, 0), (work, HOT), (work, MORE_AT), (work, MORE_AT + HOT)]}
        HOT_AT[5] = HOT_AT[6] = [(work, u * HOT) for u in range(RING)] + [(bias_flat, 0)]
        hot_src = {k: [a[0:NP, at:at + HOT].bitcast(BF16).rearrange("p (i e) -> p i e", e=P)
                       for a, at in HOT_AT[k]] for k in PICKS}
        pick_at = [arena[:, PICK_AT + u * (NP + P // 2):] for u in range(RING)] + [bias_flat[:, HOT:]]
        pick_src = [a[:, 0:NP] for a in pick_at]
        pick_tile = [a[0:NP, NP:NP + P // 2].bitcast(BF16) for a in pick_at]

        def by_edge(a):
            return a.rearrange("p (f t) -> p t f", t=GROUP + 1)[:, 1:GROUP + 1, :]

        def column(a, t):
            return a.rearrange("p (f t) -> p f t", t=GROUP + 1)[:, :, t]

        bank = [ctx.enter_context(nc.psum_tensor(f"bank{b}", [P, 512], F32)) for b in range(4)]
        hist_ps = ctx.enter_context(nc.psum_tensor("hist_ps", [P, 512], F32))
        cin_ps = ctx.enter_context(nc.psum_tensor("cin_ps", [P, 512], F32))
        cout_ps = ctx.enter_context(nc.psum_tensor("cout_ps", [P, 512], F32))
        flag_ps = ctx.enter_context(nc.psum_tensor("flag_ps", [P, 512], F32))

        pick_bank = [b[:, 0:3 * D].rearrange("p (a f) -> p a f", a=3)
                     for b in (bank[1], bank[2], bank[3], cin_ps, cout_ps)]
        source_bank = [bank[0][0:NP, u * P:(u + 1) * P] for u in range(RING)] + [hist_ps[0:NP, 0:P]]

        s_x = [sem(f"x_loaded{b}") for b in range(NBLK)]
        s_edges = sem("edges_loaded")
        s_weights = sem("weights_loaded")
        s_parts = sem("bias_parts_laid")
        s_const = sem("constants_made")
        s_zero = sem("constants_cleared")
        s_before = sem("before_loaded")
        s_flagT = sem("flags_transposed")
        s_vec = sem("vec_done")
        s_pe = sem("pe_jobs")
        s_act = sem("act_jobs")
        s_root = sem("roots_taken")
        s_norm = sem("norm_scaled")
        s_table = sem("tables_stored")
        s_idx = sem("indices_staged")
        s_land = [sem(f"rows_landed{s}") for s in range(RING)]
        s_window = [sem(f"windows_landed{s}") for s in range(WINDOWS)]
        s_query = sem("edge_queries_landed")
        s_laid = sem("queries_laid")
        s_order = sem("order_checked")
        s_spilled = sem("unsorted_stored")
        s_other = sem("other_edges_loaded")
        s_rank = sem("rank_steps")
        s_row = sem("ranked_rows_laid")
        s_placed = sem("ranked_rows_stored")
        s_back = sem("sorted_edges_loaded")
        s_far = sem("far_windows_summed")
        s_col = sem("pick_sources_laid")
        s_across = sem("pick_sources_turned")
        s_tile = sem("pick_tiles_numbered")
        s_onehot = sem("pick_onehots_made")
        s_pick = sem("rows_picked")
        s_whole = sem("picked_parts_summed")
        s_on = sem("carried_on")
        s_store = [sem(f"rows_stored{s}") for s in range(RING)]
        s_agg = sem("agg_steps")
        s_att = sem("att_steps")
        s_weigh = sem("weights_exped")
        s_rows = sem("att_rows_laid")
        s_hot = sem("hots_made")
        s_hist = sem("hist_groups")
        s_bias = sem("bias_steps")
        s_off = sem("offsets_summed")
        s_info = sem("node_info_stored")
        s_infold = sem("node_info_loaded")
        s_kvq = [sem(f"kvq_stored{i}") for i in range(QBUF)]
        s_cin = sem("carry_turned")
        s_cexp = sem("carry_exps")
        s_cout = sem("carry_turned_back")
        s_head = sem("heads_landed")
        s_hexp = sem("head_exps")
        s_patch = sem("heads_stored")
        s_node = [sem(f"node_rows_landed{b}") for b in range(NBLK)]
        s_out = sem("output_stored")

        def picks(k, s):
            return PICKS[k][s] if k in PICKS else 0

        def units(k, s):
            return [(s, GROUP - 1), (RING, GROUP - 2)][:picks(k, s)]

        pick_base, picked_before = {}, 0
        for k in PICKS:
            pick_base[k] = picked_before
            picked_before += sum(PICKS[k]) * (LOOPS - 1)

        def pick_number(k, it, s):
            return (it - 1) * sum(PICKS[k]) + (pick_base[k] + sum(PICKS[k][:s]))

        def landed(k, it, s):
            each = 16 * (GROUP - picks(k, s))
            return it * each + (16 * GROUP + land_base[k][s])

        idx_per = {SUM: 1, MAX: 1, ATT: 4}
        agg_base, att_base, land_base, weigh_base, idx_base = {}, {}, {}, {}, {}
        A_STEPS = {k: 6 + (k == 4) for k in range(PASSES)}
        B_STEPS = 3
        a = t = w = x = 0
        l = [0] * RING
        for k in range(PASSES):
            agg_base[k], att_base[k], land_base[k], weigh_base[k] = a, t, list(l), w
            idx_base[k] = x
            x += idx_per[KINDS[k]] * GROUPS
            for s in range(RING):
                l[s] += 16 * (GROUP * LOOPS - (LOOPS - 1) * picks(k, s))
            if KINDS[k] == ATT:
                t += (A_STEPS[k] + B_STEPS) * GROUPS
                w += 3 * GROUPS
            else:
                a += STEPS
        rows_base = weigh_base

        def store_base(k):
            return 16 * LOOPS * k

        def after_a(k, g, i):
            first = A_STEPS[k] * g + B_STEPS * (g - 1)
            if isinstance(g, int) and g == 0:
                first = 0
            return first + att_base[k] + i

        def after_b(k, g, i):
            na = GROUPS if isinstance(g, int) and g == GROUPS - 1 else g + 2
            return na * A_STEPS[k] + B_STEPS * g + att_base[k] + i

        W_ORDER = ["L0_gnn_W1l", "L0_gnn_W1r", "L0_gnn_W2l", "L0_gnn_W2r",
                   "L1_gnn_k_w0", "L1_gnn_v_w0", "L1_gnn_q_w0", "L1_gnn_s_w0",
                   "L1_gnn_k_w1", "L1_gnn_v_w1", "L1_gnn_q_w1", "L1_gnn_s_w1",
                   "L2_gnn_Wk", "L2_gnn_Wv", "L2_gnn_Wq", "L2_gnn_Wo", "L2_gnn_W1", "L2_gnn_W2",
                   "L3_gnn_W1", "L3_gnn_W2"]
        B_ORDER = ["L0_gnn_b1", "L0_gnn_b2",
                   "L1_gnn_k_b0", "L1_gnn_v_b0", "L1_gnn_q_b0", "L1_gnn_s_b0",
                   "L1_gnn_k_b1", "L1_gnn_v_b1", "L1_gnn_q_b1", "L1_gnn_s_b1",
                   "L2_gnn_bk", "L2_gnn_bv", "L2_gnn_bq", "L2_gnn_bo", "L2_gnn_b2", "L3_gnn_b1", "L3_gnn_b2"]
        AFFINE = ["L2_gnn_g1", "L2_gnn_be1", "L2_gnn_g2", "L2_gnn_be2"]
        wi = {n: i for i, n in enumerate(W_ORDER)}
        bi = {n: i for i, n in enumerate(B_ORDER)}
        colb = sb("colb", [P, 1])
        N_WEIGHTS = len(W_ORDER) + len(B_ORDER) + len(AFFINE) + 2

        def cin_count(k):
            return k + 1

        def att_number(k):
            return [j for j in range(PASSES) if KINDS[j] == ATT].index(k)

        def table_count(k):
            return 16 * NBLK * sum(KINDS[j] != ATT for j in range(k + 1))

        def kvq_stores(b):
            return 3 + (b in (0, NBLK - 1))

        def kvq_count(k, b):
            mine = range(b % QBUF, NBLK, QBUF)
            return 16 * (att_number(k) * sum(kvq_stores(i) for i in mine) + sum(kvq_stores(i) for i in mine if i <= b))

        def node_count(k, b):
            return 16 * (BLOCKS[b][1] - BLOCKS[b][0]) * (k + 1)

        def slot_out(k, s):
            return (out_att if KINDS[k] == ATT else out_plain)[:, s, :, :]

        block = ctx.enter_context(nc.Block())

        @block.vector
        def _(v):
            done = [0]

            def step(ins, mark=None):
                done[0] += 1
                ins.then_inc(s_vec, 1)
                v.wait_ge(s_vec, done[0])
                if mark:
                    MARK[mark] = done[0]

            def ready(semaphore, value):
                if not (isinstance(value, int) and value == 0):
                    v.wait_ge(semaphore, value)

            def tiles(a, b):
                return a[0:NP, BLOCKS[b][0]:BLOCKS[b][1], :]

            def spread(a, b, last=D):
                b0, b1 = BLOCKS[b]
                return a[0:NP, b0:b1].unsqueeze(2).to_broadcast([NP, b1 - b0, last])

            roots = {}

            def moments(name, src, b):
                b0, b1 = BLOCKS[b]
                for i in range(b0, b1):
                    ins = v.bn_stats(bn_st[0:NP, i, :], src[0:NP, i, :])
                step(ins)
                for i in range(b0, b1):
                    ins = v.bn_aggr(mean_var[0:NP, i, :], bn_st[0:NP, i, :])
                step(ins)
                step(v.tensor_scalar(var[0:NP, b0:b1], mean_var[0:NP, b0:b1, 1], EPS, None, ALU.add),
                     f"var_{name}_{b}")
                roots[name, b] = len(roots) + 1

            def rectified(src, dst, b):
                for i in range(*BLOCKS[b]):
                    ins = v.tensor_scalar(dst[0:NP, i, :], src[0:NP, i, :], mean_var[0:NP, i, 0:1], 0.0,
                                          ALU.subtract, ALU.max)
                step(ins)

            def inverse_root(name, b):
                b0, b1 = BLOCKS[b]
                v.wait_ge(s_root, roots[name, b])
                step(v.reciprocal(rinv[0:NP, b0:b1], root[0:NP, b0:b1]), f"rinv_{name}_{b}")

            def mapped(name, src, dst, b, row, more, mark=None):
                for i in range(*BLOCKS[b]):
                    ins = v.scalar_tensor_tensor(src[0:NP, i, :], src[0:NP, i, :], mean_var[0:NP, i, 0:1],
                                                 affine[0:NP, row, :], ALU.subtract, ALU.mult)
                step(ins)
                inverse_root(name, b)
                for i in range(*BLOCKS[b]):
                    ins = v.scalar_tensor_tensor(dst[0:NP, i, :], src[0:NP, i, :], rinv[0:NP, i:i + 1], more(i),
                                                 ALU.mult, ALU.add)
                step(ins, mark)

            RANK_FIRST, RANK_EACH = 5, 2 + 3 * (STEPS // SEVERAL)

            def rank_edges():
                def counted(ins, n):
                    ins.then_inc(s_rank, 1)
                    v.wait_ge(s_rank, n)

                counted(v.tensor_copy(column_no, column_no_i), 1)
                counted(v.tensor_copy(sort_half[:, :], part_less_i), 2)
                counted(v.tensor_scalar(sort_half[:, :], sort_half[:, :], 0.0, -0.5, ALU.is_lt, ALU.add), 3)
                counted(v.memset(rank, 0.0), 4)
                counted(v.memset(row4[:, :], 0), 5)
                with v.Fori(0, P) as j:
                    at = j * RANK_EACH + RANK_FIRST
                    v.wait_ge(s_other, j * 16 + 16)
                    counted(v.tensor_copy(other, other_i), at + 1)
                    counted(v.tensor_scalar(bound, dstf, sort_half[:, bass.ds(j, 1)], None, ALU.add), at + 2)
                    v.nop(nofuse=True)
                    wide = [P, SEVERAL, STEPS]
                    with v.Fori(0, STEPS // SEVERAL) as a:
                        mine = bass.ds(a * SEVERAL, SEVERAL)
                        n = at + a * 3 + 2
                        counted(v.tensor_tensor(below, bound[:, mine].unsqueeze(2).to_broadcast(wide),
                                                other.unsqueeze(1).to_broadcast(wide), ALU.is_gt), n + 1)
                        counted(v.tensor_reduce(sort_below[:, :], below, AX.X, ALU.add), n + 2)
                        counted(v.tensor_tensor(rank[:, mine], rank[:, mine], sort_below[:, :], ALU.add), n + 3)
                first = RANK_FIRST + P * RANK_EACH
                with v.Fori(0, STEPS) as t:
                    n = t * 3 + first
                    one = bass.ds(t, 1)
                    counted(v.tensor_scalar(later, column_no, column_no[:, one], None, ALU.is_gt), n + 1)
                    counted(v.scalar_tensor_tensor(equal, dstf, dstf[:, one], later, ALU.is_equal, ALU.mult), n + 2)
                    counted(v.tensor_tensor(rank, rank, equal, ALU.add), n + 3)
                first += 3 * STEPS
                counted(v.tensor_copy(rank_i, rank), first + 1)

                def row_of(t):
                    one = bass.ds(t, 1)
                    v.tensor_copy(row4[:, 0:1], src_i[:, one])
                    v.tensor_copy(row4[:, 1:2], dst_i[:, one])
                    v.tensor_copy(row4[:, 2:3], type_i[:, one])
                    v.tensor_copy(rank_one[:, :], rank_i[:, one]).then_inc(s_row, 1)

                row_of(0)
                with v.Fori(1, STEPS) as t:
                    v.wait_ge(s_placed, t * 16)
                    row_of(t)
                v.wait_ge(s_back, 32)
                v.tensor_copy(src_i[:, :], edges_back[:, :, 0])
                v.tensor_copy(dst_i[:, :], edges_back[:, :, 1])
                counted(v.tensor_copy(type_i[:, :], edges_back[:, :, 2]), first + 2)

            step(v.memset(src_i[:, :], 0))
            step(v.memset(dst_i[:, :], N))
            step(v.memset(type_i[:, :], 0))
            step(v.memset(before[:, :], -1), "pads")
            for stage, b in in_stages("start"):
                if stage == 0:
                    v.wait_ge(s_x[b], 16)
                    moments("h0", XR, b)
                    rectified(XR, H, b)
                elif stage == 1:
                    inverse_root("h0", b)
            v.wait_ge(s_const, 5)
            v.wait_ge(s_edges, 16 * 6)
            v.wait_ge(s_before, 16)
            step(v.tensor_copy(dstf, dst_i[:, :]))
            step(v.tensor_copy(small[:, 0:1], before[:, :]))
            step(v.tensor_tensor(equal[:, 0:1], dstf[:, 0:1], small[:, 0:1], ALU.is_lt))
            step(v.tensor_tensor(equal[:, 1:STEPS], dstf[:, 1:STEPS], dstf[:, 0:STEPS - 1], ALU.is_lt))
            step(v.memset(carT[:, 1, :], 1.0))
            step(v.tensor_reduce(small[:, 9:10], equal, AX.X, ALU.max), "disorder")
            v.wait_ge(s_order, 1)
            step(v.tensor_scalar(unsorted_i[:, :], flag_ps[:, 301:302], 0.0, None, ALU.is_gt), "order")
            unsorted = v.value_load(unsorted_i[0:1, 0:1], min_val=0, max_val=1)
            with v.If(unsorted > 0):
                rank_edges()
            step(v.tensor_copy(dstf, dst_i[:, :]), "ordered")
            step(v.memset(out_plain[:, RING - 1, GROUP - 1, :], 0.0))
            step(v.memset(window, 0.0))
            step(v.memset(zero_bf[:, :], 0.0))

            step(v.memset(same[:, 0:1], 0.0))
            step(v.tensor_tensor(same[:, 1:STEPS], dstf[:, 1:STEPS], dstf[:, 0:STEPS - 1], ALU.is_equal))
            step(v.tensor_scalar(fence[:, :], same[:, :], -1.0, -NEG, ALU.add, ALU.mult))
            step(v.tensor_copy(small[:, 0:1], before[:, :]))
            step(v.tensor_tensor(small[:, 1:2], dstf[:, 0:1], small[:, 0:1], ALU.is_equal))
            step(v.tensor_tensor(small[:, 2:3], dstf[:, 0:1], dstf[:, STEPS - 1:STEPS], ALU.is_equal))
            step(v.tensor_tensor(small[:, 3:4], small[:, 1:2], small[:, 2:3], ALU.mult))
            step(v.tensor_copy(tails[:, 1, :], small[:, 1:2].to_broadcast([P, P])))
            step(v.tensor_copy(tails[:, 0, :], small[:, 3:4].to_broadcast([P, P])), "whole")
            step(v.tensor_tensor(typef, dstf, dstf[:, 0:1].to_broadcast([P, STEPS]), ALU.is_equal))
            step(v.tensor_reduce(small[:, 7:8], typef, AX.X, ALU.add))
            step(v.tensor_copy(small[:, 8:9], part_i[:, :]))
            step(v.tensor_copy(tile_base[:, :], first_i[:, :]))
            step(v.tensor_tensor(head_i[:, :], small[:, 7:8], small[:, 8:9], ALU.add), "heads")
            step(v.tensor_single_scalar(lohi_i[:, 0, :], dst_i[:, :], LO - 1, ALU.bitwise_and))
            step(v.tensor_single_scalar(lohi_i[:, 1, :], dst_i[:, :], LO.bit_length() - 1, ALU.arith_shift_right))
            step(v.tensor_scalar(dst_i[:, :], dst_i[:, :], float(N - 1), None, ALU.min))
            step(v.tensor_copy(dstf, dst_i[:, :]))
            by_window = dstf.rearrange("p (g j) -> p g j", j=SPAN)
            ahead = work[:, 5 * STEPS:6 * STEPS].rearrange("p (g j) -> p g j", j=SPAN)
            step(v.tensor_tensor(ahead, by_window, by_window[:, :, 0:1].to_broadcast([P, STEPS // SPAN, SPAN]),
                                 ALU.subtract))
            step(v.tensor_reduce(small[:, 5:6], ahead, AX.XY, ALU.max))
            step(v.tensor_scalar(small[:, 5:6], small[:, 5:6], 1.0, None, ALU.is_gt), "far")
            step(v.tensor_copy(lohi[:, :, :], lohi_i[:, :, :]))
            step(v.tensor_copy(lo_iota[:, :], lo_iota_i[:, :]))

            def plain_group(k, it, s):
                g = it * RING + s
                ahead_it, ahead_s = (it, s + 2) if s + 2 < RING else (it + 1, s + 2 - RING)
                ahead = picks(k, ahead_s) and not (isinstance(ahead_it, int) and ahead_it in (0, LOOPS))
                if k in (5, 6) and ahead:
                    one_hot(k, ahead_it, ahead_s)
                picked = units(k, s) if not (isinstance(it, int) and it == 0) else []
                v.wait_ge(s_land[s], landed(k, it, s))
                ready(s_store[s], it * 16 + store_base(k))
                first = it * (RING * GROUP) + s * GROUP
                flags = same if KINDS[k] == SUM else fence
                ops = (ALU.mult, ALU.add) if KINDS[k] == SUM else (ALU.add, ALU.max)
                for j in range(GROUP):
                    if picked and j == GROUP - 1 - len(picked):
                        whole_rows(k, it, s)
                    prev = out_plain[:, s, j - 1, :] if j else out_plain[:, (s - 1) % RING, GROUP - 1, :]
                    ready(s_agg, first + (agg_base[k] + j))
                    row = ring_plain[:, s, j, :]
                    for i, (u, step_of) in enumerate(picked):
                        if j == step_of:
                            v.wait_ge(s_whole, pick_number(k, it, s) + (i + 1))
                    v.scalar_tensor_tensor(out_plain[:, s, j, :], prev, flags[:, bass.ds(first + j, 1)],
                                           row, *ops).then_inc(s_agg, 1)
                    if k == 0 and j < 2:
                        hots(it, s, j)
                    if k == 1 and j < 3:
                        edge_bias(it, s, j)
                    if k in (0, 1) and j == k + 2 and ahead:
                        one_hot(k, ahead_it, ahead_s)

            def one_hot(k, it, s):
                for i, (u, _) in enumerate(units(k, s)):
                    v.wait_ge(s_tile, pick_number(k, it, s) + (i + 1))
                    v.tensor_tensor(hot_src[k][u], pick_tile[u].unsqueeze(1).to_broadcast([NP, NB, P]), tile_no,
                                    ALU.is_equal).then_inc(s_onehot, 1)

            def whole_rows(k, it, s):
                for i, (u, j) in enumerate(units(k, s)):
                    v.wait_ge(s_pick, pick_number(k, it, s) + (i + 1))
                    v.tensor_reduce(ring_plain[:, s, j, :], pick_bank[u].rearrange("p a f -> p f a"), AX.X,
                                    ALU.add).then_inc(s_whole, 1)

            def take_apart(k):
                if k in (0, 5):
                    v.wait_ge(s_norm, NBLK if k == 0 else 4 * NBLK)
                else:
                    v.wait_ge(s_act, job_end("lin0" if k == 1 else "lin5", NBLK - 1))
                h3 = H[0:NP, :, :]
                step(v.tensor_copy(tile_no, lo_iota[0:NP, 1:NB + 1].unsqueeze(2).to_broadcast([NP, NB, P])))
                step(v.tensor_copy(parts3[:, 0, :, :], h3))
                rest = left[k]
                step(v.tensor_tensor(rest, h3, parts3[:, 0, :, :], ALU.subtract))
                step(v.tensor_copy(parts3[:, 1, :, :], rest))
                step(v.tensor_tensor(rest, rest, parts3[:, 1, :, :], ALU.subtract))
                step(v.tensor_copy(parts3[:, 2, :, :], rest), f"parts{k}")

            def hots(it, s, part):
                b = s % 2
                first = it * (RING * GROUP) + s * GROUP
                if part == 0:
                    ready(s_hist, it * RING + s)
                hot, width = ((hot_lo, LO), (hot_hi, HI))[part]
                v.tensor_tensor(hot[:, b, :, :],
                                lohi[:, part, bass.ds(first, GROUP)].unsqueeze(2).to_broadcast([P, GROUP, width]),
                                lo_iota[:, 0:width].unsqueeze(1).to_broadcast([P, GROUP, width]),
                                ALU.is_equal).then_inc(s_hot, 1)

            def edge_bias(it, s, part):
                first = it * (RING * GROUP) + s * GROUP
                g3 = (it * RING + s) * 3
                ready(s_bias, g3 + part)
                if part == 0:
                    v.tensor_tensor(hot_ty[:, :, :],
                                    typef[:, bass.ds(first, GROUP)].unsqueeze(2).to_broadcast([P, GROUP, TYPES]),
                                    lo_iota[:, 0:TYPES].unsqueeze(1).to_broadcast([P, GROUP, TYPES]),
                                    ALU.is_equal).then_inc(s_bias, 1)
                elif part == 1:
                    v.tensor_tensor(bias_k,
                                    hot_ty.unsqueeze(2).to_broadcast([P, GROUP, HEADS, TYPES]),
                                    ebias[:, :, :].rearrange("p k h -> p h k").unsqueeze(1).to_broadcast(
                                        [P, GROUP, HEADS, TYPES]), ALU.mult).then_inc(s_bias, 1)
                else:
                    v.tensor_reduce(bias[:, bass.ds(first, GROUP), :], bias_k, AX.X, ALU.add).then_inc(s_bias, 1)

            def part_a(k, it, s, g):
                b = s % 2
                n = 0

                def chain(ins):
                    nonlocal n
                    n += 1
                    ins.then_inc(s_att, 1)
                    v.wait_ge(s_att, after_a(k, g, n))

                first = it * (RING * GROUP) + s * GROUP
                wide = [P, GROUP, D]
                v.wait_ge(s_laid, g + (att_number(k) * GROUPS + 1))
                v.nop(nofuse=True)
                chain(v.copy_predicated(prod, near_late[:, s, :].unsqueeze(2).to_broadcast(wide),
                                        window[:, s // PER_WINDOW, D:2 * D].unsqueeze(1).to_broadcast(wide)))
                v.wait_ge(s_land[s], landed(k, it, s))
                chain(v.tensor_tensor(prod, prod, ring[:, s, :, 0:D], ALU.mult))
                scores = UA[:, s, 1, :, 1:GROUP + 1].rearrange("p h j -> p j h")
                chain(v.tensor_reduce(scores, prod.rearrange("p j (h c) -> p j h c", c=CH), AX.X, ALU.add))
                if k == 4:
                    chain(v.tensor_tensor(scores, scores, bias[:, bass.ds(first, GROUP), :], ALU.add))
                v.wait_ge(s_idx, g * 4 + (idx_base[k] + 4))
                chain(v.tensor_tensor_scan(flat(MS[:, s, :, :]), flat(fences[:, s, :, :]),
                                           flat(UA[:, s, 1, :, :]), 0.0, ALU.add, ALU.max))
                chain(v.tensor_tensor(UA[:, s, 0, :, 1:GROUP + 1], MS[:, s, :, 0:GROUP],
                                      fences[:, s, :, 1:GROUP + 1], ALU.add))
                chain(v.tensor_tensor(DE[:, b, :, :, :], UA[:, s, :, :, 1:GROUP + 1],
                                      MS[:, s, :, 1:GROUP + 1].unsqueeze(1).to_broadcast([P, 2, HEADS, GROUP]),
                                      ALU.subtract))
                assert n == A_STEPS[k]

            def flat(a):
                return a.rearrange("p h t -> p (h t)")

            def part_b(k, it, s, g):
                b = s % 2
                n = 0

                def chain(ins):
                    nonlocal n
                    n += 1
                    ins.then_inc(s_att, 1)
                    v.wait_ge(s_att, after_b(k, g, n))

                v.wait_ge(s_weigh, g * 3 + (weigh_base[k] + 3))
                v.wait_ge(s_on, g + (att_number(k) * GROUPS + 1))
                chain(v.tensor_tensor_scan(flat(LS[:, s, :, :]), flat(LD[:, b, :, :]), flat(LA[:, b, :, :]),
                                           0.0, ALU.mult, ALU.add))
                vals = ring[:, s, :, D:2 * D].rearrange("p j (h c) -> p j h c", c=CH)
                wts = LA[:, b, :, 1:GROUP + 1].rearrange("p h j -> p j h").unsqueeze(3).to_broadcast(
                    [P, GROUP, HEADS, CH])
                chain(v.tensor_tensor(by_edge(msg[b]).rearrange("p j (h c) -> p j h c", c=CH), vals, wts,
                                      ALU.mult))
                if not (isinstance(g, int) and g < 2):
                    v.wait_ge(s_rows, g * 3 + (rows_base[k] - 3))
                chain(v.tensor_tensor_scan(OS[b], dB[b], msg[b], 0.0, ALU.mult, ALU.add))
                assert n == B_STEPS

            def carry_scan(k):
                v.wait_ge(s_cin, cin_count(k))
                turned = cin_ps[:, 0:3 * P].rearrange("p (a q) -> p a q", a=3)
                if KINDS[k] == SUM:
                    step(v.tensor_tensor_scan(carT[:, 0, :], whole[:, :], turned[:, 0, :], 0.0, ALU.mult, ALU.add))
                elif KINDS[k] == MAX:
                    step(v.tensor_tensor_scan(carT[:, 0, :], fenceT[:, :], turned[:, 0, :], NEG, ALU.add, ALU.max))
                else:
                    m = carT[:, 1, :]
                    step(v.tensor_tensor_scan(m, fenceT[:, :], turned[:, 1, :], 0.0, ALU.add, ALU.max))
                    step(v.tensor_copy(carE[:, 0, 0:1], fenceT[:, 0:1]))
                    step(v.tensor_tensor(carE[:, 0, 1:P], m[:, 0:P - 1], fenceT[:, 1:P], ALU.add))
                    step(v.tensor_tensor(carE[:, 0, :], carE[:, 0, :], m, ALU.subtract))
                    step(v.tensor_tensor(carE[:, 1, :], turned[:, 1, :], m, ALU.subtract), f"carry_in{k}")
                    v.wait_ge(s_cexp, att_number(k) + 1)
                    for i in (0, 2):
                        step(v.tensor_tensor(carT[:, i, :], turned[:, i, :], carE[:, 1, :], ALU.mult))
                        step(v.tensor_tensor_scan(carT[:, i, :], carE[:, 0, :], carT[:, i, :], 0.0,
                                                  ALU.mult, ALU.add))
                for i in (0, 1, 2) if KINDS[k] == ATT else (0,):
                    by_max = KINDS[k] == MAX or i == 1
                    step(v.memset(tails[:, i, 0:1], NEG if by_max else 0.0))
                    step(v.tensor_tensor(tails[:, i, 1:P], carT[:, i, 0:P - 1], (contF if by_max else contT)[:, 1:P],
                                         ALU.add if by_max else ALU.mult), f"carry{k}")

            def join_heads(k):
                v.wait_ge(s_cout, k + 1)
                if KINDS[k] != ATT:
                    v.wait_ge(s_head, 16 * (k + 1))
                    step(v.tensor_tensor(head[:, 0:D], head[:, 0:D], cout_ps[:, 0:D],
                                         ALU.add if KINDS[k] == SUM else ALU.max), f"head{k}")
                    return
                before_o, before_m, before_l = (cout_ps[:, i * P:(i + 1) * P].rearrange("p (h c) -> p h c", c=CH)
                                                for i in range(3))
                mx, dn = head[:, D:D + HEADS], head[:, D + HEADS:AW]
                wide = [P, HEADS, CH]
                step(v.tensor_copy(head_w[:, 2, :], before_m[:, :, 0]))
                v.wait_ge(s_head, 16 * (k + 1))
                step(v.tensor_tensor(head_w[:, 0, :], mx, head_w[:, 2, :], ALU.max))
                step(v.tensor_tensor(head_w[:, 1, :], mx, head_w[:, 0, :], ALU.subtract))
                step(v.tensor_tensor(head_w[:, 2, :], head_w[:, 2, :], head_w[:, 0, :], ALU.subtract), f"head_in{k}")
                v.wait_ge(s_hexp, att_number(k) + 1)
                old, new = head_w[:, 2, :], head_w[:, 1, :]
                vals = head[:, 0:D].rearrange("p (h c) -> p h c", c=CH)
                more = tails[:, 0, :].rearrange("p (h c) -> p h c", c=CH)
                step(v.tensor_tensor(vals, vals, new.unsqueeze(2).to_broadcast(wide), ALU.mult))
                step(v.tensor_tensor(more, before_o, old.unsqueeze(2).to_broadcast(wide), ALU.mult))
                step(v.tensor_tensor(vals, vals, more, ALU.add))
                step(v.tensor_tensor(dn, dn, new, ALU.mult))
                step(v.tensor_tensor(old, old, before_l[:, :, 0], ALU.mult))
                step(v.tensor_tensor(dn, dn, old, ALU.add))
                step(v.tensor_copy(mx, head_w[:, 0, :]), f"head{k}")

            def finish_setup():
                v.wait_ge(s_far, 1)
                step(v.tensor_scalar(slow_i[:, :], flag_ps[:, 300:301], 0.0, None, ALU.is_gt))
                step(v.tensor_scalar(small[:, 6:7], flag_ps[:, 300:301], 0.0, None, ALU.is_equal))
                step(v.tensor_scalar(late[:, :], work[:, 5 * STEPS:6 * STEPS], 0.0, small[:, 6:7], ALU.is_gt, ALU.mult),
                     "windows")
                step(v.tensor_copy(typef, type_i[:, :]))
                v.wait_ge(s_flagT, 1)
                step(v.tensor_copy(whole[:, :], flag_ps[:, 0:P]))
                step(v.tensor_copy(contT[:, :], flag_ps[:, P:2 * P]))
                step(v.tensor_scalar(contF[:, :], contT[:, :], -1.0, -NEG, ALU.add, ALU.mult))
                step(v.tensor_scalar(fenceT[:, :], whole[:, :], -1.0, -NEG, ALU.add, ALU.mult))
                step(v.memset(MS[:, :, :, :], 0.0))
                step(v.memset(LS[:, :, :, :], 0.0))
                step(v.memset(fences[:, :, :, :], NEG))
                step(v.memset(LD[:, :, :, :], 0.0))
                step(v.memset(ones_bf[:, :], 1.0))

            def prepare_weights():
                v.wait_ge(s_weights, 16 * N_WEIGHTS)
                for name in ("L1_gnn_q_w0", "L1_gnn_q_w1", "L2_gnn_Wq"):
                    step(v.tensor_scalar(W[:, wi[name], :], W[:, wi[name], :], SCALE, None, ALU.mult))
                for name in ("L1_gnn_q_b0", "L1_gnn_q_b1", "L2_gnn_bq"):
                    step(v.tensor_scalar(brow[:, bi[name], :], brow[:, bi[name], :], SCALE, None, ALU.mult))
                parts = brow3[0:1, :, :], brow_low[:, 0, :, :], brow_low[:, 1, :, :]
                for i, part in enumerate(parts):
                    step(v.tensor_copy(part, brow), "biases")
                    if i < 2:
                        step(v.tensor_tensor(brow, brow, part, ALU.subtract))

            def run_pass(k):
                if KINDS[k] != ATT:
                    for s in range(RING):
                        if s == 1:
                            take_apart(k)
                        plain_group(k, 0, s)
                    more = [(LOOPS // 2, finish_setup), (LOOPS * 3 // 4, prepare_weights)] if k == 0 else []
                    begin = 1
                    for end, prepare in more + [(LOOPS - 1, None)]:
                        with v.Fori(begin, end) as it:
                            for s in range(RING):
                                plain_group(k, it, s)
                        if prepare:
                            prepare()
                        begin = end
                    for s in range(RING):
                        plain_group(k, LOOPS - 1, s)
                    v.wait_ge(s_agg, agg_base[k] + STEPS)
                else:
                    part_a(k, 0, 0, 0)
                    for s in range(RING):
                        att_group(k, 0, s)
                    with v.Fori(1, LOOPS - 1) as it:
                        for s in range(RING):
                            att_group(k, it, s)
                    for s in range(RING):
                        att_group(k, LOOPS - 1, s)
                    b = (RING - 1) % 2
                    step(v.tensor_copy(tails[:, 0, :], column(OS[b], GROUP)))
                    for i, a in ((1, MS), (2, LS)):
                        step(v.tensor_copy(tails[:, i, :].rearrange("p (h c) -> p h c", c=CH),
                                           a[:, RING - 1, :, GROUP].unsqueeze(2).to_broadcast([P, HEADS, CH])),
                             f"tails{k}")

            def att_group(k, it, s):
                g = it * RING + s
                if not (isinstance(it, int) and g == GROUPS - 1):
                    s1 = (s + 1) % RING
                    part_a(k, it + (1 if s == RING - 1 else 0), s1, g + 1)
                part_b(k, it, s, g)

            def degrees():
                v.wait_ge(s_hist, GROUPS + 2)
                step(v.tensor_copy(deg_sb[:, :], hist_ps[0:HI, 0:LO]))
                step(v.memset(hist_tmp[:, :], 1.0))
                step(v.tensor_tensor_scan(end_sb[:, :], hist_tmp[:, :], deg_sb[:, :], 0.0, ALU.mult, ALU.add),
                     "row_totals")
                v.wait_ge(s_off, 1)
                step(v.tensor_copy(small[0:HI, 4:5], flag_ps[0:HI, 256:257]))
                step(v.tensor_scalar(end_sb[:, :], end_sb[:, :], small[0:HI, 4:5], None, ALU.add), "info")

            deg, end, has, per_degree, tmp_n = (info[0:NP, i, :] for i in range(5))

            def node_tables():
                v.wait_ge(s_infold, 32)
                step(v.tensor_scalar(end, end, -1.0, 0.0, ALU.add, ALU.max))
                step(v.tensor_copy(last_i[0:NP, :], end), "last")
                step(v.tensor_scalar(has, deg, 1.0, None, ALU.min))
                step(v.tensor_scalar(tmp_n, deg, 1.0, None, ALU.max))
                step(v.reciprocal(tmp_n, tmp_n))
                step(v.tensor_tensor(per_degree, tmp_n, has, ALU.mult))

            def joined(k, b, name):
                v.wait_ge(s_node[b], node_count(k, b))
                rows3 = tiles(node_rows(k), b)
                weight = per_degree if KINDS[k] == SUM else has
                step(v.tensor_tensor(rows3, rows3, spread(weight, b), ALU.mult),
                     f"{name}_{b}" if KINDS[k] == SUM else None)
                if KINDS[k] == MAX:
                    step(v.tensor_tensor(rows3, rows3, tiles(H, b), ALU.add), f"{name}_{b}")

            def attended(k, b, mark=None):
                b0, b1 = BLOCKS[b]
                v.wait_ge(s_node[b], node_count(k, b))
                rows3 = tiles(node_rows(k), b)
                r3 = rden[0:NP, b0:b1, :]
                dens = rows3[:, :, D + HEADS:AW]
                if k == 4:
                    step(v.tensor_scalar(dens, dens, 1e-16, None, ALU.add))
                step(v.reciprocal(r3, dens))
                step(v.tensor_tensor(r3, r3, spread(has, b, HEADS), ALU.mult))
                vals = rows3[:, :, 0:D].rearrange("p i (h c) -> p i h c", c=CH)
                step(v.tensor_tensor(vals, vals, r3.unsqueeze(3).to_broadcast([NP, b1 - b0, HEADS, CH]), ALU.mult),
                     mark)

            def plus(dst, a, b, mark=None):
                step(v.tensor_tensor(dst, dst, a, ALU.add), mark)

            run_pass(0)
            degrees()
            carry_scan(0)
            join_heads(0)
            node_tables()
            for stage, b in in_stages("sage1"):
                if stage == 0:
                    joined(0, b, "agg0")

            run_pass(1)
            carry_scan(1)
            join_heads(1)
            for stage, b in in_stages("sage2"):
                if stage == 0:
                    joined(1, b, "agg1")
                elif stage == 2:
                    v.wait_ge(s_act, job_end("lin1", b))
                    plus(tiles(XR, b), tiles(T2, b), b)
                    moments("in2", XR, b)
                    rectified(XR, H, b)
                elif stage == 3:
                    inverse_root("in2", b)

            def clear_carries(k, name):
                v.wait_ge(s_act, job_end(name, NBLK - 1))
                step(v.memset(work[:, GD:GD + 6 * GS], 0.0), f"cleared{k}")

            clear_carries(2, "qkvs2")
            run_pass(2)
            carry_scan(2)
            join_heads(2)
            for stage, b in in_stages("conv1"):
                if stage == 0:
                    attended(2, b)
                    plus(tiles(node_rows(2), b)[:, :, 0:D], tiles(KN, b), b, f"in3_{b}")

            clear_carries(3, "qkvs3")
            run_pass(3)
            carry_scan(3)
            join_heads(3)
            for stage, b in in_stages("conv2"):
                if stage == 0:
                    attended(3, b)
                    plus(tiles(XR, b), tiles(KN, b), b)
                    plus(tiles(XR, b), tiles(node_rows(3), b)[:, :, 0:D], b)
                    moments("in4", XR, b)
                    rectified(XR, H, b)
                elif stage == 1:
                    inverse_root("in4", b)

            xr3 = XR[0:NP, :, :]
            step(v.tensor_tensor(xr3, xr3, affine[0:NP, 3, :].unsqueeze(1).to_broadcast([NP, NB, D]), ALU.add))
            clear_carries(4, "qkv4")
            run_pass(4)
            carry_scan(4)
            join_heads(4)
            for stage, b in in_stages("graph"):
                if stage == 0:
                    attended(4, b, f"att4_{b}")
                elif stage == 2:
                    v.wait_ge(s_act, job_end("wo4", b))
                    moments("ffn4", T1, b)
                elif stage == 3:
                    mapped("ffn4", T1, T2, b, 0, lambda i: affine[0:NP, 1, :], f"ffn4_{b}")
                elif stage == 7:
                    v.wait_ge(s_act, job_end("down4", b))
                    moments("out4", T1, b)
                elif stage == 8:
                    mapped("out4", T1, XR, b, 2, lambda i: XR[0:NP, i, :])
                    moments("h5", XR, b)
                    rectified(XR, H, b)
                elif stage == 9:
                    inverse_root("h5", b)

            run_pass(5)
            carry_scan(5)
            join_heads(5)
            for stage, b in in_stages("gin1"):
                if stage == 0:
                    joined(5, b, "z5")
            run_pass(6)
            carry_scan(6)
            join_heads(6)
            for stage, b in in_stages("gin2"):
                if stage == 0:
                    joined(6, b, "z6")
                elif stage == 2:
                    v.wait_ge(s_act, job_end("lin6", b))
                    plus(tiles(XR, b), tiles(T2, b), b, f"result_{b}")

        @block.scalar
        def _(act):
            scaled = [0]

            def turned(name, b, dst, func=ACT.Copy, **more):
                b0, b1 = BLOCKS[b]
                j = JOB[name, b][0]
                act.wait_ge(s_pe, j + 1)
                act.activation(dst[:, b0 * NP:b1 * NP], bank[j % 4][:, 0:(b1 - b0) * NP], func, **more)\
                    .then_inc(s_act, 1)

            def laid(name, b, dst, func=ACT.Copy):
                b0, b1 = BLOCKS[b]
                j = JOB[name, b][0]
                act.wait_ge(s_pe, j + 1)
                act.activation(dst[0:NP, b0:b1, :],
                               bank[j % 4][0:NP, 0:(b1 - b0) * D].rearrange("p (i f) -> p i f", f=D), func)\
                    .then_inc(s_act, 1)

            def projected(k, name, b, n_w):
                b0, b1 = BLOCKS[b]
                used = kvq_count(k, b) - 16 * kvq_stores(b)
                if used:
                    act.wait_ge(s_kvq[b % QBUF], used)
                for i in range(b0, b1):
                    j = JOB[name, b][0] + i - b0
                    ps = bank[j % 4][0:NP, :]
                    act.wait_ge(s_pe, j + 1)
                    if n_w == 4:
                        act.activation(KN[0:NP, i, :], ps[:, 3 * D:4 * D], ACT.Copy)
                    act.activation(kvq[:, b % QBUF, i - b0, :], ps[:, 0:3 * D], ACT.Copy).then_inc(s_act, 1)

            def take_root(name, b):
                b0, b1 = BLOCKS[b]
                act.wait_ge(s_vec, MARK[f"var_{name}_{b}"])
                act.activation(root[0:NP, b0:b1], var[0:NP, b0:b1], ACT.Sqrt).then_inc(s_root, 1)

            def scale_rows(name, b):
                act.wait_ge(s_vec, MARK[f"rinv_{name}_{b}"])
                for i in range(*BLOCKS[b]):
                    ins = act.activation(H[0:NP, i, :], H[0:NP, i, :], ACT.Copy, scale=rinv[0:NP, i:i + 1])
                ins.then_inc(s_norm, 1)
                scaled[0] += 1
                NORM[name, b] = scaled[0]

            def stage_group(k, it, s, far=False):
                first = it * (RING * GROUP) + s * GROUP
                act.copy(near_idx[:, s, 0, :], src_i[:, bass.ds(first, GROUP)]).then_inc(s_idx, 1)
                if KINDS[k] == ATT:
                    act.copy(near_late[:, s, :], late[:, bass.ds(first, GROUP)]).then_inc(s_idx, 1)
                    act.activation(near_idx[:, s, 1, :], dst_i[:, bass.ds(first, GROUP)], ACT.Copy,
                                   scale=2.0 if far else 1.0).then_inc(s_idx, 1)
                    act.copy(fences[:, s, :, 1:GROUP + 1],
                             fence[:, bass.ds(first, GROUP)].unsqueeze(1).to_broadcast([P, HEADS, GROUP]))\
                        .then_inc(s_idx, 1)

            def number_tiles(k, it, s):
                n = pick_number(k, it, s)
                for u, j in units(k, s):
                    at = it * (RING * GROUP) + (s * GROUP + j)
                    act.copy(pick_src[u], src_i[:, bass.ds(at, 1)].to_broadcast([P, NP])).then_inc(s_col, 1)
                for i, (u, _) in enumerate(units(k, s)):
                    act.wait_ge(s_across, n + (i + 1))
                    act.activation(pick_tile[u], source_bank[u], ACT.Relu, bias=tile_base[0:NP, 0:1])\
                        .then_inc(s_tile, 1)

            def weigh(k, s, g):
                b = s % 2
                act.wait_ge(s_att, after_a(k, g, A_STEPS[k]))
                act.activation(LD[:, b, :, 1:GROUP + 1], DE[:, b, 0, :, :], ACT.Exp).then_inc(s_weigh, 1)
                act.activation(LA[:, b, :, 1:GROUP + 1], DE[:, b, 1, :, :], ACT.Exp).then_inc(s_weigh, 1)
                act.activation(dB[b].rearrange("p (h c t) -> p h c t", h=HEADS, c=CH)[:, :, :, 1:GROUP + 1],
                               DE[:, b, 0, :, :].unsqueeze(2).to_broadcast([P, HEADS, CH, GROUP]), ACT.Exp)\
                    .then_inc(s_weigh, 1)

            def carry_on(s, to):
                act.copy(LA[:, to, :, 0], LS[:, s, :, GROUP])
                act.copy(column(msg[to], 0), column(OS[1 - to], GROUP)).then_inc(s_on, 1)

            def lay_rows(k, it, s, g):
                act.wait_ge(s_att, after_b(k, g, B_STEPS))
                if not (isinstance(it, int) and g == GROUPS - 1):
                    carry_on(s, 1 - s % 2)
                act.wait_ge(s_store[s], it * 16 + store_base(k))
                act.copy(out_att[:, s, :, 0:D], by_edge(OS[s % 2])).then_inc(s_rows, 1)
                act.copy(out_att[:, s, :, D:D + HEADS],
                         MS[:, s, :, 1:GROUP + 1].rearrange("p h j -> p j h")).then_inc(s_rows, 1)
                act.copy(out_att[:, s, :, D + HEADS:AW],
                         LS[:, s, :, 1:GROUP + 1].rearrange("p h j -> p j h")).then_inc(s_rows, 1)

            def lay_queries(k, it, s, g, far):
                done = g + (att_number(k) * GROUPS + 1)
                act.copy(UA[:, s, 1, :, 0], MS[:, (s - 1) % RING, :, GROUP])
                if far:
                    act.wait_ge(s_query, done * (16 * GROUP))
                    act.copy(far_note[:, :], ident[0:1, 0:1]).then_inc(s_laid, 1)
                else:
                    at = s // PER_WINDOW
                    act.wait_ge(s_window[at], it * 16 + (att_number(k) * LOOPS + 1) * 16)
                    act.copy(prod, window[:, at, 0:D].unsqueeze(1).to_broadcast([P, GROUP, D])).then_inc(s_laid, 1)

            def att_pass(k, far):
                for s in range(RING):
                    stage_group(k, 0, s, far)
                lay_queries(k, 0, 0, 0, far)
                act.wait_ge(s_vec, MARK[f"cleared{k}"])
                carry_on(RING - 1, 0)
                weigh(k, 0, 0)
                lay_queries(k, 0, 1, 1, far)
                with act.Fori(0, LOOPS - 1) as it:
                    for s in range(RING):
                        g = it * RING + s
                        weigh(k, (s + 1) % RING, g + 1)
                        lay_queries(k, it + (s + 2) // RING, (s + 2) % RING, g + 2, far)
                        lay_rows(k, it, s, g)
                        stage_group(k, it + 1, s, far)
                for s in range(RING):
                    g = (LOOPS - 1) * RING + s
                    if s + 1 < RING:
                        weigh(k, s + 1, g + 1)
                    if s + 2 < RING:
                        lay_queries(k, LOOPS - 1, s + 2, g + 2, far)
                    lay_rows(k, LOOPS - 1, s, g)

            def run_pass(k):
                if KINDS[k] == ATT:
                    with act.If(slow > 0):
                        att_pass(k, True)
                    with act.Else():
                        att_pass(k, False)
                    return
                for s in range(RING):
                    stage_group(k, 0, s)
                with act.Fori(0, LOOPS - 1) as it:
                    for s in range(RING):
                        if picks(k, s):
                            number_tiles(k, it + 1, s)
                        act.wait_ge(s_agg, it * (RING * GROUP) + (agg_base[k] + (s + 1) * GROUP))
                        stage_group(k, it + 1, s)

            def carry_exps(k):
                act.wait_ge(s_vec, MARK[f"carry_in{k}"])
                act.activation(carE[:, :, :], carE[:, :, :], ACT.Exp).then_inc(s_cexp, 1)
                act.wait_ge(s_vec, MARK[f"head_in{k}"])
                act.activation(head_w[:, 1:3, :], head_w[:, 1:3, :], ACT.Exp).then_inc(s_hexp, 1)

            for stage, b in in_stages("start"):
                if stage == 0:
                    take_root("h0", b)
                elif stage == 1:
                    scale_rows("h0", b)
                else:
                    turned("T_h0", b, KEEP)
            act.wait_ge(s_vec, MARK["ordered"])
            run_pass(0)
            for stage, b in in_stages("sage1"):
                if stage == 0:
                    turned("T_agg0", b, aT)
                elif stage == 1:
                    laid("lin0", b, H, ACT.Relu)
                else:
                    turned("T_h1", b, KEEP)
            run_pass(1)
            for stage, b in in_stages("sage2"):
                if stage == 0:
                    turned("T_agg1", b, aT)
                elif stage == 1:
                    laid("lin1", b, T2, ACT.Relu)
                elif stage == 2:
                    take_root("in2", b)
                elif stage == 3:
                    scale_rows("in2", b)
                elif stage == 4:
                    turned("T_in2", b, aT)
                else:
                    projected(2, "qkvs2", b, 4)
            act.wait_ge(s_vec, MARK["windows"])
            slow = act.value_load(slow_i[0:1, 0:1], min_val=0, max_val=1)
            run_pass(2)
            carry_exps(2)
            for stage, b in in_stages("conv1"):
                if stage == 0:
                    turned("T_in3", b, aT, ACT.Relu)
                else:
                    projected(3, "qkvs3", b, 4)
            run_pass(3)
            carry_exps(3)
            for stage, b in in_stages("conv2"):
                if stage == 0:
                    take_root("in4", b)
                elif stage == 1:
                    scale_rows("in4", b)
                elif stage == 2:
                    turned("T_in4", b, aT)
                else:
                    projected(4, "qkv4", b, 3)
            run_pass(4)
            carry_exps(4)
            for stage, b in in_stages("graph"):
                if stage == 0:
                    turned("T_att4", b, aT)
                elif stage == 1:
                    laid("wo4", b, T1)
                elif stage == 2:
                    take_root("ffn4", b)
                elif stage == 4:
                    turned("T_ffn4", b, KEEP)
                elif stage == 5:
                    turned("up4", b, aT, ACT.Gelu, bias=colb[:, 0:1])
                elif stage == 6:
                    laid("down4", b, T1)
                elif stage == 7:
                    take_root("out4", b)
                elif stage == 8:
                    take_root("h5", b)
                elif stage == 9:
                    scale_rows("h5", b)
            run_pass(5)
            for stage, b in in_stages("gin1"):
                if stage == 0:
                    turned("T_z5", b, aT)
                else:
                    laid("lin5", b, H, ACT.Relu)
            run_pass(6)
            for stage, b in in_stages("gin2"):
                if stage == 0:
                    turned("T_z6", b, aT)
                elif stage == 1:
                    laid("lin6", b, T2)

        @block.tensor
        def _(pe):
            def open_bank(j):
                if j >= 4:
                    pe.wait_ge(s_act, j - 3)
                return bank[j % 4]

            def turn(name, b, src):
                b0, b1 = BLOCKS[b]
                ps = open_bank(JOB[name, b][0])
                for i in range(b0, b1):
                    ins = pe.transpose(ps[:, (i - b0) * NP:(i - b0 + 1) * NP], src[0:NP, i, 0:D], ident[0:NP, 0:NP])
                ins.then_inc(s_pe, 1)

            def linear(name, b, terms, b_at, xt_name, more=None):
                b0, b1 = BLOCKS[b]
                ps = open_bank(JOB[name, b][0])
                pe.wait_ge(s_act, job_end(xt_name, b))
                for i in range(b0, b1):
                    acc = ps[0:NP, (i - b0) * D:(i - b0 + 1) * D]
                    for m, (xt, w_at) in enumerate(terms):
                        pe.matmul(acc, xt[:, i * NP:(i + 1) * NP], W[:, w_at, :], start=(m == 0), stop=False)
                    if more is not None:
                        pe.matmul(acc, ident[0:NP, 0:NP], more[0:NP, i, :], start=False, stop=False)
                    ins = pe.matmul(acc, ones_bf[:, 0:NP], brow3[:, b_at, :], start=False, stop=True)
                ins.then_inc(s_pe, 1)

            def project(name, b, w_at, n_w, b_at, xt_name):
                b0, b1 = BLOCKS[b]
                pe.wait_ge(s_act, job_end(xt_name, b))
                for i in range(b0, b1):
                    ps = open_bank(JOB[name, b][0] + i - b0)
                    acc = ps[0:NP, 0:n_w * D]
                    pe.matmul(acc, aT[:, i * NP:(i + 1) * NP], W[:, w_at:w_at + n_w, :], start=True, stop=False)
                    pe.matmul(acc, ones_bf[:, 0:NP], brow3[:, b_at:b_at + n_w, :], start=False, stop=True)\
                        .then_inc(s_pe, 1)

            def carry_turns(k):
                n = 3 if KINDS[k] == ATT else 1
                if KINDS[k] == ATT:
                    pe.wait_ge(s_vec, MARK[f"tails{k}"])
                else:
                    pe.wait_ge(s_agg, agg_base[k] + STEPS)
                for i in range(n):
                    src = tails[:, i, :] if KINDS[k] == ATT else out_plain[:, RING - 1, GROUP - 1, :]
                    ins = pe.transpose(cin_ps[:, i * P:(i + 1) * P], src, ident[:, :])
                ins.then_inc(s_cin, 1)
                pe.wait_ge(s_vec, MARK[f"carry{k}"])
                for i in range(n):
                    ins = pe.transpose(cout_ps[:, i * P:(i + 1) * P], tails[:, i, :], ident[:, :])
                ins.then_inc(s_cout, 1)

            def across(k, it, s):
                for i, (u, _) in enumerate(units(k, s)):
                    pe.wait_ge(s_col, pick_number(k, it, s) + (i + 1))
                    pe.nop(nofuse=True)
                    pe.matmul(source_bank[u], pick_src[u], ident[:, :], start=True, stop=True)\
                        .then_inc(s_across, 1)

            def pick(k, it, s):
                for i, (u, _) in enumerate(units(k, s)):
                    pe.wait_ge(s_onehot, pick_number(k, it, s) + (i + 1))
                    if not (isinstance(it, int) and it == 1):
                        pe.wait_ge(s_agg, it * (RING * GROUP) + (agg_base[k] + (s + 1) * GROUP - RING * GROUP))
                    for t in range(NB):
                        ins = pe.matmul(pick_bank[u], hot_src[k][u][:, t, :], parts3[:, :, t, :],
                                        start=(t == 0), stop=(t == NB - 1))
                    ins.then_inc(s_pick, 1)

            def count_degrees(k, it, s):
                if k == 0:
                    pe.wait_ge(s_hot, (it * RING + (s + 1)) * 2)
                    for j in range(GROUP):
                        ins = pe.matmul(hist_ps[0:HI, 0:LO], hot_hi[:, s % 2, j, :], hot_lo[:, s % 2, j, :],
                                        start=False, stop=False, skip_group_check=True)
                    ins.then_inc(s_hist, 1)

            def pick_rows(k):
                last = LOOPS - 1
                pe.wait_ge(s_act, job_end({0: "T_h0", 1: "T_h1", 5: "down4", 6: "lin5"}[k], NBLK - 1))
                pe.wait_ge(s_vec, MARK[f"parts{k}"])
                across(k, 1, 0)
                across(k, 1, 1)
                for s in range(3):
                    count_degrees(k, 0, s)
                pick(k, 1, 0)
                across(k, 1, 2)
                count_degrees(k, 0, 3)
                across(k, 1, 3)
                with pe.Fori(1, last) as it:
                    for s in range(RING):
                        count_degrees(k, it, s)
                        if s + 1 < RING:
                            pick(k, it, s + 1)
                        else:
                            pick(k, it + 1, 0)
                        across(k, it + 1, s)
                for s in range(RING):
                    count_degrees(k, last, s)
                    if s + 1 < RING:
                        pick(k, last, s + 1)

            pe.wait_ge(s_const, 7)
            for stage, b in in_stages("start"):
                if stage == 2:
                    pe.wait_ge(s_norm, NORM["h0", b])
                    turn("T_h0", b, H)
            pe.wait_ge(s_vec, MARK["disorder"])
            pe.matmul(flag_ps[:, 301:302], carT[:, 1, :], small[:, 9:10], start=True, stop=True).then_inc(s_order, 1)
            pe.wait_ge(s_vec, MARK["whole"])
            pe.matmul(flag_ps[:, P:2 * P], tails[:, 1, :], ident[:, :], start=True, stop=True)
            pe.matmul(flag_ps[:, 0:P], tails[:, 0, :], ident[:, :], start=True, stop=True).then_inc(s_flagT, 1)
            pe.wait_ge(s_vec, MARK["far"])
            pe.matmul(flag_ps[:, 300:301], carT[:, 1, :], small[:, 5:6], start=True, stop=True).then_inc(s_far, 1)
            pe.matmul(hist_ps[0:HI, 0:LO], zero_bf[:, 0:HI], zero_bf[:, :], start=True, stop=False,
                      skip_group_check=True).then_inc(s_hist, 1)
            pick_rows(0)
            pe.matmul(hist_ps[0:HI, 0:LO], zero_bf[:, 0:HI], zero_bf[:, :], start=False, stop=True,
                      skip_group_check=True).then_inc(s_hist, 1)
            pe.wait_ge(s_vec, MARK["row_totals"])
            pe.matmul(flag_ps[0:HI, 256:257], upper[:, :], end_sb[:, LO - 1:LO], start=True, stop=True)\
                .then_inc(s_off, 1)
            carry_turns(0)
            pe.wait_ge(s_vec, MARK["biases"])
            pe.wait_ge(s_parts, 32)
            for stage, b in in_stages("sage1"):
                if stage == 0:
                    pe.wait_ge(s_vec, MARK[f"agg0_{b}"])
                    turn("T_agg0", b, node_rows(0))
                elif stage == 1:
                    linear("lin0", b, [(aT, wi["L0_gnn_W1l"]), (KEEP, wi["L0_gnn_W1r"])], bi["L0_gnn_b1"], "T_agg0")
                else:
                    pe.wait_ge(s_act, job_end("lin0", b))
                    turn("T_h1", b, H)
            pick_rows(1)
            carry_turns(1)
            for stage, b in in_stages("sage2"):
                if stage == 0:
                    pe.wait_ge(s_vec, MARK[f"agg1_{b}"])
                    turn("T_agg1", b, node_rows(1))
                elif stage == 1:
                    linear("lin1", b, [(aT, wi["L0_gnn_W2l"]), (KEEP, wi["L0_gnn_W2r"])], bi["L0_gnn_b2"], "T_agg1")
                elif stage == 4:
                    pe.wait_ge(s_norm, NORM["in2", b])
                    turn("T_in2", b, H)
                elif stage == 5:
                    project("qkvs2", b, wi["L1_gnn_k_w0"], 4, bi["L1_gnn_k_b0"], "T_in2")
            carry_turns(2)
            for stage, b in in_stages("conv1"):
                if stage == 0:
                    pe.wait_ge(s_vec, MARK[f"in3_{b}"])
                    turn("T_in3", b, node_rows(2))
                else:
                    project("qkvs3", b, wi["L1_gnn_k_w1"], 4, bi["L1_gnn_k_b1"], "T_in3")
            carry_turns(3)
            for stage, b in in_stages("conv2"):
                if stage == 2:
                    pe.wait_ge(s_norm, NORM["in4", b])
                    turn("T_in4", b, H)
                elif stage == 3:
                    project("qkv4", b, wi["L2_gnn_Wk"], 3, bi["L2_gnn_bk"], "T_in4")
            carry_turns(4)
            for stage, b in in_stages("graph"):
                if stage == 0:
                    pe.wait_ge(s_vec, MARK[f"att4_{b}"])
                    turn("T_att4", b, node_rows(4))
                elif stage == 1:
                    linear("wo4", b, [(aT, wi["L2_gnn_Wo"])], bi["L2_gnn_bo"], "T_att4", H)
                elif stage == 4:
                    pe.wait_ge(s_vec, MARK[f"ffn4_{b}"])
                    turn("T_ffn4", b, T2)
                elif stage == 5:
                    b0, b1 = BLOCKS[b]
                    ps = open_bank(JOB["up4", b][0])
                    pe.wait_ge(s_act, job_end("T_ffn4", b))
                    pe.matmul(ps[:, 0:(b1 - b0) * NP], W[:, wi["L2_gnn_W1"], :], KEEP[:, b0 * NP:b1 * NP],
                              start=True, stop=True).then_inc(s_pe, 1)
                elif stage == 6:
                    linear("down4", b, [(aT, wi["L2_gnn_W2"])], bi["L2_gnn_b2"], "up4", T2)
            pick_rows(5)
            carry_turns(5)
            for stage, b in in_stages("gin1"):
                if stage == 0:
                    pe.wait_ge(s_vec, MARK[f"z5_{b}"])
                    turn("T_z5", b, node_rows(5))
                else:
                    linear("lin5", b, [(aT, wi["L3_gnn_W1"])], bi["L3_gnn_b1"], "T_z5")
            pick_rows(6)
            carry_turns(6)
            for stage, b in in_stages("gin2"):
                if stage == 0:
                    pe.wait_ge(s_vec, MARK[f"z6_{b}"])
                    turn("T_z6", b, node_rows(6))
                elif stage == 1:
                    linear("lin6", b, [(aT, wi["L3_gnn_W2"])], bi["L3_gnn_b2"], "T_z6")

        @block.sync
        def _(sp):
            def by_part(a):
                return a.rearrange("(p i) f -> p i f", i=NB)

            def block_of(a, b):
                return by_part(a)[:, BLOCKS[b][0]:BLOCKS[b][1], :]

            for b, (b0, b1) in enumerate(BLOCKS):
                sp.dma_start(XR[0:NP, b0:b1, :], block_of(A["x"], b)).then_inc(s_x[b], 16)
            sp.wait_ge(s_vec, MARK["pads"])
            for dst, name in ((src_i, "src"), (dst_i, "dst"), (type_i, "edge_type_8")):
                sp.dma_start(dst[0:FULL, :], A[name][0:FULL * STEPS].rearrange("(p t) -> p t", t=STEPS))\
                    .then_inc(s_edges, 16)
                sp.dma_start(dst[FULL:FULL + 1, 0:REST], A[name][FULL * STEPS:E].rearrange("(p t) -> p t", p=1))\
                    .then_inc(s_edges, 16)
            sp.dma_start(before[1:FULL + 1, :],
                         A["dst"][0:FULL * STEPS].rearrange("(p t) -> p t", t=STEPS)[:, STEPS - 1:STEPS],
                         allow_slow_non_contiguous=True).then_inc(s_before, 16)
            for b, (b0, b1) in enumerate(BLOCKS):
                sp.wait_ge(s_norm, NORM["h0", b])
                sp.dma_start(block_of(table[0], b), H[0:NP, b0:b1, :]).then_inc(s_table, 16)
            for i, n in enumerate(W_ORDER):
                sp.dma_start(W[:, i, :], A[n]).then_inc(s_weights, 16)
            for i, n in enumerate(B_ORDER):
                sp.dma_start(brow[:, i, :], A[n].unsqueeze(0)).then_inc(s_weights, 16)
            for i, n in enumerate(AFFINE):
                sp.dma_start(affine[:, i, :], A[n].partition_broadcast(P)).then_inc(s_weights, 16)
            sp.dma_start(ebias[:, :, :].rearrange("p k h -> p (k h)"),
                         A["L2_gnn_edge_bias"].rearrange("k h -> (k h)").partition_broadcast(P))\
                .then_inc(s_weights, 16)
            sp.dma_start(colb[:, :], A["L2_gnn_b1"].unsqueeze(1), allow_slow_non_contiguous=True)\
                .then_inc(s_weights, 16)

            def store_rows(k):
                w = AW if KINDS[k] == ATT else D
                dst = rows[KINDS[k]].rearrange("(p t) f -> p (t f)", t=STEPS)
                with sp.Fori(0, LOOPS) as it:
                    for s in range(RING):
                        g = it * RING + s
                        if KINDS[k] == ATT:
                            sp.wait_ge(s_rows, g * 3 + (rows_base[k] + 3))
                        else:
                            sp.wait_ge(s_agg, g * GROUP + (agg_base[k] + GROUP))
                        sp.dma_start(dst[:, bass.ds(g * (GROUP * w), GROUP * w)],
                                     slot_out(k, s).rearrange("p j f -> p (j f)")).then_inc(s_store[s], 16)

            def store_kvq(k, name):
                at, after = by_part(qtable[k][:, 0:D]), by_part(qtable[k][:, D:2 * D])
                for b, (b0, b1) in enumerate(BLOCKS):
                    rows3 = kvq[:, b % QBUF, 0:b1 - b0, :]
                    queries = rows3[:, :, 2 * D:3 * D]
                    done = s_kvq[b % QBUF]
                    sp.wait_ge(s_act, job_end(name, b))
                    sp.dma_start(block_of(table[k], b), rows3[:, :, 0:2 * D]).then_inc(done, 16)
                    sp.dma_start(at[:, b0:b1, :], queries).then_inc(done, 16)
                    if b == 0:
                        sp.dma_start(after[:, 0:b1 - 1, :], queries[:, 1:b1, :]).then_inc(done, 16)
                        sp.dma_start(after[0:NP - 1, NB - 1, :], queries[1:NP, 0, :]).then_inc(done, 16)
                    else:
                        sp.dma_start(after[:, b0 - 1:b1 - 1, :], queries).then_inc(done, 16)
                    if b == NBLK - 1:
                        sp.dma_start(after[NP - 1:NP, NB - 1, :], queries[NP - 1:NP, b1 - b0 - 1, :])\
                            .then_inc(done, 16)

            def store_linear(k, name):
                for b, (b0, b1) in enumerate(BLOCKS):
                    sp.wait_ge(s_act, job_end(name, b))
                    sp.dma_start(block_of(table[k], b), H[0:NP, b0:b1, :]).then_inc(s_table, 16)

            store_rows(0)
            sp.wait_ge(s_vec, MARK["biases"])
            for i in range(2):
                sp.dma_start(brow3[1 + i:2 + i, :, :], brow_low[:, i, :, :]).then_inc(s_parts, 16)
            sp.wait_ge(s_vec, MARK["info"])
            for i, a in enumerate((deg_sb, end_sb)):
                sp.dma_start(node_info[i].rearrange("(h l) -> h l", l=LO), a[:, :]).then_inc(s_info, 16)
            sp.wait_ge(s_info, 32)
            for i in range(2):
                sp.dma_start(info[0:NP, i, :], node_info[i, 0:N].rearrange("(p i) -> p i", i=NB))\
                    .then_inc(s_infold, 16)
            store_linear(1, "lin0")
            store_rows(1)
            store_kvq(2, "qkvs2")
            store_rows(2)
            store_kvq(3, "qkvs3")
            store_rows(3)
            store_kvq(4, "qkv4")
            store_rows(4)
            for b, (b0, b1) in enumerate(BLOCKS):
                sp.wait_ge(s_norm, NORM["h5", b])
                sp.dma_start(block_of(table[5], b), H[0:NP, b0:b1, :]).then_inc(s_table, 16)
            store_rows(5)
            store_linear(6, "lin5")
            store_rows(6)
            for b, (b0, b1) in enumerate(BLOCKS):
                sp.wait_ge(s_vec, MARK[f"result_{b}"])
                sp.dma_start(block_of(A["out"], b), XR[0:NP, b0:b1, :]).then_inc(s_out, 16)
            sp.wait_ge(s_out, 16 * NBLK)

        @block.gpsimd
        def _(pool):
            pool.iota(lo_iota_i[:, :], [[1, LO]], base=0, channel_multiplier=0).then_inc(s_const, 1)
            pool.iota(part_i[:, :], [[0, 1]], base=-1, channel_multiplier=STEPS).then_inc(s_const, 1)
            pool.iota(first_i[:, :], [[0, 1]], base=1, channel_multiplier=-NB).then_inc(s_const, 1)
            pool.iota(column_no_i, [[1, STEPS]], base=0, channel_multiplier=0).then_inc(s_const, 1)
            pool.iota(part_less_i, [[1, P]], base=0, channel_multiplier=-1).then_inc(s_const, 1)
            pool.memset(ident[:, :], 0.0).then_inc(s_zero, 1)
            pool.memset(upper[:, :], 1.0).then_inc(s_zero, 1)
            pool.wait_ge(s_zero, 2)
            pool.affine_select(out=ident[:, :], in_=ident[:, :], compare_op=ALU.not_equal, fill=1.0, base=0,
                               pattern=[[-1, P]], channel_multiplier=1).then_inc(s_const, 1)
            pool.affine_select(out=upper[:, :], in_=upper[:, :], compare_op=ALU.is_gt, fill=0.0, base=0,
                               pattern=[[1, HI]], channel_multiplier=-1).then_inc(s_const, 1)

            def fetch(dst, tab, idx, done):
                pool.indirect_dma_start(dst, None, tab, bass.IndirectOffsetOnAxis(ap=idx, axis=0))\
                    .then_inc(done, 16)

            def rows_of_group(k, s, n=GROUP):
                for j in range(n):
                    row = ring[:, s, j, :] if KINDS[k] == ATT else ring_plain[:, s, j, :]
                    fetch(row, table[k], near_idx[:, s, 0, j:j + 1], s_land[s])

            def staged(k, it, s):
                per = idx_per[KINDS[k]]
                pool.wait_ge(s_idx, (it * RING + s) * per + (idx_base[k] + per))
                pool.nop(nofuse=True)

            def far_group(k, it, s):
                g = it * RING + s
                staged(k, it, s)
                rows_of_group(k, s)
                if not (isinstance(it, int) and g == 0):
                    pool.wait_ge(s_att, after_a(k, g - 1, A_STEPS[k]))
                    pool.nop(nofuse=True)
                for j in range(GROUP):
                    fetch(prod[:, j, :], qtable[k].rearrange("n (a f) -> (n a) f", a=2),
                          near_idx[:, s, 1, j:j + 1], s_query)

            def run_pass(k):
                if KINDS[k] == ATT:
                    for b in range(NBLK - QBUF, NBLK):
                        pool.wait_ge(s_kvq[b % QBUF], kvq_count(k, b))
                else:
                    pool.wait_ge(s_table, table_count(k))
                if KINDS[k] != ATT:
                    for s in range(RING):
                        staged(k, 0, s)
                        rows_of_group(k, s)
                    with pool.Fori(1, LOOPS) as it:
                        for s in range(RING):
                            staged(k, it, s)
                            rows_of_group(k, s, GROUP - picks(k, s))
                    return
                with pool.If(slow > 0):
                    for s in range(RING):
                        far_group(k, 0, s)
                    with pool.Fori(1, LOOPS) as it:
                        for s in range(RING):
                            far_group(k, it, s)
                with pool.Else():
                    with pool.Fori(0, LOOPS) as it:
                        for s in range(RING):
                            staged(k, it, s)
                            if s % PER_WINDOW == 0:
                                at = s // PER_WINDOW
                                fetch(window[:, at, :], qtable[k], near_idx[:, s, 1, 0:1], s_window[at])
                            rows_of_group(k, s)

            def fetch_nodes(k):
                w = AW if KINDS[k] == ATT else D
                if k == 0:
                    pool.wait_ge(s_vec, MARK["heads"])
                for s in range(RING):
                    pool.wait_ge(s_store[s], store_base(k + 1))
                fetch(head[:, 0:w], rows[KINDS[k]], head_i[:, 0:1], s_head)
                pool.wait_ge(s_vec, MARK[f"head{k}"])
                pool.indirect_dma_start(rows[KINDS[k]], bass.IndirectOffsetOnAxis(ap=head_i[:, 0:1], axis=0),
                                        head[:, 0:w], None).then_inc(s_patch, 16)
                pool.wait_ge(s_patch, 16 * (k + 1))
                if k == 0:
                    pool.wait_ge(s_vec, MARK["last"])
                for b, (b0, b1) in enumerate(BLOCKS):
                    for i in range(b0, b1):
                        fetch(node_rows(k)[:, i, :], rows[KINDS[k]], last_i[0:NP, i:i + 1], s_node[b])

            def place_edges():
                first, each = 5, 2 + 3 * (STEPS // SEVERAL)
                pool.dma_start(dst_unsorted.rearrange("(p t) -> p t", t=STEPS), dst_i[:, :]).then_inc(s_spilled, 16)
                pool.wait_ge(s_spilled, 16)
                pool.dma_start(other_i, dst_unsorted[0:STEPS].partition_broadcast(P)).then_inc(s_other, 16)
                with pool.Fori(1, P) as j:
                    pool.wait_ge(s_rank, j * each + first)
                    pool.dma_start(other_i, dst_unsorted[bass.ds(j * STEPS, STEPS)].partition_broadcast(P))\
                        .then_inc(s_other, 16)
                with pool.Fori(0, STEPS) as t:
                    pool.wait_ge(s_row, t + 1)
                    pool.nop(nofuse=True)
                    pool.indirect_dma_start(sorted_edges, bass.IndirectOffsetOnAxis(ap=rank_one[:, 0:1], axis=0),
                                            row4[:, :], None).then_inc(s_placed, 16)
                pool.wait_ge(s_placed, 16 * STEPS)
                by_place = sorted_edges.rearrange("(p t) c -> p t c", t=STEPS)
                pool.dma_start(edges_back, by_place).then_inc(s_back, 16)
                pool.dma_start(before[1:P, :], by_place[0:P - 1, STEPS - 1, 1:2], allow_slow_non_contiguous=True)\
                    .then_inc(s_back, 16)

            pool.wait_ge(s_const, 7)
            pool.wait_ge(s_vec, MARK["order"])
            unsorted = pool.value_load(unsorted_i[0:1, 0:1], min_val=0, max_val=1)
            with pool.If(unsorted > 0):
                place_edges()
            run_pass(0)
            fetch_nodes(0)
            pool.wait_ge(s_vec, MARK["windows"])
            slow = pool.value_load(slow_i[0:1, 0:1], min_val=0, max_val=1)
            for k in range(1, PASSES):
                run_pass(k)
                fetch_nodes(k)


_UNUSED = ("edge_weight1",)


def kernel(**inputs):
    import numpy as _np
    import concourse.bacc as _bacc
    from concourse import mybir as _mybir
    from concourse.bass_utils import run_bass_kernel_spmd as _run

    nc = _bacc.Bacc("TRN2", target_bir_lowering=False, num_devices=1)
    arrays, handles = {}, {}
    for name in inputs:
        if name in _UNUSED:
            continue
        a = _np.ascontiguousarray(inputs[name])
        arrays[f"in_{name}"] = a
        handles[name] = nc.dram_tensor(f"in_{name}", a.shape, _mybir.dt.from_np(a.dtype), kind="ExternalInput").ap()
    handles["out"] = nc.dram_tensor("out_x", (N, D), F32, kind="ExternalOutput").ap()
    gnn_kernel(nc, handles)
    r = _run(nc, [arrays], core_ids=[0])
    return r.results[0]["out_x"]
```
